# Optimizing a Trainium2 kernel written in Bass

```python
import numpy as np
import jax
import jax.numpy as jnp

def _softmax(x, axis=-1):
    return jax.nn.softmax(x, axis=axis)

def _gelu(x):
    return jax.nn.gelu(x, approximate=True)

def _silu(x):
    return jax.nn.silu(x)

def _sigmoid(x):
    return jax.nn.sigmoid(x)

def _layernorm(x, axis=-1, eps=1e-05):
    m = jnp.mean(x, axis=axis, keepdims=True)
    v = jnp.var(x, axis=axis, keepdims=True)
    return (x - m) / jnp.sqrt(v + eps)

def _scatter_add(tgt, idx, src, axis=0):
    return tgt.at[idx].add(src)

def _segment_sum(src, seg, n):
    return jax.ops.segment_sum(src, seg, n)
kernel_name = 'mk_xattn_ffn_d2_seqx_r8_e5055e'

def setup_inputs(seed: int=0):
    np.random.seed(seed)
    _w = jnp.asarray

    def _rec_inputs():
        import jax
        import jax.numpy as jnp
        _rk = jax.random.key(seed)
        x = -0.0005207 + 1.001 * jax.random.normal(jax.random.fold_in(_rk, 1), (32, 128, 128), jnp.float32)
        _lenS = 128 - jax.random.randint(jax.random.fold_in(_rk, 7), (32,), 0, max(1, 128 // 4) + 1, jnp.int32)
        _lenS2 = 128 - jax.random.randint(jax.random.fold_in(_rk, 8), (32,), 0, max(1, 128 // 4) + 1, jnp.int32)
        _ctx_1024P = jax.random.normal(jax.random.fold_in(_rk, 11), (32, 16, 128), jnp.float32)
        _ctx_1024c = jax.random.dirichlet(jax.random.fold_in(_rk, 511), 0.3 * jnp.ones((16,), jnp.float32), (32, 128))
        _ctx_1024t = jnp.einsum('bsk,bkd->bsd', _ctx_1024c, _ctx_1024P)
        _ctx_1024t = _ctx_1024t * jax.lax.rsqrt(jnp.mean(jnp.square(_ctx_1024t)) + 1e-12) * 0.953939
        ctx_1024 = -0.000514642 + 1.00011 * (_ctx_1024t + 0.3 * jax.random.normal(jax.random.fold_in(_rk, 611), (32, 128, 128), jnp.float32))
        return (x, ctx_1024)
    x, ctx_1024 = _rec_inputs()

    def _L0_xattn_setup():
        import jax, jax.numpy as jnp
        import numpy as np
        DIM = 128
        HEADS = 8
        HEAD_DIM = DIM // HEADS
        TAU = HEAD_DIM ** 0.5
        BS, SEQ = (1, 256)
        key = jax.random.key(seed)
        kq, kk, kv, kb = jax.random.split(key, 4)
        q = jax.random.normal(kq, (BS, SEQ, DIM), jnp.float32)
        k = jax.random.normal(kk, (BS, SEQ, DIM), jnp.float32)
        v = jax.random.normal(kv, (BS, SEQ, DIM), jnp.float32)
        Wi_w = jnp.zeros((HEADS, 3 * DIM), jnp.float32)
        Wi_b = 0.1 * jax.random.normal(kb, (HEADS,), jnp.float32)
        Wf_w = jnp.zeros((HEADS, 3 * DIM), jnp.float32)
        Wf_b = jnp.linspace(3.0, 6.0, HEADS, dtype=jnp.float32)
        gn_w = jnp.ones((DIM,), jnp.float32)
        gn_b = jnp.zeros((DIM,), jnp.float32)
        return {'q': q, 'k': k, 'v': v, 'Wi_w': Wi_w, 'Wi_b': Wi_b, 'Wf_w': Wf_w, 'Wf_b': Wf_b, 'gn_w': gn_w, 'gn_b': gn_b}
    _L0_xattn_all = _L0_xattn_setup()
    _L0_xattn_in = {k: v for k, v in _L0_xattn_all.items() if k in ('Wi_w', 'Wi_b', 'Wf_w', 'Wf_b', 'gn_w', 'gn_b')}
    del _L0_xattn_all

    def _L0_ffn_setup():
        import jax, jax.numpy as jnp
        import numpy as np
        NUM_EXPERTS = 8
        TOP_K = 2
        D_MODEL = 128
        D_FF = 512
        B, S = (2, 256)
        key = jax.random.key(seed)
        k1, k2, k3, k4 = jax.random.split(key, 4)
        scale_in = 1.0 / np.sqrt(D_MODEL)
        scale_ff = 1.0 / np.sqrt(D_FF)
        return {'hidden_states': jax.random.normal(k1, (B, S, D_MODEL), dtype=jnp.float32), 'gate_w': jax.random.normal(k2, (D_MODEL, NUM_EXPERTS), dtype=jnp.float32) * scale_in, 'w1': jax.random.normal(k3, (NUM_EXPERTS, D_MODEL, D_FF), dtype=jnp.float32) * scale_in, 'w2': jax.random.normal(k4, (NUM_EXPERTS, D_FF, D_MODEL), dtype=jnp.float32) * scale_ff}
    _L0_ffn_all = _L0_ffn_setup()
    _L0_ffn_in = {k: v for k, v in _L0_ffn_all.items() if k in ('gate_w', 'w1', 'w2')}
    del _L0_ffn_all

    def _L1_xattn_setup():
        import jax, jax.numpy as jnp
        import numpy as np
        HIDDEN = 128
        HEADS = 16
        HEAD_DIM = 64
        key = jax.random.key(seed)
        ks = jax.random.split(key, 7)
        B, Q, K = (2, 256, 512)
        s = 1.0 / np.sqrt(HIDDEN)
        return {'query': jax.random.normal(ks[0], (B, Q, HIDDEN), dtype=jnp.float32), 'key': jax.random.normal(ks[1], (B, K, HIDDEN), dtype=jnp.float32), 'value': jax.random.normal(ks[2], (B, K, HIDDEN), dtype=jnp.float32), 'w_q': jax.random.normal(ks[3], (HIDDEN, HEADS * HEAD_DIM), dtype=jnp.float32) * s, 'w_k': jax.random.normal(ks[4], (HIDDEN, HEADS * HEAD_DIM), dtype=jnp.float32) * s, 'w_v': jax.random.normal(ks[5], (HIDDEN, HEADS * HEAD_DIM), dtype=jnp.float32) * s, 'w_o': jax.random.normal(ks[6], (HEADS * HEAD_DIM, HIDDEN), dtype=jnp.float32) * s}
    _L1_xattn_all = _L1_xattn_setup()
    _L1_xattn_in = {k: v for k, v in _L1_xattn_all.items() if k in ('w_q', 'w_k', 'w_v', 'w_o')}
    del _L1_xattn_all

    def _L1_ffn_setup():
        import jax, jax.numpy as jnp
        import numpy as np
        D_MODEL = 128
        M = 64
        INNER = 16
        key = jax.random.key(seed)
        ks = jax.random.split(key, 9)

        def init(k, shape, fan_in):
            bound = 1.0 / np.sqrt(fan_in)
            return jax.random.uniform(k, shape, jnp.float32, -bound, bound)
        x = jax.random.normal(ks[0], (16, 512, D_MODEL), dtype=jnp.float32)
        Win = init(ks[1], (D_MODEL, M), D_MODEL)
        bin_ = init(ks[2], (M,), D_MODEL)
        W1 = init(ks[3], (M, INNER), 1)
        b1 = init(ks[4], (M, INNER), 1)
        W2 = init(ks[5], (M, INNER), INNER)
        b2 = init(ks[6], (M,), INNER)
        Wout = init(ks[7], (M, D_MODEL), M)
        bout = init(ks[8], (D_MODEL,), M)
        return {'x': x, 'Win': Win, 'bin_': bin_, 'W1': W1, 'b1': b1, 'W2': W2, 'b2': b2, 'Wout': Wout, 'bout': bout}
    _L1_ffn_all = _L1_ffn_setup()
    _L1_ffn_in = {k: v for k, v in _L1_ffn_all.items() if k in ('Win', 'bin_', 'W1', 'b1', 'W2', 'b2', 'Wout', 'bout')}
    del _L1_ffn_all
    return {'x': x, 'ctx_1024': ctx_1024, 'L0_xattn_Wi_w': _L0_xattn_in['Wi_w'], 'L0_xattn_Wi_b': _L0_xattn_in['Wi_b'], 'L0_xattn_Wf_w': _L0_xattn_in['Wf_w'], 'L0_xattn_Wf_b': _L0_xattn_in['Wf_b'], 'L0_xattn_gn_w': _L0_xattn_in['gn_w'], 'L0_xattn_gn_b': _L0_xattn_in['gn_b'], 'L0_ffn_gate_w': _L0_ffn_in['gate_w'], 'L0_ffn_w1': _L0_ffn_in['w1'], 'L0_ffn_w2': _L0_ffn_in['w2'], 'L1_xattn_w_q': _L1_xattn_in['w_q'], 'L1_xattn_w_k': _L1_xattn_in['w_k'], 'L1_xattn_w_v': _L1_xattn_in['w_v'], 'L1_xattn_w_o': _L1_xattn_in['w_o'], 'L1_ffn_Win': _L1_ffn_in['Win'], 'L1_ffn_bin_': _L1_ffn_in['bin_'], 'L1_ffn_W1': _L1_ffn_in['W1'], 'L1_ffn_b1': _L1_ffn_in['b1'], 'L1_ffn_W2': _L1_ffn_in['W2'], 'L1_ffn_b2': _L1_ffn_in['b2'], 'L1_ffn_Wout': _L1_ffn_in['Wout'], 'L1_ffn_bout': _L1_ffn_in['bout']}

def reference(x, ctx_1024, L0_xattn_Wi_w, L0_xattn_Wi_b, L0_xattn_Wf_w, L0_xattn_Wf_b, L0_xattn_gn_w, L0_xattn_gn_b, L0_ffn_gate_w, L0_ffn_w1, L0_ffn_w2, L1_xattn_w_q, L1_xattn_w_k, L1_xattn_w_v, L1_xattn_w_o, L1_ffn_Win, L1_ffn_bin_, L1_ffn_W1, L1_ffn_b1, L1_ffn_W2, L1_ffn_b2, L1_ffn_Wout, L1_ffn_bout):
    import jax
    import jax.numpy as jnp

    def _L0_xattn_ref(q, k, v, Wi_w, Wi_b, Wf_w, Wf_b, gn_w, gn_b):
        import jax, jax.numpy as jnp
        import numpy as np
        DIM = 128
        HEADS = 8
        HEAD_DIM = DIM // HEADS
        TAU = HEAD_DIM ** 0.5
        BS, SEQ = (1, 256)
        bs, seq, dim = q.shape
        gate_in = jnp.concatenate([q, k, v], axis=-1)
        itilde = jnp.einsum('bsd,hd->bhs', gate_in, Wi_w) + Wi_b[None, :, None]
        ftilde = jnp.einsum('bsd,hd->bhs', gate_in, Wf_w) + Wf_b[None, :, None]
        csum = jnp.cumsum(jax.nn.log_sigmoid(ftilde), axis=-1)
        Fmat = csum[..., :, None] - csum[..., None, :]
        mask = jnp.tril(jnp.ones((seq, seq), dtype=bool))
        F_act = jnp.where(mask, Fmat, -jnp.inf)
        Dtilde = F_act + itilde[..., None, :]
        max_d = jnp.max(Dtilde, axis=-1, keepdims=True)
        D = jnp.exp(Dtilde - max_d)
        qh = q.reshape(bs, seq, HEADS, HEAD_DIM).transpose(0, 2, 1, 3)
        kh = k.reshape(bs, seq, HEADS, HEAD_DIM).transpose(0, 2, 1, 3)
        vh = v.reshape(bs, seq, HEADS, HEAD_DIM).transpose(0, 2, 1, 3)
        Ctilde = jnp.einsum('bhid,bhjd->bhij', qh, kh) * D / TAU
        maxit = jnp.maximum(jnp.abs(jnp.sum(Ctilde, axis=-1, keepdims=True)), jnp.exp(-max_d))
        Htilde = jnp.einsum('bhij,bhjd->bhid', Ctilde, vh) / (maxit + 1e-06)
        x = Htilde.transpose(0, 2, 1, 3).reshape(bs * seq, HEADS, HEAD_DIM)
        mean = jnp.mean(x, axis=-1, keepdims=True)
        var = jnp.var(x, axis=-1, keepdims=True)
        xn = (x - mean) / jnp.sqrt(var + 1e-05)
        out = xn.reshape(bs * seq, DIM) * gn_w + gn_b
        return out.reshape(bs, seq, DIM)

    def _L0_ffn_ref(hidden_states, gate_w, w1, w2):
        import jax, jax.numpy as jnp
        import numpy as np
        NUM_EXPERTS = 8
        TOP_K = 2
        D_MODEL = 128
        D_FF = 512
        B, S = (2, 256)
        b, s, d = hidden_states.shape
        x = hidden_states.reshape(-1, d)
        gate_logits = x @ gate_w
        top_vals, top_idx = jax.lax.top_k(gate_logits, TOP_K)
        top_w = jax.nn.softmax(top_vals.astype(jnp.float32), axis=1).astype(x.dtype)
        combine = jnp.einsum('tke,tk->te', jax.nn.one_hot(top_idx, NUM_EXPERTS, dtype=x.dtype), top_w)
        h = jax.nn.relu(jnp.einsum('td,edf->etf', x, w1))
        expert_out = jnp.einsum('etf,efd->etd', h, w2)
        final = jnp.einsum('etd,te->td', expert_out, combine)
        return final.reshape(b, s, d)

    def _L1_xattn_ref(query, key, value, w_q, w_k, w_v, w_o):
        import jax, jax.numpy as jnp
        import numpy as np
        HIDDEN = 128
        HEADS = 16
        HEAD_DIM = 64
        B, Q, _ = query.shape
        Kl = key.shape[1]
        scale = HEAD_DIM ** (-0.5)
        q = (query @ w_q).reshape(B, Q, HEADS, HEAD_DIM).transpose(0, 2, 1, 3)
        k = (key @ w_k).reshape(B, Kl, HEADS, HEAD_DIM).transpose(0, 2, 1, 3)
        v = (value @ w_v).reshape(B, Kl, HEADS, HEAD_DIM).transpose(0, 2, 1, 3)
        scores = jnp.einsum('bhqd,bhkd->bhqk', q, k) * scale
        attn = jax.nn.softmax(scores, axis=-1)
        out = jnp.einsum('bhqk,bhkd->bhqd', attn, v)
        out = out.transpose(0, 2, 1, 3).reshape(B, Q, HEADS * HEAD_DIM)
        return out @ w_o

    def _L1_ffn_ref(x, Win, bin_, W1, b1, W2, b2, Wout, bout):
        import jax, jax.numpy as jnp
        import numpy as np
        D_MODEL = 128
        M = 64
        INNER = 16
        s = jnp.einsum('btd,dm->btm', x, Win) + bin_
        h = jax.nn.relu(s[..., None] * W1 + b1)
        g = jnp.einsum('btmh,mh->btm', h, W2) + b2
        out = jnp.einsum('btm,md->btd', g, Wout) + bout
        return out
    x = x + _L0_xattn_ref(_layernorm(x, axis=-1), ctx_1024, ctx_1024, L0_xattn_Wi_w, L0_xattn_Wi_b, L0_xattn_Wf_w, L0_xattn_Wf_b, L0_xattn_gn_w, L0_xattn_gn_b)
    x = x + _L0_ffn_ref(_layernorm(x, axis=-1), L0_ffn_gate_w, L0_ffn_w1, L0_ffn_w2)
    x = x + _L1_xattn_ref(_layernorm(x, axis=-1), ctx_1024, ctx_1024, L1_xattn_w_q, L1_xattn_w_k, L1_xattn_w_v, L1_xattn_w_o)
    x = x + _L1_ffn_ref(_layernorm(x, axis=-1), L1_ffn_Win, L1_ffn_bin_, L1_ffn_W1, L1_ffn_b1, L1_ffn_W2, L1_ffn_b2, L1_ffn_Wout, L1_ffn_bout)
    return x

_drawn_inputs = setup_inputs


def setup_inputs(seed=0):
    import zlib

    import numpy as np

    out = dict(_drawn_inputs(seed))
    spreads = {'L0_xattn_Wi_w': (0.0, 0.1),
     'L0_xattn_Wf_w': (0.0, 0.1),
     'L0_xattn_gn_w': (1.0, 0.2),
     'L0_xattn_gn_b': (0.0, 0.1)}
    factors = {'L0_xattn_Wi_b': 64.0, 'L1_ffn_bin_': 23.641}
    for name, (base, spread) in spreads.items():
        noise = np.random.default_rng([zlib.crc32(name.encode()), seed]).standard_normal(out[name].shape)
        drawn = base * np.exp(spread * noise) if base else spread * noise
        out[name] = jnp.asarray(drawn.astype(out[name].dtype))
    for name, factor in factors.items():
        out[name] = (out[name] * factor).astype(out[name].dtype)
    return out
```

```python
from contextlib import ExitStack

import concourse.bass as bass
from concourse import mybir

F32 = mybir.dt.float32
F32R = mybir.dt.float32r
BF16 = mybir.dt.bfloat16
U32 = mybir.dt.uint32
ALU = mybir.AluOpType
ACT = mybir.ActivationFunctionType
AX = mybir.AxisListType.X

P = 128
G = 4
T = G * P
H0, D0 = 8, 16
E0, F0 = 8, 512
FC = F0 // P
NU = E0 * FC
H1, D1 = 16, 64
HQ = 4
NK = (H1 // HQ) * G
MI = 8
ROW2 = 32
BIG = 1e30
EPS = 1e-5


class Group:

    def __init__(self, base, off=0):
        self.base, self.off = base, off

    def count(self, per, n):
        return self.base * per + (self.off * per + n)

    def known(self):
        return isinstance(self.base, int)

    def shift(self, d):
        return Group(self.base, self.off + d)


class Signal:

    def __init__(self, sem, per):
        self.sem, self.per = sem, per

    def at(self, g, n=None):
        v = g.count(self.per, self.per if n is None else n)
        return max(v, 0) if isinstance(v, int) else v


class Chain:

    def __init__(self, signal, eng):
        self.s, self.eng = signal, eng

    def begin(self, g):
        self.g, self.n = g, 0

    def link(self, ins):
        self.n += 1
        ins.then_inc(self.s.sem, 1)
        self.eng.wait_ge(self.s.sem, self.s.at(self.g, self.n))

    def end(self):
        assert self.n == self.s.per, (self.n, self.s.per)


def build(nc, x, ctx_in, Wi_w, Wi_b, Wf_w, Wf_b, gn_w, gn_b, gate_w, w1, w2, w_q, w_k, w_v, w_o,
          Win, bin_, W1, b1, W2, b2, Wout, bout, out):
    NG = x.shape[0] // G
    x_g = x.rearrange("(g b) s d -> g s b d", b=G)
    c_g = ctx_in.rearrange("(g b) s d -> g s b d", b=G)
    out_g = out.rearrange("(g b) s d -> g s b d", b=G)

    with ExitStack() as es:
        def sb(name, shape, dt=F32):
            return es.enter_context(nc.sbuf_tensor(name, shape, dt))

        def sig(name, per):
            return Signal(es.enter_context(nc.semaphore(name)), per)

        bank = [es.enter_context(nc.psum_tensor(f"bank{i}", [P, T], F32)) for i in range(8)]
        UP = bank[0:2]
        YB = bank[2:4]
        TB = bank[4]
        DB, SB = bank[5], bank[6]
        HB = bank[7]
        PTB = [DB, SB]

        ident = sb("ident", [P, P])
        ident_bf = sb("ident_bf", [P, P], BF16)
        causal = sb("causal", [P, P], BF16)
        sel = sb("sel", [ROW2 * 2, 8, P], F32R)
        headmask = sb("headmask", [P, H0])
        expert_no = sb("expert_no", [P, G, E0])
        neg_half, eps_col = sb("neg_half", [P, 32]), sb("eps_col", [P, 32])
        spare = sb("spare", [1, 1])
        keep = sb("keep", [H0, T])
        drop = sb("drop", [H0, T])
        wg = sb("wg", [ROW2 * 2, 3 * P])
        wgx = sb("wgx", [P, ROW2 * 2])
        wgc = sb("wgc", [P, ROW2 * 2])
        gbias = sb("gbias", [ROW2 * 2, 1])
        gnw = sb("gnw", [P, P])
        gnb = sb("gnb", [P, P])
        wgate = sb("wgate", [P, E0])
        w1h, w1l = sb("w1h", [P, E0, F0], F32R), sb("w1l", [P, E0, F0], F32R)
        w2h, w2l = sb("w2h", [P, NU, P], F32R), sb("w2l", [P, NU, P], F32R)
        wqk_h, wqk_l = sb("wqk_h", [P, H1, P], F32R), sb("wqk_l", [P, H1, P], F32R)
        wvo_h, wvo_l = sb("wvo_h", [P, H1, P], F32R), sb("wvo_l", [P, H1, P], F32R)
        f_in = sb("f_in", [P, MI * P])
        f_bias = sb("f_bias", [P, MI])
        f_out = sb("f_out", [P, MI, P])
        f_last = sb("f_last", [P, P])
        x0, c0 = sb("x0", [P, G, P]), sb("c0", [P, G, P])
        xh = sb("xh", [P, G, P])
        xhT, cT = sb("xhT", [P, G, P]), sb("cT", [P, G, P])
        caug = sb("caug", [P, G, H0, D0 + 1])
        irow, frow = sb("irow", [H0, T]), sb("frow", [H0, T])
        trow = sb("trow", [H0, T])
        acat = sb("acat", [P, T])
        mhl = sb("mhl", [ROW2 * 2, G, P], F32R)
        acol, emd = sb("acol", [P, G, H0]), sb("emd", [P, G, H0])
        work = sb("work", [P, 5632])
        qm = work[:, 0:2048].rearrange("p (n h i) -> p n h i", n=2, h=H0)
        ex = work[:, 2048:3072].rearrange("p (n h i) -> p n h i", n=2, h=4)
        pr = work[:, 3072:4608].rearrange("p (n h i) -> p n h i", n=3, h=HQ)
        pts = work[:, 4608:5632].rearrange("p (n h i) -> p n h i", n=2, h=HQ)
        hs = sb("hs", [P, G * H0, D0 + 1])
        hn = sb("hn", [P, G * H0, D0])
        hq = work[:, 2048:2560].rearrange("p (r d) -> p r d", d=D0)
        sm = sb("sm", [P, 8, 32])
        stats = sm[:, 6:8, :].rearrange("p a r -> p (a r)")[:, 0:6 * G].rearrange("p (b s) -> p b s", s=6)
        mv = [sb(f"mv{i}", [P, G, 2]) for i in range(4)]
        rstd = [sb(f"rstd{i}", [P, 32 if i == 4 else G]) for i in range(5)]
        x1, x2, x3 = sb("x1", [P, G, P]), sb("x2", [P, G, P]), sb("x3", [P, G, P])
        xh2T = sb("xh2T", [P, G, P])
        x2h, x2l = sb("x2h", [P, T], F32R), sb("x2l", [P, T], F32R)
        logit = sb("logit", [P, G, E0])
        top = sb("top", [P, G, 8])
        topi = sb("topi", [P, G, 8], U32)
        topf = sb("topf", [P, G, 2])
        pe12 = sb("pe12", [P, 4, G])
        comb = sb("comb", [P, 3, G, E0])
        chl = sb("chl", [ROW2 * 2, T], F32R)
        cb = sb("cb", [P, 2, T])
        yacc = sb("yacc", [P, G, P])
        ytmp = sb("ytmp", [P, 2, T])
        uh = sb("uh", [P, HQ, T], F32R)
        ul = sb("ul", [P, HQ, T], F32R)
        cA = sb("cA", [P, G, P])
        cTh, cTl = sb("cTh", [P, G, P], F32R), sb("cTl", [P, G, P], F32R)
        xg = sb("xg", [P, G, P])
        x3h, x3l = sb("x3h", [P, G, P], F32R), sb("x3l", [P, G, P], F32R)
        vv = cb[:, :, :].rearrange("p n (h d) -> p n h d", h=HQ)
        pm = sb("pm", [P, 3, 3, HQ])
        xh4T = yacc[:, :, :].rearrange("p b d -> p (b d)")
        fh = ytmp
        res = sb("res", [P, G, P])
        x3b = res

        set_dma = es.enter_context(nc.semaphore("set_dma"))
        set_pool = es.enter_context(nc.semaphore("set_pool"))
        stage_in = [es.enter_context(nc.semaphore(f"stage_in{i}")) for i in range(2)]
        stage_hi = es.enter_context(nc.semaphore("stage_hi"))
        stage_lo = es.enter_context(nc.semaphore("stage_lo"))
        proj_in = es.enter_context(nc.semaphore("proj_in"))
        fold_in = es.enter_context(nc.semaphore("fold_in"))
        set_pe = es.enter_context(nc.semaphore("set_pe"))
        set_act = es.enter_context(nc.semaphore("set_act"))
        set_dve = es.enter_context(nc.semaphore("set_dve"))
        ffn_in = es.enter_context(nc.semaphore("ffn_in"))
        ffn_fold = es.enter_context(nc.semaphore("ffn_fold"))
        ffn_pe = es.enter_context(nc.semaphore("ffn_pe"))
        zeroed = es.enter_context(nc.semaphore("zeroed"))

        x_in, c_in, ca_in = sig("x_in", 16), sig("c_in", 16), sig("ca_in", 16)
        stored = sig("stored", 16)
        ln_var = [sig(f"ln_var{i}", 1) for i in range(5)]
        ln_rstd = [sig(f"ln_rstd{i}", 1) for i in range(5)]
        dve_ln = [sig(f"dve_ln{i}", 1) for i in range(4)]
        pool_ln = [sig(f"pool_ln{i}", 1) for i in range(5)]
        xh1_ready, xh1_turned, xhT_ready = sig("xh1_ready", 1), sig("xh1_turned", 1), sig("xhT_ready", 1)
        c_turned, cT_ready, caug_ready = sig("c_turned", 1), sig("cT_ready", 1), sig("caug_ready", 1)
        gates_done, gates_read = sig("gates_done", 1), sig("gates_read", 1)
        act_gates, softplus_ready = sig("act_gates", 3), sig("softplus_ready", 1)
        dve_rows = sig("dve_rows", 6)
        acat_ready, acat_turned, acol_ready = sig("acat_ready", 1), sig("acat_turned", 1), sig("acol_ready", 1)
        qm_ready = sig("qm_ready", G)
        d_done, e_added, e_exp = sig("d_done", 2 * G), sig("e_added", 2 * G), sig("e_exp", 2 * G)
        s_done, c_done, h_done = sig("s_done", 2 * G), sig("c_done", 2 * G), sig("h_done", 2 * G)
        hs_ready, dve_gn = sig("hs_ready", G), sig("dve_gn", 12)
        x1_ready = sig("x1_ready", 1)
        xh2_ready, xh2_turned, xh2T_ready = sig("xh2_ready", 1), sig("xh2_turned", 1), sig("xh2T_ready", 1)
        x2hl_ready, dve_split = sig("x2hl_ready", 1), sig("dve_split", 1)
        logits_done, logits_read = sig("logits_done", 1), sig("logits_read", 1)
        dve_top, top_diff, top_exp = sig("dve_top", 9), sig("top_diff", 1), sig("top_exp", 1)
        comb_ready, comb_turned, chl_ready = sig("comb_ready", 1), sig("comb_turned", 1), sig("chl_ready", 1)
        dve_chl = sig("dve_chl", 1)
        cb_done, cb_ready = sig("cb_done", E0), sig("cb_ready", E0)
        up_done, hh_ready, hl_ready = sig("up_done", NU), sig("hh_ready", NU), sig("hl_ready", NU)
        down_done, ymul = sig("down_done", NU), sig("ymul", E0)
        yadd, y_turned, x2_ready = sig("yadd", E0 - 1), sig("y_turned", 1), sig("x2_ready", 1)
        ca_turned, cth_ready, ctl_ready = sig("ca_turned", 1), sig("cth_ready", 1), sig("ctl_ready", 1)
        xh3_ready, xh3_turned = sig("xh3_ready", 1), sig("xh3_turned", 1)
        x3h_ready, x3l_ready = sig("x3h_ready", 1), sig("x3l_ready", 1)
        u_done, uh_ready, ul_ready = sig("u_done", H1), sig("uh_ready", H1), sig("ul_ready", H1)
        v_done, v_ready = sig("v_done", NK), sig("v_ready", NK)
        a_done, a_max, p_sub, p_exp = sig("a_done", NK), sig("a_max", NK), sig("p_sub", NK), sig("p_exp", NK)
        p_sum, r_ready, p_ready = sig("p_sum", NK), sig("r_ready", NK), sig("p_ready", NK)
        pt_done, pts_ready, pv_done = sig("pt_done", NK), sig("pts_ready", NK), sig("pv_done", NK)
        x3_ready, x3b_ready = sig("x3_ready", 1), sig("x3b_ready", 1)
        xh4_ready, xh4_turned, xh4T_ready = sig("xh4_ready", 1), sig("xh4_turned", 1), sig("xh4T_ready", 1)
        fu_done, fh_ready, fd_done = sig("fu_done", MI), sig("fh_ready", MI), sig("fd_done", MI)
        res_ready = sig("res_ready", 1)

        selw = ytmp[0:ROW2 * 2, :, :].rearrange("p a (h i) -> p (a h) i", i=P)
        w1row = x1[:, :, :].rearrange("p b d -> p (b d)"), x2[:, :, :].rearrange("p b d -> p (b d)")
        win_s, wout_s, b2_rep = xh4T[:, 0:64], xh4T[0:64, 64:192], xh4T[0:64, 192:320]
        bout_row, b2_col = xh4T[:, 320:448], xh4T[0:64, 448:449]
        bin_c, w1_c, b1_c, w2_c = (sm[:, i, 0:MI] for i in range(4))
        wqk_s, wT = work[:, 0:2048], work[:, 2048:4096]
        stage = work[:, 4096:5120].rearrange("p (n f) -> p n f", n=2)

        block = es.enter_context(nc.Block())

        def pick(v, g):
            if g.known():
                return v[g.base + g.off]
            return v[bass.ds(g.base + g.off, 1)].rearrange("o s b d -> (o s) b d")

        def load(sp, signal, dst, src, g):
            sp.dma_start(dst[:, :, :], pick(src, g)).then_inc(signal.sem, 16)

        def store(sp, g):
            sp.dma_start(pick(out_g, g), res[:, :, :]).then_inc(stored.sem, 16)

        def run(body, prologue, last):
            prologue()
            body(Group(0), True)
            with last.Fori(1, NG - 1) as g:
                body(Group(g), True)
            body(Group(NG - 1), False)

        @block.sync
        def _(sp):
            n = 0
            sp.wait_ge(zeroed, 2)
            for dst, src in [
                (wg[0:H0, :], Wi_w), (wg[ROW2:ROW2 + H0, :], Wf_w),
                (gbias[0:H0, :], Wi_b.rearrange("(h o) -> h o", o=1)),
                (gbias[ROW2:ROW2 + H0, :], Wf_b.rearrange("(h o) -> h o", o=1)),
                (gnw[:, :], gn_w.partition_broadcast(P)), (gnb[:, :], gn_b.partition_broadcast(P)),
                (wgate[:, :], gate_w),
            ]:
                sp.dma_start(dst, src).then_inc(set_dma, 16)
            load(sp, x_in, x0, x_g, Group(0))
            load(sp, c_in, c0, c_g, Group(0))
            sp.dma_start(wqk_s[:, 0:1024], w_q).then_inc(proj_in, 16)
            sp.dma_start(wqk_s[:, 1024:2048], w_k).then_inc(proj_in, 16)
            sp.wait_ge(set_dve, 4)
            sp.dma_start(wqk_s[:, 0:1024], w_v).then_inc(proj_in, 16)
            sp.dma_start(wqk_s[:, 1024:2048].rearrange("p (c d) -> p c d", c=8),
                         w_o.rearrange("(c p) d -> p c d", p=P)).then_inc(proj_in, 16)

            for e in range(2 * E0):
                if e >= 2:
                    sp.wait_ge(stage_lo, e - 1)
                src = (w1[e // 2] if e % 2 == 0 else
                       w2[e // 2].rearrange("(c p) d -> p c d", p=P))
                dst = stage[:, e % 2, :]
                if e % 2:
                    dst = dst.rearrange("p (c d) -> p c d", c=FC)
                sp.dma_start(dst, src).then_inc(stage_in[e % 2], 16)
            units = lambda w: w.rearrange("(c m) i -> (m i) c", c=MI)
            for dst, src in [
                (w1row[0], W1[0:32].rearrange("m i -> (m i)").partition_broadcast(P)),
                (w1row[1], W1[32:64].rearrange("m i -> (m i)").partition_broadcast(P)), (win_s, Win), (wout_s, Wout),
                (bout_row, bout.partition_broadcast(P)), (b2_col, b2.rearrange("(m o) -> m o", o=1)),
                (w1_c, units(W1)), (b1_c, units(b1)), (w2_c, units(W2)),
            ]:
                sp.dma_start(dst, src, allow_slow_non_contiguous=True).then_inc(ffn_in, 16)
            for m in range(8):
                rows = slice(16 * m, 16 * m + 16)
                sp.dma_start(bin_c[rows, :], bin_.rearrange("(c m) -> m c", c=MI)[m].partition_broadcast(16),
                             allow_slow_non_contiguous=True).then_inc(ffn_in, 16)
                sp.dma_start(f_out[rows, :, :], Wout.rearrange("(c m) d -> m c d", c=MI)[m].partition_broadcast(16),
                             allow_slow_non_contiguous=True).then_inc(ffn_in, 16)

            def body(g, more):
                if more:
                    sp.wait_ge(x1_ready.sem, x1_ready.at(g))
                    load(sp, x_in, x0, x_g, g.shift(1))
                    sp.wait_ge(caug_ready.sem, caug_ready.at(g))
                    sp.wait_ge(c_turned.sem, c_turned.at(g))
                    load(sp, c_in, c0, c_g, g.shift(1))
                sp.wait_ge(ca_turned.sem, ca_turned.at(g.shift(-1)))
                load(sp, ca_in, cA, c_g, g)
                sp.wait_ge(res_ready.sem, res_ready.at(g))
                store(sp, g)

            run(body, lambda: None, sp)
            sp.wait_ge(stored.sem, stored.at(Group(NG - 1)))

        @block.gpsimd
        def _(pool):
            gp = nc.gpsimd
            gp.memset(gbias[:], 0.0).then_inc(zeroed, 1)
            gp.memset(wg[:], 0.0).then_inc(zeroed, 1)
            gp.memset(acat[:], 0.0)
            gp.memset(ident[:], 0.0)
            gp.memset(mhl[:].bitcast(F32), 0.0)
            gp.memset(chl[:].bitcast(F32), 0.0)
            gp.memset(caug[:], 1.0)
            gp.memset(causal[:], 0.0)
            gp.memset(headmask[:], D0 ** -0.5)
            gp.memset(neg_half[:], -0.5)
            gp.memset(eps_col[:], EPS)
            gp.memset(keep[:], 1.0)
            gp.memset(selw, 0.0)
            gp.memset(drop[:], 0.0).then_inc(set_pool, 1)
            pool.wait_ge(set_pool, 1)
            gp.affine_select(out=ident[:], in_=ident[:], compare_op=ALU.not_equal, fill=1.0, base=0,
                             pattern=[[-1, P]], channel_multiplier=1)
            gp.affine_select(out=causal[:], in_=causal[:], compare_op=ALU.is_ge, fill=-BIG, base=0,
                             pattern=[[1, P]], channel_multiplier=-1)
            gp.affine_select(out=headmask[:], in_=headmask[:], compare_op=ALU.is_ge, fill=0.0, base=0,
                             pattern=[[-D0, H0]], channel_multiplier=1)
            gp.affine_select(out=selw, in_=selw, compare_op=ALU.not_equal, fill=1.0, base=0,
                             pattern=[[-1, 8], [0, P]], channel_multiplier=1)
            gp.affine_select(out=keep[:], in_=keep[:], compare_op=ALU.not_equal, fill=0.0, base=0,
                             pattern=[[0, G], [1, P]], channel_multiplier=0)
            gp.affine_select(out=drop[:], in_=drop[:], compare_op=ALU.not_equal, fill=-3e38, base=0,
                             pattern=[[0, G], [1, P]], channel_multiplier=0)
            gp.iota(expert_no[:], pattern=[[0, G], [1, E0]], base=0, channel_multiplier=0,
                    allow_small_or_imprecise_dtypes=True).then_inc(set_pool, 1)
            pool.wait_ge(set_pool, 2)
            gp.affine_select(out=headmask[:], in_=headmask[:], compare_op=ALU.is_ge, fill=0.0,
                             base=D0 - 1, pattern=[[D0, H0]], channel_multiplier=-1)
            gp.affine_select(out=selw, in_=selw, compare_op=ALU.not_equal, fill=1.0, base=-ROW2,
                             pattern=[[-1, 8], [0, P]], channel_multiplier=1).then_inc(set_pool, 1)

            def rsqrt(i, g, var, n):
                r = rstd[i][:, 0:n]
                pool.wait_ge(ln_var[i].sem, ln_var[i].at(g))
                gp.tensor_tensor(r, var, eps_col[:, 0:n], ALU.add).then_inc(pool_ln[i].sem, 1)
                pool.wait_ge(pool_ln[i].sem, pool_ln[i].at(g))
                gp.tensor_tensor(r, r, neg_half[:, 0:n], ALU.pow).then_inc(ln_rstd[i].sem, 1)

            def front(g):
                rsqrt(0, g, mv[0][:, :, 1], G)
                pool.wait_ge(xhT_ready.sem, xhT_ready.at(g))
                for b in range(G):
                    if b >= 2:
                        pool.wait_ge(s_done.sem, s_done.at(g, 2 * (b - 2) + 2))
                    else:
                        pool.wait_ge(s_done.sem, s_done.at(g.shift(-1)))
                    gp.tensor_tensor(qm[:, b % 2], xhT[:, b, :].unsqueeze(1).to_broadcast([P, H0, P]),
                                     headmask[:, :].unsqueeze(2).to_broadcast([P, H0, P]),
                                     ALU.mult).then_inc(qm_ready.sem, 1)
                rsqrt(4, g, sm[:, 5, :], 32)
                rsqrt(1, g, mv[1][:, :, 1], G)

            def experts(g):
                for e in range(1, E0):
                    pool.wait_ge(ymul.sem, ymul.at(g, e + 1))
                    if e >= 2:
                        pool.wait_ge(yadd.sem, yadd.at(g, e - 1))
                    gp.tensor_tensor(yacc[:, :, :].rearrange("p b d -> p (b d)"),
                                     yacc[:, :, :].rearrange("p b d -> p (b d)"), ytmp[:, e % 2, :],
                                     ALU.add).then_inc(yadd.sem, 1)

            def attention(g):
                rsqrt(2, g, mv[2][:, :, 1], G)
                for k in range(NK):
                    pool.wait_ge(r_ready.sem, r_ready.at(g, k + 1))
                    gp.tensor_tensor(pr[:, k % 3], pr[:, k % 3],
                                     pm[:, k % 3, 2, :].unsqueeze(2).to_broadcast([P, HQ, P]),
                                     ALU.mult).then_inc(p_ready.sem, 1)
                rsqrt(3, g, mv[3][:, :, 1], G)
                pool.wait_ge(x3_ready.sem, x3_ready.at(g))
                pool.wait_ge(stored.sem, stored.at(g.shift(-1)))
                gp.tensor_tensor(x3b[:], x3[:], f_last[:, :].unsqueeze(1).to_broadcast([P, G, P]),
                                 ALU.add).then_inc(x3b_ready.sem, 1)

            def body(g, more):
                experts(g)
                if more:
                    front(g.shift(1))
                attention(g)

            run(body, lambda: front(Group(0)), pool)

        @block.scalar
        def _(act):
            sc = nc.scalar
            act.preload_act_table_set("natural_log_exp_and_others")

            def setup():
                act.wait_ge(set_pe, 1)
                sc.activation(wgx[:], TB[:, 0:64], ACT.Copy)
                sc.activation(wgc[:], TB[:, 64:128], ACT.Copy).then_inc(set_act, 1)
                n_pe, n_act = 1, 1
                for w in range(3):
                    for half in range(2):
                        n_pe += 1
                        act.wait_ge(set_pe, n_pe)
                        dst = wT[:, 1024 * (w % 2) + 512 * half:1024 * (w % 2) + 512 * half + 512]
                        sc.activation(dst, UP[half][:, :], ACT.Copy).then_inc(set_act, 1)
                    if w == 0:
                        continue
                    hi = wqk_h if w == 1 else wvo_h
                    scale = D1 ** -0.5 if w == 1 else 1.0
                    for q in range(4):
                        n_pe += 1
                        act.wait_ge(set_pe, n_pe)
                        dst = hi[:, :, :].rearrange("p (i two) d -> p two i d", two=2)[:, q % 2, 4 * (q // 2):4 * (q // 2) + 4]
                        sc.activation(dst, YB[q % 2][:, :].rearrange("p (i d) -> p i d", i=4),
                                      ACT.Copy, scale=scale).then_inc(set_act, 1)
                for e in range(2 * E0):
                    act.wait_ge(stage_in[e % 2], 16 * (e // 2 + 1))
                    hi = w1h[:, e // 2, :] if e % 2 == 0 else w2h[:, FC * (e // 2):FC * (e // 2) + FC, :].rearrange("p c d -> p (c d)")
                    sc.activation(hi, stage[:, e % 2, :], ACT.Copy).then_inc(stage_hi, 1)

            def front(g):
                act.wait_ge(xh1_turned.sem, xh1_turned.at(g))
                act.wait_ge(s_done.sem, s_done.at(g.shift(-1)))
                sc.activation(xhT[:].rearrange("p b d -> p (b d)"), TB[:, :], ACT.Copy).then_inc(xhT_ready.sem, 1)
                act.wait_ge(c_turned.sem, c_turned.at(g))
                act.wait_ge(h_done.sem, h_done.at(g.shift(-1)))
                sc.activation(caug[:, :, :, 0:D0], c0[:, :, :].rearrange("p b (h d) -> p b h d", h=H0),
                              ACT.Copy).then_inc(caug_ready.sem, 1)
                sc.activation(cT[:].rearrange("p b d -> p (b d)"), TB[:, :], ACT.Copy).then_inc(cT_ready.sem, 1)
                act.wait_ge(gates_done.sem, gates_done.at(g))
                act.wait_ge(dve_rows.sem, dve_rows.at(g.shift(-1)))
                sc.activation(frow[:], TB[ROW2:ROW2 + H0, :], ACT.Identity,
                              bias=gbias[ROW2:ROW2 + H0, :]).then_inc(act_gates.sem, 1)
                sc.activation(irow[:], TB[0:H0, :], ACT.Identity, bias=gbias[0:H0, :]).then_inc(gates_read.sem, 1)
                act.wait_ge(act_gates.sem, act_gates.at(g, 1))
                sc.activation(trow[:], frow[:], ACT.Abs).then_inc(act_gates.sem, 1)
                act.wait_ge(act_gates.sem, act_gates.at(g, 2))
                sc.activation(trow[:], trow[:], ACT.Exp, scale=-1.0).then_inc(act_gates.sem, 1)
                act.wait_ge(act_gates.sem, act_gates.at(g, 3))
                sc.activation(trow[:], trow[:], ACT.Ln, bias=1.0).then_inc(softplus_ready.sem, 1)
                act.wait_ge(acat_turned.sem, acat_turned.at(g))
                act.wait_ge(x1_ready.sem, x1_ready.at(g.shift(-1)))
                tb = TB[:, :].rearrange("p (b r) -> p b r", b=G)
                sc.activation(acol[:], tb[:, :, 0:H0], ACT.Copy)
                sc.activation(emd[:], tb[:, :, ROW2:ROW2 + H0], ACT.Exp, scale=-1.0).then_inc(acol_ready.sem, 1)
                for k in range(2 * G + 1):
                    if k < 2 * G:
                        act.wait_ge(e_added.sem, e_added.at(g, k + 1))
                        sc.activation(ex[:, k % 2], ex[:, k % 2], ACT.Exp).then_inc(e_exp.sem, 1)
                    if k >= 2 and k % 2 == 0:
                        b = k // 2 - 1
                        act.wait_ge(h_done.sem, h_done.at(g, 2 * b + 2))
                        sc.activation(hs[:, H0 * b:H0 * b + H0, :].rearrange("p h d -> p (h d)"),
                                      HB[:, 0:H0 * (D0 + 1)], ACT.Copy).then_inc(hs_ready.sem, 1)
                act.wait_ge(xh2_turned.sem, xh2_turned.at(g))
                sc.activation(xh2T[:].rearrange("p b d -> p (b d)"), TB[:, :], ACT.Copy).then_inc(xh2T_ready.sem, 1)
                act.wait_ge(logits_done.sem, logits_done.at(g))
                sc.activation(logit[:].rearrange("p b e -> p (b e)"), TB[:, 0:G * E0], ACT.Copy).then_inc(logits_read.sem, 1)
                act.wait_ge(top_diff.sem, top_diff.at(g))
                sc.activation(pe12[:, 1, :], pe12[:, 0, :], ACT.Exp).then_inc(top_exp.sem, 1)

            def experts(g):
                for u in range(NU):
                    e = u // FC
                    if u % FC == 0:
                        act.wait_ge(cb_done.sem, cb_done.at(g, e + 1))
                        if e >= 2:
                            act.wait_ge(ymul.sem, ymul.at(g, e - 1))
                        else:
                            act.wait_ge(ymul.sem, ymul.at(g.shift(-1)))
                        sc.activation(cb[:, e % 2, :], TB[:, :], ACT.Copy).then_inc(cb_ready.sem, 1)
                    act.wait_ge(up_done.sem, up_done.at(g, u + 1))
                    if u >= 4:
                        act.wait_ge(down_done.sem, down_done.at(g, u - 3))
                    sc.activation(uh[:, u % 4, :], UP[u % 2][:, :], ACT.Relu).then_inc(hh_ready.sem, 1)

            def attention(g):
                act.wait_ge(ca_turned.sem, ca_turned.at(g))
                sc.activation(cTh[:].rearrange("p b d -> p (b d)"), TB[:, :], ACT.Copy).then_inc(cth_ready.sem, 1)
                act.wait_ge(xh3_turned.sem, xh3_turned.at(g))
                sc.activation(x3h[:].rearrange("p b d -> p (b d)"), TB[:, :], ACT.Copy).then_inc(x3h_ready.sem, 1)

                def key_side(q):
                    for h in range(HQ * q, HQ * q + HQ):
                        act.wait_ge(u_done.sem, u_done.at(g, h + 1))
                        sc.activation(uh[:, h % HQ, :], UP[0][:, :], ACT.Copy).then_inc(uh_ready.sem, 1)

                def turned(k):
                    act.wait_ge(pt_done.sem, pt_done.at(g, k + 1))
                    if k >= 2:
                        act.wait_ge(pv_done.sem, pv_done.at(g, k - 1))
                    sc.activation(pts[:, k % 2].rearrange("p h i -> p (h i)"), PTB[k % 2][:, :],
                                  ACT.Copy).then_inc(pts_ready.sem, 1)

                def values(k):
                    act.wait_ge(v_done.sem, v_done.at(g, k + 1))
                    if k >= 2:
                        act.wait_ge(pv_done.sem, pv_done.at(g, k - 1))
                    sc.activation(vv[:, k % 2].rearrange("p h i -> p (h i)"), UP[1][:, :],
                                  ACT.Copy).then_inc(v_ready.sem, 1)

                key_side(0)
                for k in range(NK + 2):
                    if k >= 2:
                        turned(k - 2)
                    if k < NK:
                        act.wait_ge(p_sub.sem, p_sub.at(g, k + 1))
                        sc.activation(pr[:, k % 3], pr[:, k % 3], ACT.Exp).then_inc(p_exp.sem, 1)
                    if 1 <= k < NK + 1:
                        values(k - 1)
                    if k % HQ == HQ - 1 and k < NK - 1:
                        key_side(k // HQ + 1)
                act.wait_ge(xh4_turned.sem, xh4_turned.at(g))
                sc.activation(xh4T, TB[:, :], ACT.Copy).then_inc(xh4T_ready.sem, 1)
                for c in range(MI):
                    act.wait_ge(fu_done.sem, fu_done.at(g, c + 1))
                    if c >= 2:
                        act.wait_ge(fd_done.sem, fd_done.at(g, c - 1))
                    sc.activation(fh[:, c % 2, :], UP[c % 2][:, :], ACT.Relu,
                                  bias=f_bias[:, c:c + 1]).then_inc(fh_ready.sem, 1)

            def body(g, more):
                experts(g)
                if more:
                    front(g.shift(1))
                attention(g)

            def prologue():
                setup()
                front(Group(0))

            run(body, prologue, act)

        @block.vector
        def _(dve):
            v = nc.vector
            ln_chain = [Chain(s, dve) for s in dve_ln]
            rows, gn, tp = Chain(dve_rows, dve), Chain(dve_gn, dve), Chain(dve_top, dve)

            def setup():
                dve.wait_ge(set_pool, 3)
                v.tensor_copy(sel[:], selw)
                v.tensor_copy(ident_bf[:], ident[:]).then_inc(fold_in, 1)
                dve.wait_ge(set_dma, 16 * 7)
                v.tensor_tensor(wg[:, P:2 * P], wg[:, P:2 * P], wg[:, 2 * P:3 * P], ALU.add).then_inc(fold_in, 1)
                n_act = 1
                for w in range(3):
                    n_act += 2
                    if w == 0:
                        continue
                    hi, lo = (wqk_h, wqk_l) if w == 1 else (wvo_h, wvo_l)
                    scale = D1 ** -0.5 if w == 1 else 1.0
                    for q in range(4):
                        n_act += 1
                        dve.wait_ge(set_act, n_act)
                        view = lambda t: t[:, :, :].rearrange("p (i two) d -> p two i d", two=2)[:, q % 2, 4 * (q // 2):4 * (q // 2) + 4]
                        v.scalar_tensor_tensor(view(lo), YB[q % 2][:, :].rearrange("p (i d) -> p i d", i=4), scale,
                                               view(hi), ALU.mult, ALU.subtract).then_inc(set_dve, 1)
                for e in range(2 * E0):
                    dve.wait_ge(stage_hi, e + 1)
                    if e % 2 == 0:
                        hi, lo = w1h[:, e // 2, :], w1l[:, e // 2, :]
                    else:
                        hi, lo = (t[:, FC * (e // 2):FC * (e // 2) + FC, :].rearrange("p c d -> p (c d)") for t in (w2h, w2l))
                    v.tensor_tensor(lo, stage[:, e % 2, :], hi, ALU.subtract).then_inc(stage_lo, 1)
                dve.wait_ge(ffn_in, 16 * 25)
                v.tensor_copy(b2_rep, b2_col.to_broadcast([64, P])).then_inc(ffn_fold, 1)
                v.tensor_tensor(bin_c, bin_c, w1_c, ALU.mult).then_inc(ffn_fold, 1)
                for n in range(2):
                    v.tensor_tensor(f_in[:, 512 * n:512 * n + 512].rearrange("p (m i) -> p m i", i=16),
                                    win_s[:, 32 * n:32 * n + 32].unsqueeze(2).to_broadcast([P, 32, 16]),
                                    w1row[n].rearrange("p (m i) -> p m i", i=16), ALU.mult)
                v.tensor_tensor(f_out[:], f_out[:], w2_c.unsqueeze(2).to_broadcast([P, MI, P]), ALU.mult)
                dve.wait_ge(ffn_fold, 2)
                v.tensor_tensor(f_bias[:], bin_c, b1_c, ALU.add)
                dve.wait_ge(ffn_pe, 1)
                v.tensor_tensor(f_last[:], TB[:, 0:P], bout_row, ALU.add).then_inc(ffn_fold, 1)

            def normalise(i, g, src, dst, ready):
                ch = ln_chain[i]
                ch.begin(g)
                for b in range(G):
                    last = v.bn_stats(stats[:, b, :], src[:, b, :])
                ch.link(last)
                v.memset(spare[:, :], 0.0)
                for b in range(G):
                    last = v.bn_aggr(mv[i][:, b, :], stats[:, b, :])
                last.then_inc(ln_var[i].sem, 1)
                dve.wait_ge(ln_rstd[i].sem, ln_rstd[i].at(g))
                for b in range(G):
                    last = v.tensor_scalar(dst[:, b, :], src[:, b, :], mv[i][:, b, 0:1],
                                           rstd[i][:, b:b + 1], ALU.subtract, ALU.mult)
                last.then_inc(ready.sem, 1)

            def front(g):
                dve.wait_ge(x_in.sem, x_in.at(g))
                dve.wait_ge(xh2_turned.sem, xh2_turned.at(g.shift(-1)))
                normalise(0, g, x0, xh, xh1_ready)
                dve.wait_ge(softplus_ready.sem, softplus_ready.at(g))
                dve.wait_ge(gates_read.sem, gates_read.at(g))
                rows.begin(g)
                rows.link(v.scalar_tensor_tensor(trow[:], frow[:], 0.0, trow[:], ALU.min, ALU.subtract))
                rows.link(v.tensor_tensor_scan(frow[:], keep[:], trow[:], 0.0, ALU.mult, ALU.add))
                rows.link(v.tensor_tensor(acat[0:H0, :], irow[:], frow[:], ALU.subtract))
                rows.link(v.tensor_tensor_scan(trow[:], drop[:], acat[0:H0, :], 0.0, ALU.add, ALU.max))
                v.tensor_tensor(acat[ROW2:ROW2 + H0, :], frow[:], trow[:], ALU.add).then_inc(acat_ready.sem, 1)
                dve.wait_ge(d_done.sem, d_done.at(g.shift(-1)))
                mh = mhl[:].rearrange("p b d -> p (b d)")
                rows.link(v.tensor_scalar(mh[0:H0, :], trow[:], -1.0, None, ALU.mult))
                rows.link(v.scalar_tensor_tensor(mh[ROW2:ROW2 + H0, :], trow[:], -1.0, mh[0:H0, :],
                                                 ALU.mult, ALU.subtract))
                rows.end()
                dve.wait_ge(acol_ready.sem, acol_ready.at(g))

                def decay(k):
                    b, hf = k // 2, k % 2
                    dve.wait_ge(d_done.sem, d_done.at(g, k + 1))
                    dve.wait_ge(h_done.sem, h_done.at(g, k - 1))
                    v.tensor_tensor(ex[:, k % 2], DB[:, :].rearrange("p (h i) -> p h i", h=4),
                                    acol[:, b, 4 * hf:4 * hf + 4].unsqueeze(2).to_broadcast([P, 4, P]),
                                    ALU.add).then_inc(e_added.sem, 1)

                def weigh(k):
                    dve.wait_ge(s_done.sem, s_done.at(g, k + 1))
                    dve.wait_ge(e_exp.sem, e_exp.at(g, k + 1))
                    v.tensor_tensor(ex[:, k % 2], SB[:, :].rearrange("p (h i) -> p h i", h=4),
                                    ex[:, k % 2], ALU.mult).then_inc(c_done.sem, 1)

                decay(0)
                for k in range(2 * G):
                    if k + 1 < 2 * G:
                        decay(k + 1)
                    weigh(k)
                dve.wait_ge(hs_ready.sem, hs_ready.at(g))
                gn.begin(g)
                R = G * H0
                wide = lambda ap: ap.unsqueeze(2).to_broadcast([P, R, D0])
                gn.link(v.scalar_tensor_tensor(sm[:, 0, :], hs[:, :, D0], -1.0, hs[:, :, D0], ALU.mult, ALU.max))
                gn.link(v.tensor_tensor(sm[:, 0, :], sm[:, 0, :], emd[:].rearrange("p b h -> p (b h)"), ALU.max))
                gn.link(v.tensor_scalar(sm[:, 1, :], sm[:, 0, :], 1e-6, None, ALU.add))
                gn.link(v.reciprocal(sm[:, 2, :], sm[:, 1, :]))
                gn.link(v.tensor_tensor(hn[:], hs[:, :, 0:D0], wide(sm[:, 2, :]), ALU.mult))
                gn.link(v.reduce_sum(sm[:, 3, :], hn[:], AX))
                gn.link(v.scalar_tensor_tensor(hn[:], wide(sm[:, 3, :]), -1.0 / D0, hn[:], ALU.mult, ALU.add))
                gn.link(v.tensor_tensor(hq[:], hn[:], hn[:], ALU.mult))
                gn.link(v.reduce_sum(sm[:, 4, :], hq[:], AX))
                v.tensor_scalar(sm[:, 5, :], sm[:, 4, :], 1.0 / D0, None, ALU.mult).then_inc(ln_var[4].sem, 1)
                dve.wait_ge(ln_rstd[4].sem, ln_rstd[4].at(g))
                gn.link(v.tensor_tensor(hn[:], hn[:], wide(rstd[4][:, :]), ALU.mult))
                hb = hn[:].rearrange("p (b h) d -> p b (h d)", b=G)
                row = lambda t: t[:, :].unsqueeze(1).to_broadcast([P, G, P])
                gn.link(v.tensor_tensor(hb, hb, row(gnw), ALU.mult))
                gn.link(v.tensor_tensor(hb, hb, row(gnb), ALU.add))
                dve.wait_ge(x2_ready.sem, x2_ready.at(g.shift(-1)))
                gn.end()
                v.tensor_tensor(x1[:], hb, x0[:], ALU.add).then_inc(x1_ready.sem, 1)
                dve.wait_ge(x1_ready.sem, x1_ready.at(g))
                dve.wait_ge(xh1_turned.sem, xh1_turned.at(g))
                normalise(1, g, x1, xh, xh2_ready)
                dve.wait_ge(xh2T_ready.sem, xh2T_ready.at(g))
                dve.wait_ge(up_done.sem, up_done.at(g.shift(-1)))
                xs = xh2T[:].rearrange("p b d -> p (b d)")
                v.tensor_copy(x2h[:], xs).then_inc(dve_split.sem, 1)
                dve.wait_ge(dve_split.sem, dve_split.at(g))
                v.tensor_tensor(x2l[:], xs, x2h[:], ALU.subtract).then_inc(x2hl_ready.sem, 1)
                dve.wait_ge(logits_read.sem, logits_read.at(g))
                dve.memset(spare[:, :], 0.0)
                tp.begin(g)
                for b in range(G):
                    last = v.max(top[:, b, :], logit[:, b, :])
                tp.link(last)
                v.memset(spare[:, :], 0.0)
                for b in range(G):
                    last = v.max_index(topi[:, b, :], top[:, b, :], logit[:, b, :])
                tp.link(last)
                v.tensor_tensor(pe12[:, 0, :], top[:, :, 1], top[:, :, 0], ALU.subtract).then_inc(top_diff.sem, 1)
                tp.link(v.tensor_copy(topf[:], topi[:, :, 0:2]))
                wide2 = lambda ap: ap.unsqueeze(2).to_broadcast([P, G, E0])
                v.tensor_tensor(comb[:, 0], expert_no[:], wide2(topf[:, :, 0]), ALU.is_equal)
                tp.link(v.tensor_tensor(comb[:, 1], expert_no[:], wide2(topf[:, :, 1]), ALU.is_equal))
                dve.wait_ge(top_exp.sem, top_exp.at(g))
                tp.link(v.tensor_scalar(pe12[:, 2, :], pe12[:, 1, :], 1.0, None, ALU.add))
                tp.link(v.reciprocal(pe12[:, 3, :], pe12[:, 2, :]))
                tp.link(v.tensor_tensor(pe12[:, 2, :], pe12[:, 1, :], pe12[:, 3, :], ALU.mult))
                tp.link(v.tensor_tensor(comb[:, 0], comb[:, 0], wide2(pe12[:, 3, :]), ALU.mult))
                tp.link(v.tensor_tensor(comb[:, 1], comb[:, 1], wide2(pe12[:, 2, :]), ALU.mult))
                tp.end()
                dve.wait_ge(comb_turned.sem, comb_turned.at(g.shift(-1)))
                v.tensor_tensor(comb[:, 2], comb[:, 0], comb[:, 1], ALU.add).then_inc(comb_ready.sem, 1)
                dve.wait_ge(comb_turned.sem, comb_turned.at(g))
                dve.wait_ge(cb_done.sem, cb_done.at(g.shift(-1)))
                v.tensor_copy(chl[0:E0, :], TB[0:E0, :]).then_inc(dve_chl.sem, 1)
                dve.wait_ge(dve_chl.sem, dve_chl.at(g))
                v.tensor_tensor(chl[ROW2:ROW2 + E0, :], TB[0:E0, :], chl[0:E0, :],
                                ALU.subtract).then_inc(chl_ready.sem, 1)

            def experts(g):
                def scale_out(e):
                    dve.wait_ge(down_done.sem, down_done.at(g, FC * e + FC))
                    dve.wait_ge(cb_ready.sem, cb_ready.at(g, e + 1))
                    if e == 0:
                        dve.wait_ge(y_turned.sem, y_turned.at(g.shift(-1)))
                        dst = yacc[:].rearrange("p b d -> p (b d)")
                    else:
                        if e >= 3:
                            dve.wait_ge(yadd.sem, yadd.at(g, e - 2))
                        else:
                            dve.wait_ge(yadd.sem, yadd.at(g.shift(-1)))
                        dst = ytmp[:, e % 2, :]
                    v.tensor_tensor(dst, YB[e % 2][:, :], cb[:, e % 2, :], ALU.mult).then_inc(ymul.sem, 1)

                for u in range(NU):
                    dve.wait_ge(hh_ready.sem, hh_ready.at(g, u + 1))
                    v.scalar_tensor_tensor(ul[:, u % 4, :], UP[u % 2][:, :], 0.0, uh[:, u % 4, :],
                                           ALU.max, ALU.subtract).then_inc(hl_ready.sem, 1)
                    if u % FC == 2 and u > FC:
                        scale_out(u // FC - 1)
                scale_out(E0 - 1)
                dve.wait_ge(y_turned.sem, y_turned.at(g))
                v.tensor_tensor(x2[:].rearrange("p b d -> p (b d)"), TB[:, :],
                                x1[:].rearrange("p b d -> p (b d)"), ALU.add).then_inc(x2_ready.sem, 1)

            def attention(g):
                dve.wait_ge(cth_ready.sem, cth_ready.at(g))
                flat = lambda t: t[:].rearrange("p b d -> p (b d)")
                v.tensor_tensor(flat(cTl), TB[:, :], flat(cTh), ALU.subtract).then_inc(ctl_ready.sem, 1)
                dve.wait_ge(x2_ready.sem, x2_ready.at(g))
                dve.wait_ge(xh4_turned.sem, xh4_turned.at(g.shift(-1)))
                normalise(2, g, x2, xg, xh3_ready)
                dve.wait_ge(x3h_ready.sem, x3h_ready.at(g))
                v.tensor_tensor(flat(x3l), TB[:, :], flat(x3h), ALU.subtract).then_inc(x3l_ready.sem, 1)

                def key_side(q):
                    for h in range(HQ * q, HQ * q + HQ):
                        dve.wait_ge(uh_ready.sem, uh_ready.at(g, h + 1))
                        v.tensor_tensor(ul[:, h % HQ, :], UP[0][:, :], uh[:, h % HQ, :],
                                        ALU.subtract).then_inc(ul_ready.sem, 1)

                def row_max(k):
                    s = YB[k % 2][:, :].rearrange("p (h j) -> p h j", h=HQ)
                    dve.wait_ge(a_done.sem, a_done.at(g, k + 1))
                    if k >= 3:
                        dve.wait_ge(pt_done.sem, pt_done.at(g, k - 2))
                    v.reduce_max(pm[:, k % 3, 0, :], s, AX).then_inc(a_max.sem, 1)
                    dve.wait_ge(a_max.sem, a_max.at(g, k + 1))
                    v.tensor_tensor(pr[:, k % 3], s, pm[:, k % 3, 0, :].unsqueeze(2).to_broadcast([P, HQ, P]),
                                    ALU.subtract).then_inc(p_sub.sem, 1)

                def row_sum(k):
                    dve.wait_ge(p_exp.sem, p_exp.at(g, k + 1))
                    v.reduce_sum(pm[:, k % 3, 1, :], pr[:, k % 3], AX).then_inc(p_sum.sem, 1)
                    dve.wait_ge(p_sum.sem, p_sum.at(g, k + 1))
                    v.reciprocal(pm[:, k % 3, 2, :], pm[:, k % 3, 1, :]).then_inc(r_ready.sem, 1)

                key_side(0)
                for k in range(NK + 1):
                    if k < NK:
                        row_max(k)
                    if k >= 1:
                        row_sum(k - 1)
                    if k % HQ == HQ - 1 and k < NK - 1:
                        key_side(k // HQ + 1)
                dve.wait_ge(pv_done.sem, pv_done.at(g))
                v.tensor_tensor(flat(x3), HB[:, :], flat(x2), ALU.add).then_inc(x3_ready.sem, 1)
                dve.wait_ge(x3_ready.sem, x3_ready.at(g))
                dve.wait_ge(xh3_turned.sem, xh3_turned.at(g))
                normalise(3, g, x3, xg, xh4_ready)
                dve.wait_ge(fd_done.sem, fd_done.at(g))
                dve.wait_ge(x3b_ready.sem, x3b_ready.at(g))
                v.tensor_tensor(flat(res), YB[0][:, :], flat(x3b), ALU.add).then_inc(res_ready.sem, 1)

            def body(g, more):
                experts(g)
                if more:
                    front(g.shift(1))
                attention(g)

            def prologue():
                setup()
                front(Group(0))

            run(body, prologue, dve)

        @block.tensor
        def _(pe):
            def split(o, lh, ll, rh, rl, start, stop):
                pe.matmul(o, lh, rh, start=start, stop=False)
                pe.matmul(o, lh, rl, start=False, stop=False)
                return pe.matmul(o, ll, rh, start=False, stop=stop)

            def turn(src, signal):
                for b in range(G):
                    last = pe.transpose(TB[:, P * b:P * b + P], src[:, b, :], ident[:])
                last.then_inc(signal.sem, 1)

            def setup():
                pe.wait_ge(fold_in, 2)
                pe.transpose(TB[:, 0:64], wg[:, 0:P], ident[0:64, 0:64])
                pe.transpose(TB[:, 64:128], wg[:, P:2 * P], ident[0:64, 0:64]).then_inc(set_pe, 1)
                n_act = 1
                for w in range(3):
                    pe.wait_ge(proj_in, 16 * (2 if w < 2 else 4))
                    for half in range(2):
                        if w:
                            pe.wait_ge(set_act, n_act - 1 + half if w == 1 else n_act)
                        for i in range(4):
                            c = 4 * half + i
                            col = 1024 * (w % 2) + P * c
                            last = pe.transpose(UP[half][:, P * i:P * i + P], wqk_s[:, col:col + P], ident[:])
                        last.then_inc(set_pe, 1)
                    n_act += 2
                    if w == 0:
                        continue
                    pe.wait_ge(set_act, n_act)
                    for q in range(4):
                        if q >= 2 or w == 2:
                            pe.wait_ge(set_dve, 4 * (w - 1) + q - 1)
                        par, lo = q % 2, 4 * (q // 2)
                        rows = slice(64 * par, 64 * par + 64)
                        for i in range(4):
                            c = lo + i
                            if w == 1:
                                lhs = wT[rows, 1024 + P * c:1024 + P * c + P]
                                rhs = wT[rows, P * c:P * c + P]
                            else:
                                lhs = wT[rows, P * c:P * c + P]
                                rhs = wqk_s[rows, 1024 + P * c:1024 + P * c + P]
                            last = pe.matmul(YB[par][:, P * i:P * i + P], lhs, rhs, start=True, stop=True)
                        last.then_inc(set_pe, 1)
                    n_act += 4
                pe.wait_ge(ffn_fold, 1)
                pe.matmul(TB[:, 0:P], b2_rep, wout_s, start=True, stop=True).then_inc(ffn_pe, 1)
                pe.wait_ge(ffn_fold, 3)

            def front(g):
                pe.wait_ge(xh1_ready.sem, xh1_ready.at(g))
                turn(xh, xh1_turned)
                pe.wait_ge(c_in.sem, c_in.at(g))
                pe.wait_ge(xhT_ready.sem, xhT_ready.at(g))
                turn(c0, c_turned)
                pe.wait_ge(cT_ready.sem, cT_ready.at(g))
                flat = lambda t: t[:].rearrange("p b d -> p (b d)")
                pe.matmul(TB[0:64, :], wgx[:], flat(xhT), start=True, stop=False)
                pe.matmul(TB[0:64, :], wgc[:], flat(cT), start=False, stop=True).then_inc(gates_done.sem, 1)
                pe.wait_ge(gates_read.sem, gates_read.at(g))
                pe.wait_ge(act_gates.sem, act_gates.at(g, 1))
                pe.wait_ge(acat_ready.sem, acat_ready.at(g))
                for b in range(G):
                    last = pe.transpose(TB[:, P * b:P * b + P], acat[:, P * b:P * b + P], ident[:])
                last.then_inc(acat_turned.sem, 1)

                def decay(k):
                    b, hf = k // 2, k % 2
                    pe.wait_ge(e_added.sem, e_added.at(g, k))
                    if k == 0:
                        pe.wait_ge(dve_rows.sem, dve_rows.at(g))
                    pe.matmul(DB[:, :], ident_bf[:], causal[:, :].unsqueeze(1).to_broadcast([P, 4, P]),
                              start=True, stop=True)
                    for i in range(4):
                        last = pe.matmul(DB[:, P * i:P * i + P], sel[:, 4 * hf + i, :], mhl[:, b, :],
                                         start=False, stop=True, skip_group_check=True)
                    last.then_inc(d_done.sem, 1)

                def scores(k):
                    b, hf = k // 2, k % 2
                    pe.wait_ge(c_done.sem, c_done.at(g, k))
                    pe.wait_ge(qm_ready.sem, qm_ready.at(g, b + 1))
                    pe.matmul(SB[:, :], cT[:, b, :], qm[:, b % 2, 4 * hf:4 * hf + 4, :].rearrange("p h i -> p (h i)"),
                              start=True, stop=True).then_inc(s_done.sem, 1)

                def outputs(k):
                    b, hf = k // 2, k % 2
                    pe.wait_ge(c_done.sem, c_done.at(g, k + 1))
                    pe.wait_ge(caug_ready.sem, caug_ready.at(g))
                    if hf == 0:
                        pe.wait_ge(hs_ready.sem, hs_ready.at(g, b))
                    for i in range(4):
                        h = 4 * hf + i
                        last = pe.matmul(HB[:, h * (D0 + 1):(h + 1) * (D0 + 1)], ex[:, k % 2, i, :],
                                         caug[:, b, h, :], start=True, stop=True)
                    last.then_inc(h_done.sem, 1)

                for k in range(2 * G + 1):
                    if k < 2 * G:
                        decay(k)
                        scores(k)
                    if k >= 1:
                        outputs(k - 1)
                pe.wait_ge(xh2_ready.sem, xh2_ready.at(g))
                turn(xh, xh2_turned)
                pe.wait_ge(xh2T_ready.sem, xh2T_ready.at(g))
                for b in range(G):
                    last = pe.matmul(TB[:, E0 * b:E0 * b + E0], xh2T[:, b, :], wgate[:], start=True, stop=True)
                last.then_inc(logits_done.sem, 1)
                pe.wait_ge(comb_ready.sem, comb_ready.at(g))
                for b in range(G):
                    last = pe.transpose(TB[0:E0, P * b:P * b + P], comb[:, 2, b, :], ident[:])
                last.then_inc(comb_turned.sem, 1)
                pe.wait_ge(chl_ready.sem, chl_ready.at(g))

            def experts(g):
                pe.wait_ge(x2hl_ready.sem, x2hl_ready.at(g))
                pe.wait_ge(chl_ready.sem, chl_ready.at(g))

                def up(u):
                    e, c = u // FC, u % FC
                    if c == 0:
                        if e:
                            pe.wait_ge(cb_ready.sem, cb_ready.at(g, e))
                        pe.matmul(TB[:, :], sel[:, e, :], chl[:, :], start=True, stop=True).then_inc(cb_done.sem, 1)
                    if u >= 2:
                        pe.wait_ge(hl_ready.sem, hl_ready.at(g, u - 1))
                    cols = slice(P * c, P * c + P)
                    split(UP[u % 2][:, :], w1h[:, e, cols], w1l[:, e, cols], x2h[:], x2l[:],
                          True, True).then_inc(up_done.sem, 1)

                def down(u):
                    e, c = u // FC, u % FC
                    pe.wait_ge(hl_ready.sem, hl_ready.at(g, u + 1))
                    if c == 0 and e >= 2:
                        pe.wait_ge(ymul.sem, ymul.at(g, e - 1))
                    elif u == 0:
                        pe.wait_ge(res_ready.sem, res_ready.at(g.shift(-1)))
                    split(YB[e % 2][:, :], w2h[:, u, :], w2l[:, u, :], uh[:, u % 4, :], ul[:, u % 4, :],
                          c == 0, c == FC - 1).then_inc(down_done.sem, 1)

                for u in range(NU + 2):
                    if u < NU:
                        up(u)
                    if u >= 2:
                        down(u - 2)
                pe.wait_ge(yadd.sem, yadd.at(g))
                pe.wait_ge(cb_ready.sem, cb_ready.at(g))
                turn(yacc, y_turned)

            def attention(g):
                pe.wait_ge(ca_in.sem, ca_in.at(g))
                pe.wait_ge(x2_ready.sem, x2_ready.at(g))
                turn(cA, ca_turned)
                pe.wait_ge(ctl_ready.sem, ctl_ready.at(g))
                pe.wait_ge(xh3_ready.sem, xh3_ready.at(g))
                turn(xg, xh3_turned)

                def key_side(q):
                    for h in range(HQ * q, HQ * q + HQ):
                        if h == 0:
                            pe.wait_ge(hl_ready.sem, hl_ready.at(g))
                        else:
                            pe.wait_ge(ul_ready.sem, ul_ready.at(g, h))
                        split(UP[0][:, :], wqk_h[:, h, :], wqk_l[:, h, :], cTh[:].rearrange("p b d -> p (b d)"),
                              cTl[:].rearrange("p b d -> p (b d)"), True, True).then_inc(u_done.sem, 1)

                def scores(k):
                    q, b = k // G, k % G
                    if k == 0:
                        pe.wait_ge(x3l_ready.sem, x3l_ready.at(g))
                    if b == 0:
                        pe.wait_ge(ul_ready.sem, ul_ready.at(g, HQ * (q + 1)))
                    if k >= 2:
                        pe.wait_ge(p_sub.sem, p_sub.at(g, k - 1))
                    cols = slice(P * b, P * b + P)
                    split(YB[k % 2][:, :].rearrange("p (h j) -> p h j", h=HQ), x3h[:, b, :], x3l[:, b, :],
                          uh[:, :, cols], ul[:, :, cols], True, True).then_inc(a_done.sem, 1)

                def values(k):
                    q, b = k // G, k % G
                    if k:
                        pe.wait_ge(v_ready.sem, v_ready.at(g, k))
                    cols = slice(HQ * q, HQ * q + HQ)
                    split(UP[1][:, :].rearrange("p (h j) -> p h j", h=HQ), cTh[:, b, :], cTl[:, b, :],
                          wvo_h[:, cols, :], wvo_l[:, cols, :], True, True).then_inc(v_done.sem, 1)

                def turn_probs(k):
                    pe.wait_ge(p_ready.sem, p_ready.at(g, k + 1))
                    if k >= 2:
                        pe.wait_ge(pts_ready.sem, pts_ready.at(g, k - 1))
                    for i in range(HQ):
                        last = pe.transpose(PTB[k % 2][:, P * i:P * i + P], pr[:, k % 3, i, :], ident[:])
                    last.then_inc(pt_done.sem, 1)

                def weighted(k):
                    q, b = k // G, k % G
                    pe.wait_ge(pts_ready.sem, pts_ready.at(g, k + 1))
                    pe.wait_ge(v_ready.sem, v_ready.at(g, k + 1))
                    for i in range(HQ):
                        last = pe.matmul(HB[:, P * b:P * b + P], pts[:, k % 2, i, :], vv[:, k % 2, i, :],
                                         start=(k == 0 and i == 0), stop=(q == 3 and i == HQ - 1),
                                         skip_group_check=True)
                    last.then_inc(pv_done.sem, 1)

                key_side(0)
                for k in range(NK + 2):
                    if k >= 2:
                        turn_probs(k - 2)
                    if k < NK:
                        scores(k)
                    if 1 <= k < NK + 1:
                        values(k - 1)
                    if k % HQ == HQ - 1 and k < NK - 1:
                        key_side(k // HQ + 1)
                    if k >= 2:
                        weighted(k - 2)
                pe.wait_ge(xh4_ready.sem, xh4_ready.at(g))
                turn(xg, xh4_turned)
                pe.wait_ge(xh4T_ready.sem, xh4T_ready.at(g))

                def inner(c):
                    if c == 0:
                        pe.wait_ge(ul_ready.sem, ul_ready.at(g))
                    elif c == 1:
                        pe.wait_ge(v_ready.sem, v_ready.at(g))
                    else:
                        pe.wait_ge(fh_ready.sem, fh_ready.at(g, c - 1))
                    pe.matmul(UP[c % 2][:, :], f_in[:, P * c:P * c + P], xh4T, start=True,
                              stop=True).then_inc(fu_done.sem, 1)

                def outer(c):
                    pe.wait_ge(fh_ready.sem, fh_ready.at(g, c + 1))
                    for b in range(G):
                        last = pe.matmul(YB[0][:, P * b:P * b + P], fh[:, c % 2, P * b:P * b + P], f_out[:, c, :],
                                         start=(c == 0 and b == 0), stop=(c == MI - 1), skip_group_check=True)
                    last.then_inc(fd_done.sem, 1)

                for c in range(MI + 1):
                    if c < MI:
                        inner(c)
                    if c >= 1:
                        outer(c - 1)

            def body(g, more):
                experts(g)
                if more:
                    front(g.shift(1))
                attention(g)

            def prologue():
                setup()
                front(Group(0))

            run(body, prologue, pe)


_INS = ['x', 'ctx_1024', 'L0_xattn_Wi_w', 'L0_xattn_Wi_b', 'L0_xattn_Wf_w', 'L0_xattn_Wf_b', 'L0_xattn_gn_w',
        'L0_xattn_gn_b', 'L0_ffn_gate_w', 'L0_ffn_w1', 'L0_ffn_w2', 'L1_xattn_w_q', 'L1_xattn_w_k',
        'L1_xattn_w_v', 'L1_xattn_w_o', 'L1_ffn_Win', 'L1_ffn_bin_', 'L1_ffn_W1', 'L1_ffn_b1', 'L1_ffn_W2',
        'L1_ffn_b2', 'L1_ffn_Wout', 'L1_ffn_bout']


def kernel(**inputs):
    import numpy as _np
    import concourse.bacc as _bacc
    from concourse import mybir as _mybir
    from concourse.bass_utils import run_bass_kernel_spmd as _run

    nc = _bacc.Bacc("TRN2", target_bir_lowering=False, num_devices=1, dynamic_dma_scratch_size=256)
    arrays, args = {}, []
    for name in _INS:
        a = _np.ascontiguousarray(inputs[name])
        arrays[f"in_{name}_dram"] = a
        args.append(nc.dram_tensor(f"in_{name}_dram", a.shape, _mybir.dt.from_np(a.dtype), kind="ExternalInput").ap())
    shape = arrays["in_x_dram"].shape
    args.append(nc.dram_tensor("out_0_dram", shape, _mybir.dt.float32, kind="ExternalOutput").ap())
    build(nc, *args)
    r = _run(nc, [arrays], core_ids=[0])
    return r.results[0]["out_0_dram"]
```

```python
from contextlib import ExitStack

import concourse.bass as bass
from concourse import mybir

F32 = mybir.dt.float32
F32R = mybir.dt.float32r
BF16 = mybir.dt.bfloat16
U32 = mybir.dt.uint32
ALU = mybir.AluOpType
ACT = mybir.ActivationFunctionType
AX = mybir.AxisListType.X

P = 128
G = 4
T = G * P
H0, D0 = 8, 16
E0, F0 = 8, 512
FC = F0 // P
NU = E0 * FC
H1, D1 = 16, 64
HQ = 4
NK = (H1 // HQ) * G
MI = 8
ROW2 = 32
BIG = 1e30
UNIT_AT = [16, 18, 20, 22, 24, 26]
LAG = 3
HS_AT = {21: 0, 25: 1}
MLP_AT = 5
EPS = 1e-5


class Group:

    def __init__(self, base, off=0):
        self.base, self.off = base, off

    def count(self, per, n):
        return self.base * per + (self.off * per + n)

    def known(self):
        return isinstance(self.base, int)

    def shift(self, d):
        return Group(self.base, self.off + d)


class Signal:

    def __init__(self, sem, per):
        self.sem, self.per = sem, per

    def at(self, g, n=None):
        v = g.count(self.per, self.per if n is None else n)
        return max(v, 0) if isinstance(v, int) else v


class Chain:

    def __init__(self, signal, eng):
        self.s, self.eng = signal, eng

    def begin(self, g):
        self.g, self.n = g, 0

    def link(self, ins):
        self.n += 1
        ins.then_inc(self.s.sem, 1)
        self.eng.wait_ge(self.s.sem, self.s.at(self.g, self.n))

    def end(self):
        assert self.n == self.s.per, (self.n, self.s.per)


def build(nc, x, ctx_in, Wi_w, Wi_b, Wf_w, Wf_b, gn_w, gn_b, gate_w, w1, w2, w_q, w_k, w_v, w_o,
          Win, bin_, W1, b1, W2, b2, Wout, bout, out):
    NG = x.shape[0] // G
    x_g = x.rearrange("(g b) s d -> g s b d", b=G)
    c_g = ctx_in.rearrange("(g b) s d -> g s b d", b=G)
    out_g = out.rearrange("(g b) s d -> g s b d", b=G)

    with ExitStack() as es:
        def sb(name, shape, dt=F32):
            return es.enter_context(nc.sbuf_tensor(name, shape, dt))

        def sig(name, per):
            return Signal(es.enter_context(nc.semaphore(name)), per)

        bank = [es.enter_context(nc.psum_tensor(f"bank{i}", [P, T], F32)) for i in range(8)]
        UP = bank[0:3]
        YB = bank[3:5]
        TB = bank[5]
        XB = bank[6]
        HB = bank[7]
        PTB = [XB, UP[2]]

        ident = sb("ident", [P, P])
        ident_bf = sb("ident_bf", [P, P], BF16)
        causal = sb("causal", [P, P], BF16)
        sel = sb("sel", [ROW2 * 2, 8, P], F32R)
        headmask = sb("headmask", [P, H0])
        expert_no = sb("expert_no", [P, G, E0])
        neg_half, eps_col = sb("neg_half", [P, 32]), sb("eps_col", [P, 32])
        spare = sb("spare", [1, 1])
        keep = sb("keep", [H0, T])
        drop = sb("drop", [H0, T])
        wg = sb("wg", [ROW2 * 2, 3 * P])
        wgx = sb("wgx", [P, ROW2 * 2])
        wgc = sb("wgc", [P, ROW2 * 2])
        gbias = sb("gbias", [ROW2 * 2, 1])
        gnw = sb("gnw", [P, P])
        gnb = sb("gnb", [P, P])
        wgate = sb("wgate", [P, E0])
        w1h, w1l = sb("w1h", [P, E0, F0], F32R), sb("w1l", [P, E0, F0], F32R)
        w2h, w2l = sb("w2h", [P, NU, P], F32R), sb("w2l", [P, NU, P], F32R)
        wqk_h, wqk_l = sb("wqk_h", [P, H1, P], F32R), sb("wqk_l", [P, H1, P], F32R)
        wvo_h, wvo_l = sb("wvo_h", [P, H1, P], F32R), sb("wvo_l", [P, H1, P], F32R)
        f_in = sb("f_in", [P, MI * P])
        f_bias = sb("f_bias", [P, MI])
        f_out = sb("f_out", [P, MI, P])
        f_last = sb("f_last", [P, P])
        x0, c0 = sb("x0", [P, G, P]), sb("c0", [P, G, P])
        xh = sb("xh", [P, G, P])
        xhT, cT = sb("xhT", [P, G, P]), sb("cT", [P, G, P])
        caug = sb("caug", [P, G, H0, D0 + 1])
        irow, frow = sb("irow", [H0, T]), sb("frow", [H0, T])
        trow = sb("trow", [H0, T])
        acat = sb("acat", [P, T])
        mhl = sb("mhl", [ROW2 * 2, G, P], F32R)
        acol, emd = sb("acol", [P, G, H0]), sb("emd", [P, G, H0])
        work = sb("work", [P, 5632])
        qm = work[:, 0:2048].rearrange("p (n h i) -> p n h i", n=2, h=H0)
        ex = work[:, 2048:3072].rearrange("p (n h i) -> p n h i", n=2, h=4)
        pr = work[:, 3072:4608].rearrange("p (n h i) -> p n h i", n=3, h=HQ)
        pts = work[:, 4608:5632].rearrange("p (n h i) -> p n h i", n=2, h=HQ)
        hs = sb("hs", [P, G * H0, D0 + 1])
        hn = sb("hn", [P, G * H0, D0])
        hq = work[:, 2048:2560].rearrange("p (r d) -> p r d", d=D0)
        sm = sb("sm", [P, 8, 32])
        stats = sm[:, 6:8, :].rearrange("p a r -> p (a r)")[:, 0:6 * G].rearrange("p (b s) -> p b s", s=6)
        mv = [sb(f"mv{i}", [P, G, 2]) for i in range(4)]
        rstd = [sb(f"rstd{i}", [P, 32 if i == 4 else G]) for i in range(5)]
        x1, x2, x3 = sb("x1", [P, G, P]), sb("x2", [P, G, P]), sb("x3", [P, G, P])
        xh2T = sb("xh2T", [P, G, P])
        x2h, x2l = sb("x2h", [P, T], F32R), sb("x2l", [P, T], F32R)
        logit = sb("logit", [P, G, E0])
        top = sb("top", [P, G, 8])
        topi = sb("topi", [P, G, 8], U32)
        topf = sb("topf", [P, G, 2])
        pe12 = sb("pe12", [P, 4, G])
        comb = sb("comb", [P, 3, G, E0])
        chl = sb("chl", [ROW2 * 2, T], F32R)
        cb = sb("cb", [P, 2, T])
        yacc = sb("yacc", [P, G, P])
        ytmp = sb("ytmp", [P, 2, T])
        uh = sb("uh", [P, HQ, T], F32R)
        ul = sb("ul", [P, HQ, T], F32R)
        cA = sb("cA", [P, G, P])
        cTh, cTl = sb("cTh", [P, G, P], F32R), sb("cTl", [P, G, P], F32R)
        xg = sb("xg", [P, G, P])
        x3h, x3l = sb("x3h", [P, G, P], F32R), sb("x3l", [P, G, P], F32R)
        vv = cb[:, :, :].rearrange("p n (h d) -> p n h d", h=HQ)
        pm = sb("pm", [P, 3, 3, HQ])
        xh4T = work[:, 3072:3584]
        fh = work[:, 4608:5632].rearrange("p (n t) -> p n t", n=2)
        res = sb("res", [P, G, P])
        x3b = res

        set_dma = es.enter_context(nc.semaphore("set_dma"))
        set_pool = es.enter_context(nc.semaphore("set_pool"))
        stage_in = [es.enter_context(nc.semaphore(f"stage_in{i}")) for i in range(2)]
        stage_hi = es.enter_context(nc.semaphore("stage_hi"))
        stage_lo = es.enter_context(nc.semaphore("stage_lo"))
        proj_in = es.enter_context(nc.semaphore("proj_in"))
        fold_in = es.enter_context(nc.semaphore("fold_in"))
        set_pe = es.enter_context(nc.semaphore("set_pe"))
        set_act = es.enter_context(nc.semaphore("set_act"))
        set_dve = es.enter_context(nc.semaphore("set_dve"))
        ffn_in = es.enter_context(nc.semaphore("ffn_in"))
        ffn_fold = es.enter_context(nc.semaphore("ffn_fold"))
        ffn_pe = es.enter_context(nc.semaphore("ffn_pe"))
        zeroed = es.enter_context(nc.semaphore("zeroed"))

        x_in, c_in, ca_in = sig("x_in", 16), sig("c_in", 16), sig("ca_in", 16)
        stored = sig("stored", 16)
        ln_var = [sig(f"ln_var{i}", 1) for i in range(5)]
        ln_rstd = [sig(f"ln_rstd{i}", 4 if i == 4 else 1) for i in range(5)]
        dve_ln = [sig(f"dve_ln{i}", 1) for i in range(4)]
        pool_ln = [sig(f"pool_ln{i}", 1) for i in range(5)]
        xh1_ready, xh1_turned, xhT_ready = sig("xh1_ready", 1), sig("xh1_turned", 1), sig("xhT_ready", 1)
        c_turned, cT_ready, caug_ready = sig("c_turned", 1), sig("cT_ready", 1), sig("caug_ready", 1)
        gates_done, gates_read = sig("gates_done", 1), sig("gates_read", 1)
        act_gates, softplus_ready = sig("act_gates", 3), sig("softplus_ready", 1)
        dve_rows = sig("dve_rows", 6)
        acat_ready, acat_turned, acol_ready = sig("acat_ready", 1), sig("acat_turned", 1), sig("acol_ready", 1)
        qm_ready = sig("qm_ready", G)
        d_done, e_added, e_exp = sig("d_done", 2 * G), sig("e_added", 2 * G), sig("e_exp", 2 * G)
        s_done, c_done, h_done = sig("s_done", 2 * G), sig("c_done", 2 * G), sig("h_done", 2 * G)
        hs_ready, dve_gn = sig("hs_ready", G), sig("dve_gn", 9)
        hn_scaled, pool_gn = sig("hn_scaled", 1), sig("pool_gn", 2)
        x1_ready = sig("x1_ready", 1)
        xh2_ready, xh2_turned, xh2T_ready = sig("xh2_ready", 1), sig("xh2_turned", 1), sig("xh2T_ready", 1)
        x2hl_ready, dve_split = sig("x2hl_ready", 1), sig("dve_split", 1)
        logits_done, logits_read = sig("logits_done", 1), sig("logits_read", 1)
        dve_top, top_diff, top_exp = sig("dve_top", 9), sig("top_diff", 1), sig("top_exp", 1)
        comb_ready, comb_turned, chl_ready = sig("comb_ready", 1), sig("comb_turned", 1), sig("chl_ready", 1)
        dve_chl = sig("dve_chl", 1)
        cb_done, cb_ready = sig("cb_done", E0), sig("cb_ready", E0)
        up_done, hh_ready, hl_ready = sig("up_done", NU), sig("hh_ready", NU), sig("hl_ready", NU)
        down_done, ymul = sig("down_done", NU), sig("ymul", E0)
        yadd, y_turned, x2_ready = sig("yadd", E0 - 1), sig("y_turned", 1), sig("x2_ready", 1)
        ca_turned, cth_ready, ctl_ready = sig("ca_turned", 1), sig("cth_ready", 1), sig("ctl_ready", 1)
        xh3_ready, xh3_turned = sig("xh3_ready", 1), sig("xh3_turned", 1)
        x3h_ready, x3l_ready = sig("x3h_ready", 1), sig("x3l_ready", 1)
        u_done, uh_ready, ul_ready = sig("u_done", H1), sig("uh_ready", H1), sig("ul_ready", H1)
        v_done, v_ready = sig("v_done", NK), sig("v_ready", NK)
        a_done, a_max, p_sub, p_exp = sig("a_done", NK), sig("a_max", NK), sig("p_sub", NK), sig("p_exp", NK)
        p_sum, r_ready, p_ready = sig("p_sum", NK), sig("r_ready", NK), sig("p_ready", NK)
        pt_done, pts_ready, pv_done = sig("pt_done", NK), sig("pts_ready", NK), sig("pv_done", NK)
        x3_ready, x3b_ready = sig("x3_ready", 1), sig("x3b_ready", 1)
        xh4_ready, xh4_turned, xh4T_ready = sig("xh4_ready", 1), sig("xh4_turned", 1), sig("xh4T_ready", 1)
        fu_done, fh_ready, fd_done = sig("fu_done", MI), sig("fh_ready", MI), sig("fd_done", MI)
        res_ready = sig("res_ready", 1)

        selw = ytmp[0:ROW2 * 2, :, :].rearrange("p a (h i) -> p (a h) i", i=P)
        w1row = x1[:, :, :].rearrange("p b d -> p (b d)"), x2[:, :, :].rearrange("p b d -> p (b d)")
        yrow = yacc[:, :, :].rearrange("p b d -> p (b d)")
        win_s, wout_s, b2_rep = yrow[:, 0:64], yrow[0:64, 64:192], yrow[0:64, 192:320]
        bout_row, b2_col = yrow[:, 320:448], yrow[0:64, 448:449]
        bin_c, w1_c, b1_c, w2_c = (sm[:, i, 0:MI] for i in range(4))
        wqk_s, wT = work[:, 0:2048], work[:, 2048:4096]
        stage = work[:, 4096:5120].rearrange("p (n f) -> p n f", n=2)

        block = es.enter_context(nc.Block())

        def pick(v, g):
            if g.known():
                return v[g.base + g.off]
            return v[bass.ds(g.base + g.off, 1)].rearrange("o s b d -> (o s) b d")

        def load(sp, signal, dst, src, g):
            sp.dma_start(dst[:, :, :], pick(src, g)).then_inc(signal.sem, 16)

        def store(sp, g):
            sp.dma_start(pick(out_g, g), res[:, :, :]).then_inc(stored.sem, 16)

        def run(body, prologue, epilogue, eng):
            prologue()
            body(Group(0), True, False)
            with eng.Fori(1, NG - 1) as g:
                body(Group(g), True, True)
            body(Group(NG - 1), False, True)
            epilogue(Group(NG - 1))

        @block.sync
        def _(sp):
            n = 0
            sp.wait_ge(zeroed, 2)
            for dst, src in [
                (wg[0:H0, :], Wi_w), (wg[ROW2:ROW2 + H0, :], Wf_w),
                (gbias[0:H0, :], Wi_b.rearrange("(h o) -> h o", o=1)),
                (gbias[ROW2:ROW2 + H0, :], Wf_b.rearrange("(h o) -> h o", o=1)),
                (gnw[:, :], gn_w.partition_broadcast(P)), (gnb[:, :], gn_b.partition_broadcast(P)),
                (wgate[:, :], gate_w),
            ]:
                sp.dma_start(dst, src).then_inc(set_dma, 16)
            load(sp, x_in, x0, x_g, Group(0))
            load(sp, c_in, c0, c_g, Group(0))
            sp.dma_start(wqk_s[:, 0:1024], w_q).then_inc(proj_in, 16)
            sp.dma_start(wqk_s[:, 1024:2048], w_k).then_inc(proj_in, 16)
            sp.wait_ge(set_dve, 4)
            sp.dma_start(wqk_s[:, 0:1024], w_v).then_inc(proj_in, 16)
            sp.dma_start(wqk_s[:, 1024:2048].rearrange("p (c d) -> p c d", c=8),
                         w_o.rearrange("(c p) d -> p c d", p=P)).then_inc(proj_in, 16)

            for e in range(2 * E0):
                if e >= 2:
                    sp.wait_ge(stage_lo, e - 1)
                src = (w1[e // 2] if e % 2 == 0 else
                       w2[e // 2].rearrange("(c p) d -> p c d", p=P))
                dst = stage[:, e % 2, :]
                if e % 2:
                    dst = dst.rearrange("p (c d) -> p c d", c=FC)
                sp.dma_start(dst, src).then_inc(stage_in[e % 2], 16)
            units = lambda w: w.rearrange("(c m) i -> (m i) c", c=MI)
            for dst, src in [
                (w1row[0], W1[0:32].rearrange("m i -> (m i)").partition_broadcast(P)),
                (w1row[1], W1[32:64].rearrange("m i -> (m i)").partition_broadcast(P)), (win_s, Win), (wout_s, Wout),
                (bout_row, bout.partition_broadcast(P)), (b2_col, b2.rearrange("(m o) -> m o", o=1)),
                (w1_c, units(W1)), (b1_c, units(b1)), (w2_c, units(W2)),
            ]:
                sp.dma_start(dst, src, allow_slow_non_contiguous=True).then_inc(ffn_in, 16)
            for m in range(8):
                rows = slice(16 * m, 16 * m + 16)
                sp.dma_start(bin_c[rows, :], bin_.rearrange("(c m) -> m c", c=MI)[m].partition_broadcast(16),
                             allow_slow_non_contiguous=True).then_inc(ffn_in, 16)
                sp.dma_start(f_out[rows, :, :], Wout.rearrange("(c m) d -> m c d", c=MI)[m].partition_broadcast(16),
                             allow_slow_non_contiguous=True).then_inc(ffn_in, 16)

            def finish(g):
                sp.wait_ge(res_ready.sem, res_ready.at(g))
                store(sp, g)

            def body(g, more, prev):
                if more:
                    sp.wait_ge(x1_ready.sem, x1_ready.at(g))
                    load(sp, x_in, x0, x_g, g.shift(1))
                    sp.wait_ge(caug_ready.sem, caug_ready.at(g))
                    sp.wait_ge(c_turned.sem, c_turned.at(g))
                    load(sp, c_in, c0, c_g, g.shift(1))
                sp.wait_ge(ca_turned.sem, ca_turned.at(g.shift(-1)))
                load(sp, ca_in, cA, c_g, g)
                if prev:
                    finish(g.shift(-1))

            run(body, lambda: None, finish, sp)
            sp.wait_ge(stored.sem, stored.at(Group(NG - 1)))

        @block.gpsimd
        def _(pool):
            gp = nc.gpsimd
            gp.memset(gbias[:], 0.0).then_inc(zeroed, 1)
            gp.memset(wg[:], 0.0).then_inc(zeroed, 1)
            gp.memset(acat[:], 0.0)
            gp.memset(ident[:], 0.0)
            gp.memset(mhl[:].bitcast(F32), 0.0)
            gp.memset(chl[:].bitcast(F32), 0.0)
            gp.memset(caug[:], 1.0)
            gp.memset(causal[:], 0.0)
            gp.memset(headmask[:], D0 ** -0.5)
            gp.memset(neg_half[:], -0.5)
            gp.memset(eps_col[:], EPS)
            gp.memset(keep[:], 1.0)
            gp.memset(selw, 0.0)
            gp.memset(drop[:], 0.0).then_inc(set_pool, 1)
            pool.wait_ge(set_pool, 1)
            gp.affine_select(out=ident[:], in_=ident[:], compare_op=ALU.not_equal, fill=1.0, base=0,
                             pattern=[[-1, P]], channel_multiplier=1)
            gp.affine_select(out=causal[:], in_=causal[:], compare_op=ALU.is_ge, fill=-BIG, base=0,
                             pattern=[[1, P]], channel_multiplier=-1)
            gp.affine_select(out=headmask[:], in_=headmask[:], compare_op=ALU.is_ge, fill=0.0, base=0,
                             pattern=[[-D0, H0]], channel_multiplier=1)
            gp.affine_select(out=selw, in_=selw, compare_op=ALU.not_equal, fill=1.0, base=0,
                             pattern=[[-1, 8], [0, P]], channel_multiplier=1)
            gp.affine_select(out=keep[:], in_=keep[:], compare_op=ALU.not_equal, fill=0.0, base=0,
                             pattern=[[0, G], [1, P]], channel_multiplier=0)
            gp.affine_select(out=drop[:], in_=drop[:], compare_op=ALU.not_equal, fill=-3e38, base=0,
                             pattern=[[0, G], [1, P]], channel_multiplier=0)
            gp.iota(expert_no[:], pattern=[[0, G], [1, E0]], base=0, channel_multiplier=0,
                    allow_small_or_imprecise_dtypes=True).then_inc(set_pool, 1)
            pool.wait_ge(set_pool, 2)
            gp.affine_select(out=headmask[:], in_=headmask[:], compare_op=ALU.is_ge, fill=0.0,
                             base=D0 - 1, pattern=[[D0, H0]], channel_multiplier=-1)
            gp.affine_select(out=selw, in_=selw, compare_op=ALU.not_equal, fill=1.0, base=-ROW2,
                             pattern=[[-1, 8], [0, P]], channel_multiplier=1).then_inc(set_pool, 1)

            def rsqrt(i, g, var):
                n = var.shape[-1]
                r = rstd[i][:, 0:n]
                pool.wait_ge(ln_var[i].sem, ln_var[i].at(g))
                gp.tensor_tensor(r, var, eps_col[:, 0:n], ALU.add).then_inc(pool_ln[i].sem, 1)
                pool.wait_ge(pool_ln[i].sem, pool_ln[i].at(g))
                gp.tensor_tensor(r, r, neg_half[:, 0:n], ALU.pow).then_inc(ln_rstd[i].sem, 1)

            def masked_queries(g, b):
                if b == 0:
                    pool.wait_ge(xhT_ready.sem, xhT_ready.at(g))
                if b >= 2:
                    pool.wait_ge(s_done.sem, s_done.at(g, 2 * (b - 2) + 2))
                else:
                    pool.wait_ge(s_done.sem, s_done.at(g.shift(-1)))
                gp.tensor_tensor(qm[:, b % 2], xhT[:, b, :].unsqueeze(1).to_broadcast([P, H0, P]),
                                 headmask[:, :].unsqueeze(2).to_broadcast([P, H0, P]),
                                 ALU.mult).then_inc(qm_ready.sem, 1)

            def head_rstd(g, part):
                if part == 0:
                    pool.wait_ge(ln_var[4].sem, ln_var[4].at(g))
                    gp.tensor_tensor(rstd[4][:], sm[:, 5, :], eps_col[:], ALU.add).then_inc(pool_ln[4].sem, 1)
                    pool.wait_ge(pool_ln[4].sem, pool_ln[4].at(g))
                r = rstd[4][:, 8 * part:8 * part + 8]
                gp.tensor_tensor(r, r, neg_half[:, 0:8], ALU.pow).then_inc(ln_rstd[4].sem, 1)

            hb = hn[:].rearrange("p (b h) d -> p b (h d)", b=G)
            row = lambda t: t[:, :].unsqueeze(1).to_broadcast([P, G, P])

            def affine(g):
                pool.wait_ge(hn_scaled.sem, hn_scaled.at(g))
                gp.tensor_tensor(hb, hb, row(gnw), ALU.mult).then_inc(pool_gn.sem, 1)
                pool.wait_ge(pool_gn.sem, pool_gn.at(g, 1))
                gp.tensor_tensor(hb, hb, row(gnb), ALU.add).then_inc(pool_gn.sem, 1)

            def residual0(g):
                pool.wait_ge(pool_gn.sem, pool_gn.at(g, 2))
                pool.wait_ge(x2_ready.sem, x2_ready.at(g.shift(-1)))
                gp.tensor_tensor(x1[:], hb, x0[:], ALU.add).then_inc(x1_ready.sem, 1)

            def expert_sum(g, e):
                pool.wait_ge(ymul.sem, ymul.at(g, e + 1))
                if e >= 2:
                    pool.wait_ge(yadd.sem, yadd.at(g, e - 1))
                gp.tensor_tensor(yacc[:, :, :].rearrange("p b d -> p (b d)"),
                                 yacc[:, :, :].rearrange("p b d -> p (b d)"), ytmp[:, e % 2, :],
                                 ALU.add).then_inc(yadd.sem, 1)

            def experts(g, more):
                n = g.shift(1)
                if more:
                    rsqrt(0, n, mv[0][:, :, 1])
                    masked_queries(n, 0)
                expert_sum(g, 1)
                if more:
                    masked_queries(n, 1)
                for e in range(2, E0):
                    expert_sum(g, e)
                    if more and e in (3, 4):
                        masked_queries(n, e - 1)

            def attention(g, more):
                n = g.shift(1)
                rsqrt(2, g, mv[2][:, :, 1])
                for k in range(NK):
                    pool.wait_ge(r_ready.sem, r_ready.at(g, k + 1))
                    gp.tensor_tensor(pr[:, k % 3], pr[:, k % 3],
                                     pm[:, k % 3, 2, :].unsqueeze(2).to_broadcast([P, HQ, P]),
                                     ALU.mult).then_inc(p_ready.sem, 1)
                    if more:
                        if k in (4, 5):
                            head_rstd(n, 2 * (k - 4))
                            head_rstd(n, 2 * (k - 4) + 1)
                        elif k == 6:
                            affine(n)
                        elif k == 7:
                            residual0(n)
                        elif k == 8:
                            rsqrt(1, n, mv[1][:, :, 1])
                rsqrt(3, g, mv[3][:, :, 1])
                pool.wait_ge(x3_ready.sem, x3_ready.at(g))
                pool.wait_ge(stored.sem, stored.at(g.shift(-1)))
                gp.tensor_tensor(x3b[:], x3[:], f_last[:, :].unsqueeze(1).to_broadcast([P, G, P]),
                                 ALU.add).then_inc(x3b_ready.sem, 1)

            def body(g, more, prev):
                experts(g, more)
                attention(g, more)

            def prologue():
                g = Group(0)
                rsqrt(0, g, mv[0][:, :, 1])
                for b in range(G):
                    masked_queries(g, b)
                for part in range(4):
                    head_rstd(g, part)
                affine(g)
                residual0(g)
                rsqrt(1, g, mv[1][:, :, 1])

            run(body, prologue, lambda g: None, pool)

        @block.scalar
        def _(act):
            sc = nc.scalar
            act.preload_act_table_set("natural_log_exp_and_others")

            def setup():
                act.wait_ge(set_pe, 1)
                sc.activation(wgx[:], TB[:, 0:64], ACT.Copy)
                sc.activation(wgc[:], TB[:, 64:128], ACT.Copy).then_inc(set_act, 1)
                n_pe, n_act = 1, 1
                for w in range(3):
                    for half in range(2):
                        n_pe += 1
                        act.wait_ge(set_pe, n_pe)
                        dst = wT[:, 1024 * (w % 2) + 512 * half:1024 * (w % 2) + 512 * half + 512]
                        sc.activation(dst, UP[half][:, :], ACT.Copy).then_inc(set_act, 1)
                    if w == 0:
                        continue
                    hi = wqk_h if w == 1 else wvo_h
                    scale = D1 ** -0.5 if w == 1 else 1.0
                    for q in range(4):
                        n_pe += 1
                        act.wait_ge(set_pe, n_pe)
                        dst = hi[:, :, :].rearrange("p (i two) d -> p two i d", two=2)[:, q % 2, 4 * (q // 2):4 * (q // 2) + 4]
                        sc.activation(dst, YB[q % 2][:, :].rearrange("p (i d) -> p i d", i=4),
                                      ACT.Copy, scale=scale).then_inc(set_act, 1)
                for e in range(2 * E0):
                    act.wait_ge(stage_in[e % 2], 16 * (e // 2 + 1))
                    hi = w1h[:, e // 2, :] if e % 2 == 0 else w2h[:, FC * (e // 2):FC * (e // 2) + FC, :].rearrange("p c d -> p (c d)")
                    sc.activation(hi, stage[:, e % 2, :], ACT.Copy).then_inc(stage_hi, 1)

            flat = lambda t: t[:].rearrange("p b d -> p (b d)")

            def queries(g):
                act.wait_ge(xh1_turned.sem, xh1_turned.at(g))
                act.wait_ge(s_done.sem, s_done.at(g.shift(-1)))
                sc.activation(flat(xhT), TB[:, :], ACT.Copy).then_inc(xhT_ready.sem, 1)

            def contexts(g):
                act.wait_ge(c_turned.sem, c_turned.at(g))
                act.wait_ge(h_done.sem, h_done.at(g.shift(-1)))
                sc.activation(flat(cT), TB[:, :], ACT.Copy).then_inc(cT_ready.sem, 1)
                sc.activation(caug[:, :, :, 0:D0], c0[:, :, :].rearrange("p b (h d) -> p b h d", h=H0),
                              ACT.Copy).then_inc(caug_ready.sem, 1)

            def gates(g):
                act.wait_ge(gates_done.sem, gates_done.at(g))
                act.wait_ge(dve_rows.sem, dve_rows.at(g.shift(-1)))
                sc.activation(frow[:], TB[ROW2:ROW2 + H0, :], ACT.Identity,
                              bias=gbias[ROW2:ROW2 + H0, :]).then_inc(act_gates.sem, 1)
                sc.activation(irow[:], TB[0:H0, :], ACT.Identity, bias=gbias[0:H0, :]).then_inc(gates_read.sem, 1)

            def softplus(g):
                act.wait_ge(act_gates.sem, act_gates.at(g, 1))
                sc.activation(trow[:], frow[:], ACT.Abs).then_inc(act_gates.sem, 1)
                act.wait_ge(act_gates.sem, act_gates.at(g, 2))
                sc.activation(trow[:], trow[:], ACT.Exp, scale=-1.0).then_inc(act_gates.sem, 1)
                act.wait_ge(act_gates.sem, act_gates.at(g, 3))
                sc.activation(trow[:], trow[:], ACT.Ln, bias=1.0).then_inc(softplus_ready.sem, 1)

            def columns(g):
                act.wait_ge(acat_turned.sem, acat_turned.at(g))
                act.wait_ge(x1_ready.sem, x1_ready.at(g.shift(-1)))
                tb = TB[:, :].rearrange("p (b r) -> p b r", b=G)
                sc.activation(acol[:], tb[:, :, 0:H0], ACT.Copy)
                sc.activation(emd[:], tb[:, :, ROW2:ROW2 + H0], ACT.Exp, scale=-1.0).then_inc(acol_ready.sem, 1)

            def decayed(g, k):
                act.wait_ge(e_added.sem, e_added.at(g, k + 1))
                sc.activation(ex[:, k % 2], ex[:, k % 2], ACT.Exp).then_inc(e_exp.sem, 1)

            def head_outputs(g, b):
                act.wait_ge(h_done.sem, h_done.at(g, 2 * b + 2))
                sc.activation(hs[:, H0 * b:H0 * b + H0, :].rearrange("p h d -> p (h d)"),
                              HB[:, 0:H0 * (D0 + 1)], ACT.Copy).then_inc(hs_ready.sem, 1)

            def tokens2(g):
                act.wait_ge(xh2_turned.sem, xh2_turned.at(g))
                sc.activation(flat(xh2T), TB[:, :], ACT.Copy).then_inc(xh2T_ready.sem, 1)

            def logits(g):
                act.wait_ge(logits_done.sem, logits_done.at(g))
                sc.activation(logit[:].rearrange("p b e -> p (b e)"), TB[:, 0:G * E0], ACT.Copy).then_inc(logits_read.sem, 1)

            def top_weight(g):
                act.wait_ge(top_diff.sem, top_diff.at(g))
                sc.activation(pe12[:, 1, :], pe12[:, 0, :], ACT.Exp).then_inc(top_exp.sem, 1)

            def tokens4(g):
                act.wait_ge(xh4_turned.sem, xh4_turned.at(g))
                sc.activation(xh4T, TB[:, :], ACT.Copy).then_inc(xh4T_ready.sem, 1)

            def mlp_inner(g, c):
                act.wait_ge(fu_done.sem, fu_done.at(g, c + 1))
                if c >= 2:
                    act.wait_ge(fd_done.sem, fd_done.at(g, c - 1))
                sc.activation(fh[:, c % 2, :], XB[:, :], ACT.Relu,
                              bias=f_bias[:, c:c + 1]).then_inc(fh_ready.sem, 1)

            def experts(g, more, prev):
                n, p = g.shift(1), g.shift(-1)
                for u in range(NU):
                    e = u // FC
                    if u % FC == 0:
                        act.wait_ge(cb_done.sem, cb_done.at(g, e + 1))
                        if e >= 2:
                            act.wait_ge(ymul.sem, ymul.at(g, e - 1))
                        else:
                            act.wait_ge(ymul.sem, ymul.at(g.shift(-1)))
                        sc.activation(cb[:, e % 2, :], TB[:, :], ACT.Copy).then_inc(cb_ready.sem, 1)
                    act.wait_ge(up_done.sem, up_done.at(g, u + 1))
                    if u >= 4:
                        act.wait_ge(down_done.sem, down_done.at(g, u - 3))
                    sc.activation(uh[:, u % 4, :], UP[u % 3][:, :], ACT.Relu).then_inc(hh_ready.sem, 1)
                    if prev:
                        if u == 3:
                            tokens4(p)
                        if MLP_AT <= u < MLP_AT + MI:
                            mlp_inner(p, u - MLP_AT)
                    if more:
                        if u == 6:
                            queries(n)
                        elif u == 7:
                            contexts(n)
                        elif u == 9:
                            gates(n)
                        elif u == 10:
                            softplus(n)
                        elif u == 15:
                            columns(n)
                        if u - 1 in UNIT_AT:
                            decayed(n, UNIT_AT.index(u - 1))
                        if u in HS_AT:
                            head_outputs(n, HS_AT[u])
                    if u == 30:
                        act.wait_ge(ca_turned.sem, ca_turned.at(g))
                        sc.activation(flat(cTh), TB[:, :], ACT.Copy).then_inc(cth_ready.sem, 1)

            def attention(g, more):
                n = g.shift(1)

                def key_side(h):
                    act.wait_ge(u_done.sem, u_done.at(g, h + 1))
                    sc.activation(uh[:, h % HQ, :], UP[(h + 1) % 2][:, :], ACT.Copy).then_inc(uh_ready.sem, 1)

                def turned(k):
                    act.wait_ge(pt_done.sem, pt_done.at(g, k + 1))
                    if k >= 2:
                        act.wait_ge(pv_done.sem, pv_done.at(g, k - 1))
                    sc.activation(pts[:, k % 2].rearrange("p h i -> p (h i)"), PTB[k % 2][:, :],
                                  ACT.Copy).then_inc(pts_ready.sem, 1)

                def values(k):
                    act.wait_ge(v_done.sem, v_done.at(g, k + 1))
                    if k >= 2:
                        act.wait_ge(pv_done.sem, pv_done.at(g, k - 1))
                    sc.activation(vv[:, k % 2].rearrange("p h i -> p (h i)"), UP[1][:, :],
                                  ACT.Copy).then_inc(v_ready.sem, 1)

                for h in range(HQ):
                    key_side(h)
                if more:
                    head_outputs(n, 2)
                values(0)
                if more:
                    decayed(n, 6)
                values(1)
                act.wait_ge(xh3_turned.sem, xh3_turned.at(g))
                sc.activation(flat(x3h), TB[:, :], ACT.Copy).then_inc(x3h_ready.sem, 1)
                if more:
                    decayed(n, 7)
                for k in range(NK + LAG):
                    next_q = k % HQ == HQ - 1 and k < NK - 1
                    if next_q:
                        key_side(k + 1)
                    if k >= LAG:
                        turned(k - LAG)
                    if k < NK:
                        act.wait_ge(p_sub.sem, p_sub.at(g, k + 1))
                        sc.activation(pr[:, k % 3], pr[:, k % 3], ACT.Exp).then_inc(p_exp.sem, 1)
                    if next_q:
                        for h in range(k + 2, k + 1 + HQ):
                            key_side(h)
                    if 2 <= k - 1 < NK:
                        values(k - 1)
                    if more:
                        if k == 1:
                            head_outputs(n, 3)
                        elif k == 11:
                            tokens2(n)
                        elif k == 12:
                            logits(n)
                        elif k == 13:
                            top_weight(n)

            def body(g, more, prev):
                experts(g, more, prev)
                attention(g, more)

            def prologue():
                setup()
                g = Group(0)
                queries(g)
                contexts(g)
                gates(g)
                softplus(g)
                columns(g)
                for k in range(2 * G + 1):
                    if k < 2 * G:
                        decayed(g, k)
                    if k >= 2 and k % 2 == 0:
                        head_outputs(g, k // 2 - 1)
                tokens2(g)
                logits(g)
                top_weight(g)

            def epilogue(g):
                tokens4(g)
                for c in range(MI):
                    mlp_inner(g, c)

            run(body, prologue, epilogue, act)

        @block.vector
        def _(dve):
            v = nc.vector
            ln_chain = [Chain(s, dve) for s in dve_ln]
            rows, gn, tp = Chain(dve_rows, dve), Chain(dve_gn, dve), Chain(dve_top, dve)

            def setup():
                dve.wait_ge(set_pool, 3)
                v.tensor_copy(sel[:], selw)
                v.tensor_copy(ident_bf[:], ident[:]).then_inc(fold_in, 1)
                dve.wait_ge(set_dma, 16 * 7)
                v.tensor_tensor(wg[:, P:2 * P], wg[:, P:2 * P], wg[:, 2 * P:3 * P], ALU.add).then_inc(fold_in, 1)
                n_act = 1
                for w in range(3):
                    n_act += 2
                    if w == 0:
                        continue
                    hi, lo = (wqk_h, wqk_l) if w == 1 else (wvo_h, wvo_l)
                    scale = D1 ** -0.5 if w == 1 else 1.0
                    for q in range(4):
                        n_act += 1
                        dve.wait_ge(set_act, n_act)
                        view = lambda t: t[:, :, :].rearrange("p (i two) d -> p two i d", two=2)[:, q % 2, 4 * (q // 2):4 * (q // 2) + 4]
                        v.scalar_tensor_tensor(view(lo), YB[q % 2][:, :].rearrange("p (i d) -> p i d", i=4), scale,
                                               view(hi), ALU.mult, ALU.subtract).then_inc(set_dve, 1)
                for e in range(2 * E0):
                    dve.wait_ge(stage_hi, e + 1)
                    if e % 2 == 0:
                        hi, lo = w1h[:, e // 2, :], w1l[:, e // 2, :]
                    else:
                        hi, lo = (t[:, FC * (e // 2):FC * (e // 2) + FC, :].rearrange("p c d -> p (c d)") for t in (w2h, w2l))
                    v.tensor_tensor(lo, stage[:, e % 2, :], hi, ALU.subtract).then_inc(stage_lo, 1)
                dve.wait_ge(ffn_in, 16 * 25)
                v.tensor_copy(b2_rep, b2_col.to_broadcast([64, P])).then_inc(ffn_fold, 1)
                v.tensor_tensor(bin_c, bin_c, w1_c, ALU.mult).then_inc(ffn_fold, 1)
                for n in range(2):
                    v.tensor_tensor(f_in[:, 512 * n:512 * n + 512].rearrange("p (m i) -> p m i", i=16),
                                    win_s[:, 32 * n:32 * n + 32].unsqueeze(2).to_broadcast([P, 32, 16]),
                                    w1row[n].rearrange("p (m i) -> p m i", i=16), ALU.mult)
                v.tensor_tensor(f_out[:], f_out[:], w2_c.unsqueeze(2).to_broadcast([P, MI, P]), ALU.mult)
                dve.wait_ge(ffn_fold, 2)
                v.tensor_tensor(f_bias[:], bin_c, b1_c, ALU.add)
                dve.wait_ge(ffn_pe, 1)
                v.tensor_tensor(f_last[:], TB[:, 0:P], bout_row, ALU.add).then_inc(ffn_fold, 1)

            flat = lambda t: t[:].rearrange("p b d -> p (b d)")

            def moments(i, g, src):
                ch = ln_chain[i]
                ch.begin(g)
                for b in range(G):
                    last = v.bn_stats(stats[:, b, :], src[:, b, :])
                ch.link(last)
                v.memset(spare[:, :], 0.0)
                for b in range(G):
                    last = v.bn_aggr(mv[i][:, b, :], stats[:, b, :])
                last.then_inc(ln_var[i].sem, 1)

            def normalise(i, g, src, dst, ready):
                dve.wait_ge(ln_rstd[i].sem, ln_rstd[i].at(g))
                for b in range(G):
                    last = v.tensor_scalar(dst[:, b, :], src[:, b, :], mv[i][:, b, 0:1],
                                           rstd[i][:, b:b + 1], ALU.subtract, ALU.mult)
                last.then_inc(ready.sem, 1)

            def moments0(g):
                dve.wait_ge(x_in.sem, x_in.at(g))
                moments(0, g, x0)

            def normalise0(g):
                dve.wait_ge(xh2_turned.sem, xh2_turned.at(g.shift(-1)))
                normalise(0, g, x0, xh, xh1_ready)

            def gate_rows(g, part):
                if part == 0:
                    dve.wait_ge(softplus_ready.sem, softplus_ready.at(g))
                    dve.wait_ge(gates_read.sem, gates_read.at(g))
                    rows.begin(g)
                    rows.link(v.scalar_tensor_tensor(trow[:], frow[:], 0.0, trow[:], ALU.min, ALU.subtract))
                    rows.link(v.tensor_tensor_scan(frow[:], keep[:], trow[:], 0.0, ALU.mult, ALU.add))
                elif part == 1:
                    rows.link(v.tensor_tensor(acat[0:H0, :], irow[:], frow[:], ALU.subtract))
                    rows.link(v.tensor_tensor_scan(trow[:], drop[:], acat[0:H0, :], 0.0, ALU.add, ALU.max))
                    v.tensor_tensor(acat[ROW2:ROW2 + H0, :], frow[:], trow[:], ALU.add).then_inc(acat_ready.sem, 1)
                else:
                    dve.wait_ge(d_done.sem, d_done.at(g.shift(-1)))
                    mh = flat(mhl)
                    rows.link(v.tensor_scalar(mh[0:H0, :], trow[:], -1.0, None, ALU.mult))
                    rows.link(v.scalar_tensor_tensor(mh[ROW2:ROW2 + H0, :], trow[:], -1.0, mh[0:H0, :],
                                                     ALU.mult, ALU.subtract))
                    rows.end()

            def decay(g, k):
                b, hf = k // 2, k % 2
                if k == 0:
                    dve.wait_ge(acol_ready.sem, acol_ready.at(g))
                dve.wait_ge(d_done.sem, d_done.at(g, k + 1))
                dve.wait_ge(h_done.sem, h_done.at(g, k - 1))
                v.tensor_tensor(ex[:, k % 2], XB[:, :].rearrange("p (h i) -> p h i", h=4),
                                acol[:, b, 4 * hf:4 * hf + 4].unsqueeze(2).to_broadcast([P, 4, P]),
                                ALU.add).then_inc(e_added.sem, 1)

            def weigh(g, k):
                dve.wait_ge(s_done.sem, s_done.at(g, k + 1))
                dve.wait_ge(e_exp.sem, e_exp.at(g, k + 1))
                v.tensor_tensor(ex[:, k % 2], XB[:, :].rearrange("p (h i) -> p h i", h=4),
                                ex[:, k % 2], ALU.mult).then_inc(c_done.sem, 1)

            def head_norm(g, part):
                R = G * H0
                wide = lambda ap: ap.unsqueeze(2).to_broadcast([P, R, D0])
                if part == 0:
                    dve.wait_ge(hs_ready.sem, hs_ready.at(g))
                    gn.begin(g)
                    gn.link(v.scalar_tensor_tensor(sm[:, 0, :], hs[:, :, D0], -1.0, hs[:, :, D0], ALU.mult, ALU.max))
                    gn.link(v.tensor_tensor(sm[:, 0, :], sm[:, 0, :], emd[:].rearrange("p b h -> p (b h)"), ALU.max))
                    gn.link(v.tensor_scalar(sm[:, 1, :], sm[:, 0, :], 1e-6, None, ALU.add))
                    gn.link(v.reciprocal(sm[:, 2, :], sm[:, 1, :]))
                    gn.link(v.tensor_tensor(hn[:], hs[:, :, 0:D0], wide(sm[:, 2, :]), ALU.mult))
                elif part == 1:
                    gn.link(v.reduce_sum(sm[:, 3, :], hn[:], AX))
                    gn.link(v.scalar_tensor_tensor(hn[:], wide(sm[:, 3, :]), -1.0 / D0, hn[:], ALU.mult, ALU.add))
                elif part == 2:
                    gn.link(v.tensor_tensor(hq[:], hn[:], hn[:], ALU.mult))
                    gn.link(v.reduce_sum(sm[:, 4, :], hq[:], AX))
                    v.tensor_scalar(sm[:, 5, :], sm[:, 4, :], 1.0 / D0, None, ALU.mult).then_inc(ln_var[4].sem, 1)
                    gn.end()
                else:
                    dve.wait_ge(ln_rstd[4].sem, ln_rstd[4].at(g))
                    v.tensor_tensor(hn[:], hn[:], wide(rstd[4][:, :]), ALU.mult).then_inc(hn_scaled.sem, 1)

            def moments1(g):
                dve.wait_ge(x1_ready.sem, x1_ready.at(g))
                moments(1, g, x1)

            def normalise1(g):
                dve.wait_ge(xh1_turned.sem, xh1_turned.at(g))
                normalise(1, g, x1, xh, xh2_ready)

            def split_tokens(g):
                dve.wait_ge(xh2T_ready.sem, xh2T_ready.at(g))
                dve.wait_ge(up_done.sem, up_done.at(g.shift(-1)))
                v.tensor_copy(x2h[:], flat(xh2T)).then_inc(dve_split.sem, 1)
                dve.wait_ge(dve_split.sem, dve_split.at(g))
                v.tensor_tensor(x2l[:], flat(xh2T), x2h[:], ALU.subtract).then_inc(x2hl_ready.sem, 1)

            def choose(g, part):
                wide2 = lambda ap: ap.unsqueeze(2).to_broadcast([P, G, E0])
                if part == 0:
                    dve.wait_ge(logits_read.sem, logits_read.at(g))
                    dve.memset(spare[:, :], 0.0)
                    tp.begin(g)
                    for b in range(G):
                        last = v.max(top[:, b, :], logit[:, b, :])
                    tp.link(last)
                    v.memset(spare[:, :], 0.0)
                    v.tensor_tensor(pe12[:, 0, :], top[:, :, 1], top[:, :, 0], ALU.subtract).then_inc(top_diff.sem, 1)
                    for b in range(G):
                        last = v.max_index(topi[:, b, :], top[:, b, :], logit[:, b, :])
                    tp.link(last)
                    tp.link(v.tensor_copy(topf[:], topi[:, :, 0:2]))
                    v.tensor_tensor(comb[:, 0], expert_no[:], wide2(topf[:, :, 0]), ALU.is_equal)
                    tp.link(v.tensor_tensor(comb[:, 1], expert_no[:], wide2(topf[:, :, 1]), ALU.is_equal))
                else:
                    dve.wait_ge(top_exp.sem, top_exp.at(g))
                    tp.link(v.tensor_scalar(pe12[:, 2, :], pe12[:, 1, :], 1.0, None, ALU.add))
                    tp.link(v.reciprocal(pe12[:, 3, :], pe12[:, 2, :]))
                    tp.link(v.tensor_tensor(pe12[:, 2, :], pe12[:, 1, :], pe12[:, 3, :], ALU.mult))
                    tp.link(v.tensor_tensor(comb[:, 0], comb[:, 0], wide2(pe12[:, 3, :]), ALU.mult))
                    tp.link(v.tensor_tensor(comb[:, 1], comb[:, 1], wide2(pe12[:, 2, :]), ALU.mult))
                    tp.end()
                    dve.wait_ge(comb_turned.sem, comb_turned.at(g.shift(-1)))
                    v.tensor_tensor(comb[:, 2], comb[:, 0], comb[:, 1], ALU.add).then_inc(comb_ready.sem, 1)

            def expert_rows(g):
                dve.wait_ge(comb_turned.sem, comb_turned.at(g))
                dve.wait_ge(cb_done.sem, cb_done.at(g.shift(-1)))
                v.tensor_copy(chl[0:E0, :], TB[0:E0, :]).then_inc(dve_chl.sem, 1)
                dve.wait_ge(dve_chl.sem, dve_chl.at(g))
                v.tensor_tensor(chl[ROW2:ROW2 + E0, :], TB[0:E0, :], chl[0:E0, :],
                                ALU.subtract).then_inc(chl_ready.sem, 1)

            def normalise3(g):
                dve.wait_ge(xh3_turned.sem, xh3_turned.at(g))
                normalise(3, g, x3, xg, xh4_ready)

            def result(g):
                dve.wait_ge(fd_done.sem, fd_done.at(g))
                dve.wait_ge(x3b_ready.sem, x3b_ready.at(g))
                v.tensor_tensor(flat(res), HB[:, :], flat(x3b), ALU.add).then_inc(res_ready.sem, 1)

            def experts(g, more, prev):
                n, p = g.shift(1), g.shift(-1)

                def scale_out(e):
                    dve.wait_ge(down_done.sem, down_done.at(g, FC * e + FC))
                    dve.wait_ge(cb_ready.sem, cb_ready.at(g, e + 1))
                    if e == 0:
                        dve.wait_ge(y_turned.sem, y_turned.at(g.shift(-1)))
                        dst = flat(yacc)
                    else:
                        if e >= 3:
                            dve.wait_ge(yadd.sem, yadd.at(g, e - 2))
                        else:
                            dve.wait_ge(yadd.sem, yadd.at(g.shift(-1)))
                        dst = ytmp[:, e % 2, :]
                    v.tensor_tensor(dst, YB[e % 2][:, :], cb[:, e % 2, :], ALU.mult).then_inc(ymul.sem, 1)

                for u in range(NU):
                    dve.wait_ge(hh_ready.sem, hh_ready.at(g, u + 1))
                    v.scalar_tensor_tensor(ul[:, u % 4, :], UP[u % 3][:, :], 0.0, uh[:, u % 4, :],
                                           ALU.max, ALU.subtract).then_inc(hl_ready.sem, 1)
                    if u % FC == FC - 1 and u > FC:
                        scale_out(u // FC - 1)
                    if prev:
                        if u == 1:
                            normalise3(p)
                        elif u == MLP_AT + MI + 1:
                            result(p)
                    if more:
                        if u == 2:
                            moments0(n)
                        elif u == 4:
                            normalise0(n)
                        elif 11 <= u <= 13:
                            gate_rows(n, u - 11)
                        if u - 1 in UNIT_AT:
                            weigh(n, UNIT_AT.index(u - 1))
                        if u in UNIT_AT:
                            decay(n, UNIT_AT.index(u))
                    if u == 30:
                        dve.wait_ge(cth_ready.sem, cth_ready.at(g))
                        v.tensor_tensor(flat(cTl), TB[:, :], flat(cTh), ALU.subtract).then_inc(ctl_ready.sem, 1)
                scale_out(E0 - 1)

            def attention(g, more):
                n = g.shift(1)

                def key_side(h):
                    dve.wait_ge(uh_ready.sem, uh_ready.at(g, h + 1))
                    v.tensor_tensor(ul[:, h % HQ, :], UP[(h + 1) % 2][:, :], uh[:, h % HQ, :],
                                    ALU.subtract).then_inc(ul_ready.sem, 1)

                def row_max(k):
                    s = YB[k % 2][:, :].rearrange("p (h j) -> p h j", h=HQ)
                    dve.wait_ge(a_done.sem, a_done.at(g, k + 1))
                    v.reduce_max(pm[:, k % 3, 0, :], s, AX).then_inc(a_max.sem, 1)
                    dve.wait_ge(a_max.sem, a_max.at(g, k + 1))
                    if k >= 3:
                        dve.wait_ge(pt_done.sem, pt_done.at(g, k - 2))
                    v.tensor_tensor(pr[:, k % 3], s, pm[:, k % 3, 0, :].unsqueeze(2).to_broadcast([P, HQ, P]),
                                    ALU.subtract).then_inc(p_sub.sem, 1)

                def row_sum(k):
                    dve.wait_ge(p_exp.sem, p_exp.at(g, k + 1))
                    v.reduce_sum(pm[:, k % 3, 1, :], pr[:, k % 3], AX).then_inc(p_sum.sem, 1)
                    dve.wait_ge(p_sum.sem, p_sum.at(g, k + 1))
                    v.reciprocal(pm[:, k % 3, 2, :], pm[:, k % 3, 1, :]).then_inc(r_ready.sem, 1)

                for h in range(HQ):
                    key_side(h)
                dve.wait_ge(y_turned.sem, y_turned.at(g))
                v.tensor_tensor(flat(x2), TB[:, :], flat(x1), ALU.add).then_inc(x2_ready.sem, 1)
                dve.wait_ge(x2_ready.sem, x2_ready.at(g))
                moments(2, g, x2)
                if more:
                    decay(n, 6)
                dve.wait_ge(xh4_turned.sem, xh4_turned.at(g.shift(-1)))
                normalise(2, g, x2, xg, xh3_ready)
                if more:
                    weigh(n, 6)
                dve.wait_ge(x3h_ready.sem, x3h_ready.at(g))
                v.tensor_tensor(flat(x3l), TB[:, :], flat(x3h), ALU.subtract).then_inc(x3l_ready.sem, 1)
                if more:
                    decay(n, 7)
                for k in range(NK + 1):
                    next_q = k % HQ == HQ - 1 and k < NK - 1
                    if k < NK:
                        row_max(k)
                    if next_q:
                        key_side(k + 1)
                    if k >= 1:
                        row_sum(k - 1)
                    if next_q:
                        for h in range(k + 2, k + 1 + HQ):
                            key_side(h)
                    if more:
                        if k == 0:
                            weigh(n, 7)
                        elif 2 <= k <= 4:
                            head_norm(n, k - 2)
                        elif k == 7:
                            head_norm(n, 3)
                        elif k == 9:
                            moments1(n)
                        elif k == 10:
                            normalise1(n)
                        elif k == 12:
                            split_tokens(n)
                        elif k == 13:
                            choose(n, 0)
                        elif k == 14:
                            choose(n, 1)
                        elif k == 16:
                            expert_rows(n)
                dve.wait_ge(pv_done.sem, pv_done.at(g))
                v.tensor_tensor(flat(x3), HB[:, :], flat(x2), ALU.add).then_inc(x3_ready.sem, 1)
                dve.wait_ge(x3_ready.sem, x3_ready.at(g))
                moments(3, g, x3)

            def body(g, more, prev):
                experts(g, more, prev)
                attention(g, more)

            def prologue():
                setup()
                g = Group(0)
                moments0(g)
                normalise0(g)
                for part in range(3):
                    gate_rows(g, part)
                for k in range(2 * G):
                    decay(g, k)
                    weigh(g, k)
                for part in range(4):
                    head_norm(g, part)
                moments1(g)
                normalise1(g)
                split_tokens(g)
                choose(g, 0)
                choose(g, 1)
                expert_rows(g)

            def epilogue(g):
                normalise3(g)
                result(g)

            run(body, prologue, epilogue, dve)

        @block.tensor
        def _(pe):
            def split(o, lh, ll, rh, rl, start, stop):
                pe.matmul(o, lh, rh, start=start, stop=False)
                pe.matmul(o, lh, rl, start=False, stop=False)
                return pe.matmul(o, ll, rh, start=False, stop=stop)

            def turn(src, signal):
                for b in range(G):
                    last = pe.transpose(TB[:, P * b:P * b + P], src[:, b, :], ident[:])
                last.then_inc(signal.sem, 1)

            def setup():
                pe.wait_ge(fold_in, 2)
                pe.transpose(TB[:, 0:64], wg[:, 0:P], ident[0:64, 0:64])
                pe.transpose(TB[:, 64:128], wg[:, P:2 * P], ident[0:64, 0:64]).then_inc(set_pe, 1)
                n_act = 1
                for w in range(3):
                    pe.wait_ge(proj_in, 16 * (2 if w < 2 else 4))
                    for half in range(2):
                        if w:
                            pe.wait_ge(set_act, n_act - 1 + half if w == 1 else n_act)
                        for i in range(4):
                            c = 4 * half + i
                            col = 1024 * (w % 2) + P * c
                            last = pe.transpose(UP[half][:, P * i:P * i + P], wqk_s[:, col:col + P], ident[:])
                        last.then_inc(set_pe, 1)
                    n_act += 2
                    if w == 0:
                        continue
                    pe.wait_ge(set_act, n_act)
                    for q in range(4):
                        if q >= 2 or w == 2:
                            pe.wait_ge(set_dve, 4 * (w - 1) + q - 1)
                        par, lo = q % 2, 4 * (q // 2)
                        rows = slice(64 * par, 64 * par + 64)
                        for i in range(4):
                            c = lo + i
                            if w == 1:
                                lhs = wT[rows, 1024 + P * c:1024 + P * c + P]
                                rhs = wT[rows, P * c:P * c + P]
                            else:
                                lhs = wT[rows, P * c:P * c + P]
                                rhs = wqk_s[rows, 1024 + P * c:1024 + P * c + P]
                            last = pe.matmul(YB[par][:, P * i:P * i + P], lhs, rhs, start=True, stop=True)
                        last.then_inc(set_pe, 1)
                    n_act += 4
                pe.wait_ge(ffn_fold, 1)
                pe.matmul(TB[:, 0:P], b2_rep, wout_s, start=True, stop=True).then_inc(ffn_pe, 1)
                pe.wait_ge(ffn_fold, 3)

            flat = lambda t: t[:].rearrange("p b d -> p (b d)")

            def gates(g):
                pe.wait_ge(cT_ready.sem, cT_ready.at(g))
                pe.matmul(TB[0:64, :], wgx[:], flat(xhT), start=True, stop=False)
                pe.matmul(TB[0:64, :], wgc[:], flat(cT), start=False, stop=True).then_inc(gates_done.sem, 1)

            def turn_rows(g):
                pe.wait_ge(acat_ready.sem, acat_ready.at(g))
                for b in range(G):
                    last = pe.transpose(TB[:, P * b:P * b + P], acat[:, P * b:P * b + P], ident[:])
                last.then_inc(acat_turned.sem, 1)

            def decay(g, k):
                b, hf = k // 2, k % 2
                pe.wait_ge(c_done.sem, c_done.at(g, k))
                if k == 0:
                    pe.wait_ge(dve_rows.sem, dve_rows.at(g))
                pe.matmul(XB[:, :], ident_bf[:], causal[:, :].unsqueeze(1).to_broadcast([P, 4, P]),
                          start=True, stop=True)
                for i in range(4):
                    last = pe.matmul(XB[:, P * i:P * i + P], sel[:, 4 * hf + i, :], mhl[:, b, :],
                                     start=False, stop=True, skip_group_check=True)
                last.then_inc(d_done.sem, 1)

            def scores0(g, k):
                b, hf = k // 2, k % 2
                pe.wait_ge(e_added.sem, e_added.at(g, k + 1))
                pe.wait_ge(qm_ready.sem, qm_ready.at(g, b + 1))
                pe.matmul(XB[:, :], cT[:, b, :], qm[:, b % 2, 4 * hf:4 * hf + 4, :].rearrange("p h i -> p (h i)"),
                          start=True, stop=True).then_inc(s_done.sem, 1)

            def outputs(g, k):
                b, hf = k // 2, k % 2
                pe.wait_ge(c_done.sem, c_done.at(g, k + 1))
                pe.wait_ge(caug_ready.sem, caug_ready.at(g))
                if hf == 0:
                    pe.wait_ge(hs_ready.sem, hs_ready.at(g, b))
                for i in range(4):
                    h = 4 * hf + i
                    last = pe.matmul(HB[:, h * (D0 + 1):(h + 1) * (D0 + 1)], ex[:, k % 2, i, :],
                                     caug[:, b, h, :], start=True, stop=True)
                last.then_inc(h_done.sem, 1)

            def logits(g):
                pe.wait_ge(xh2T_ready.sem, xh2T_ready.at(g))
                for b in range(G):
                    last = pe.matmul(TB[:, E0 * b:E0 * b + E0], xh2T[:, b, :], wgate[:], start=True, stop=True)
                last.then_inc(logits_done.sem, 1)

            def turn_choice(g):
                pe.wait_ge(logits_read.sem, logits_read.at(g))
                pe.wait_ge(comb_ready.sem, comb_ready.at(g))
                for b in range(G):
                    last = pe.transpose(TB[0:E0, P * b:P * b + P], comb[:, 2, b, :], ident[:])
                last.then_inc(comb_turned.sem, 1)

            def inner(g, c):
                if c == 0:
                    pe.wait_ge(xh4T_ready.sem, xh4T_ready.at(g))
                if c:
                    pe.wait_ge(fh_ready.sem, fh_ready.at(g, c))
                pe.matmul(XB[:, :], f_in[:, P * c:P * c + P], xh4T, start=True,
                          stop=True).then_inc(fu_done.sem, 1)

            def outer(g, c):
                pe.wait_ge(fh_ready.sem, fh_ready.at(g, c + 1))
                for b in range(G):
                    last = pe.matmul(HB[:, P * b:P * b + P], fh[:, c % 2, P * b:P * b + P], f_out[:, c, :],
                                     start=(c == 0 and b == 0), stop=(c == MI - 1), skip_group_check=True)
                last.then_inc(fd_done.sem, 1)

            def experts(g, more, prev):
                n, p = g.shift(1), g.shift(-1)
                pe.wait_ge(x2hl_ready.sem, x2hl_ready.at(g))

                def spread(e):
                    if e == 0:
                        pe.wait_ge(chl_ready.sem, chl_ready.at(g))
                    else:
                        pe.wait_ge(cb_ready.sem, cb_ready.at(g, e))
                    if prev and e == 1:
                        pe.wait_ge(xh4T_ready.sem, xh4T_ready.at(p))
                    if more and e == 2:
                        pe.wait_ge(cT_ready.sem, cT_ready.at(n))
                    elif more and e == 3:
                        pe.wait_ge(gates_read.sem, gates_read.at(n))
                        pe.wait_ge(act_gates.sem, act_gates.at(n, 1))
                    elif more and e == 4:
                        pe.wait_ge(acol_ready.sem, acol_ready.at(n))
                    pe.matmul(TB[:, :], sel[:, e, :], chl[:, :], start=True, stop=True).then_inc(cb_done.sem, 1)

                def up(u):
                    e, c = u // FC, u % FC
                    if c == 0:
                        spread(e)
                    if u >= 3:
                        pe.wait_ge(hl_ready.sem, hl_ready.at(g, u - 2))
                    cols = slice(P * c, P * c + P)
                    split(UP[u % 3][:, :], w1h[:, e, cols], w1l[:, e, cols], x2h[:], x2l[:],
                          True, True).then_inc(up_done.sem, 1)

                def down(u):
                    e, c = u // FC, u % FC
                    pe.wait_ge(hl_ready.sem, hl_ready.at(g, u + 1))
                    if c == 0 and e >= 2:
                        pe.wait_ge(ymul.sem, ymul.at(g, e - 1))
                    split(YB[e % 2][:, :], w2h[:, u, :], w2l[:, u, :], uh[:, u % 4, :], ul[:, u % 4, :],
                          c == 0, c == FC - 1).then_inc(down_done.sem, 1)

                for u in range(NU + 3):
                    if u < NU:
                        up(u)
                    if u >= 3:
                        down(u - 3)
                    if prev:
                        if u == 3:
                            pe.wait_ge(xh4_ready.sem, xh4_ready.at(p))
                            pe.wait_ge(cb_ready.sem, cb_ready.at(g, 1))
                            turn(xg, xh4_turned)
                        if MLP_AT <= u < MLP_AT + MI:
                            inner(p, u - MLP_AT)
                        if MLP_AT < u <= MLP_AT + MI:
                            outer(p, u - MLP_AT - 1)
                    if more:
                        if u == 6:
                            pe.wait_ge(xh1_ready.sem, xh1_ready.at(n))
                            pe.wait_ge(cb_ready.sem, cb_ready.at(g, 2))
                            turn(xh, xh1_turned)
                        elif u == 7:
                            pe.wait_ge(c_in.sem, c_in.at(n))
                            pe.wait_ge(xhT_ready.sem, xhT_ready.at(n))
                            turn(c0, c_turned)
                        elif u == 9:
                            pe.wait_ge(cb_ready.sem, cb_ready.at(g, 3))
                            gates(n)
                        elif u == 15:
                            pe.wait_ge(cb_ready.sem, cb_ready.at(g, 4))
                            turn_rows(n)
                        if u in UNIT_AT:
                            k = UNIT_AT.index(u)
                            if k == 0 and prev:
                                pe.wait_ge(fh_ready.sem, fh_ready.at(p))
                                pe.wait_ge(res_ready.sem, res_ready.at(p))
                            decay(n, k)
                            if k:
                                outputs(n, k - 1)
                        if u - 1 in UNIT_AT:
                            scores0(n, UNIT_AT.index(u - 1))
                    if u == 30:
                        pe.wait_ge(ca_in.sem, ca_in.at(g))
                        pe.wait_ge(cb_ready.sem, cb_ready.at(g, E0))
                        turn(cA, ca_turned)

            def attention(g, more, prev):
                n = g.shift(1)

                def key_side(h):
                    if h == 0:
                        pe.wait_ge(ctl_ready.sem, ctl_ready.at(g))
                        pe.wait_ge(hl_ready.sem, hl_ready.at(g))
                    elif h >= 2:
                        pe.wait_ge(ul_ready.sem, ul_ready.at(g, h - 1))
                    if h and h % HQ == 0:
                        pe.wait_ge(v_ready.sem, v_ready.at(g, h - 2))
                    split(UP[(h + 1) % 2][:, :], wqk_h[:, h, :], wqk_l[:, h, :], flat(cTh), flat(cTl),
                          True, True).then_inc(u_done.sem, 1)

                def scores(k):
                    q, b = k // G, k % G
                    if k == 0:
                        pe.wait_ge(x3l_ready.sem, x3l_ready.at(g))
                    if b == 0:
                        pe.wait_ge(ul_ready.sem, ul_ready.at(g, HQ * (q + 1)))
                    if k == 1:
                        pe.wait_ge(ymul.sem, ymul.at(g))
                    if k >= 2:
                        pe.wait_ge(p_sub.sem, p_sub.at(g, k - 1))
                    cols = slice(P * b, P * b + P)
                    split(YB[k % 2][:, :].rearrange("p (h j) -> p h j", h=HQ), x3h[:, b, :], x3l[:, b, :],
                          uh[:, :, cols], ul[:, :, cols], True, True).then_inc(a_done.sem, 1)

                def values(k):
                    q, b = k // G, k % G
                    if k:
                        pe.wait_ge(v_ready.sem, v_ready.at(g, k))
                    if k == 0:
                        pe.wait_ge(ul_ready.sem, ul_ready.at(g, HQ - 1))
                    elif k % HQ == 2 and k < NK - 2:
                        pe.wait_ge(ul_ready.sem, ul_ready.at(g, HQ * (q + 2) - 1))
                    cols = slice(HQ * q, HQ * q + HQ)
                    split(UP[1][:, :].rearrange("p (h j) -> p h j", h=HQ), cTh[:, b, :], cTl[:, b, :],
                          wvo_h[:, cols, :], wvo_l[:, cols, :], True, True).then_inc(v_done.sem, 1)

                def turn_probs(k):
                    pe.wait_ge(p_ready.sem, p_ready.at(g, k + 1))
                    if k >= 2:
                        pe.wait_ge(pts_ready.sem, pts_ready.at(g, k - 1))
                    for i in range(HQ):
                        last = pe.transpose(PTB[k % 2][:, P * i:P * i + P], pr[:, k % 3, i, :], ident[:])
                    last.then_inc(pt_done.sem, 1)

                def weighted(k):
                    q, b = k // G, k % G
                    if k == 0 and more:
                        pe.wait_ge(hs_ready.sem, hs_ready.at(n))
                    elif k == 0 and prev:
                        pe.wait_ge(res_ready.sem, res_ready.at(g.shift(-1)))
                    pe.wait_ge(pts_ready.sem, pts_ready.at(g, k + 1))
                    pe.wait_ge(v_ready.sem, v_ready.at(g, k + 1))
                    for i in range(HQ):
                        last = pe.matmul(HB[:, P * b:P * b + P], pts[:, k % 2, i, :], vv[:, k % 2, i, :],
                                         start=(k == 0 and i == 0), stop=(q == 3 and i == HQ - 1),
                                         skip_group_check=True)
                    last.then_inc(pv_done.sem, 1)

                for h in range(HQ):
                    key_side(h)
                pe.wait_ge(yadd.sem, yadd.at(g))
                turn(yacc, y_turned)
                if more:
                    decay(n, 6)
                    outputs(n, 5)
                values(0)
                if more:
                    scores0(n, 6)
                values(1)
                pe.wait_ge(x2_ready.sem, x2_ready.at(g))
                pe.wait_ge(xh3_ready.sem, xh3_ready.at(g))
                turn(xg, xh3_turned)
                if more:
                    decay(n, 7)
                    outputs(n, 6)
                for k in range(NK + LAG):
                    next_q = k % HQ == HQ - 1 and k < NK - 1
                    if k < NK and k % HQ:
                        scores(k)
                    if next_q:
                        key_side(k + 1)
                    if k >= LAG:
                        turn_probs(k - LAG)
                    if k < NK and k % HQ == 0:
                        scores(k)
                    if next_q:
                        key_side(k + 2)
                        key_side(k + 3)
                    if k >= LAG:
                        weighted(k - LAG)
                    if next_q:
                        key_side(k + 4)
                    if 2 <= k - 1 < NK:
                        values(k - 1)
                    if more:
                        if k == 0:
                            scores0(n, 7)
                        elif k == 1:
                            outputs(n, 7)
                        elif k == 11:
                            pe.wait_ge(xh2_ready.sem, xh2_ready.at(n))
                            turn(xh, xh2_turned)
                        elif k == 12:
                            logits(n)
                        elif k == 15:
                            turn_choice(n)

            def body(g, more, prev):
                experts(g, more, prev)
                attention(g, more, prev)

            def prologue():
                setup()
                g = Group(0)
                pe.wait_ge(xh1_ready.sem, xh1_ready.at(g))
                turn(xh, xh1_turned)
                pe.wait_ge(c_in.sem, c_in.at(g))
                pe.wait_ge(xhT_ready.sem, xhT_ready.at(g))
                turn(c0, c_turned)
                gates(g)
                pe.wait_ge(gates_read.sem, gates_read.at(g))
                pe.wait_ge(act_gates.sem, act_gates.at(g, 1))
                turn_rows(g)
                for k in range(2 * G + 1):
                    if k < 2 * G:
                        decay(g, k)
                        scores0(g, k)
                    if k >= 1:
                        outputs(g, k - 1)
                pe.wait_ge(xh2_ready.sem, xh2_ready.at(g))
                turn(xh, xh2_turned)
                logits(g)
                turn_choice(g)

            def epilogue(g):
                pe.wait_ge(xh4_ready.sem, xh4_ready.at(g))
                turn(xg, xh4_turned)
                for c in range(MI + 1):
                    if c < MI:
                        inner(g, c)
                    if c >= 1:
                        outer(g, c - 1)

            run(body, prologue, epilogue, pe)


_INS = ['x', 'ctx_1024', 'L0_xattn_Wi_w', 'L0_xattn_Wi_b', 'L0_xattn_Wf_w', 'L0_xattn_Wf_b', 'L0_xattn_gn_w',
        'L0_xattn_gn_b', 'L0_ffn_gate_w', 'L0_ffn_w1', 'L0_ffn_w2', 'L1_xattn_w_q', 'L1_xattn_w_k',
        'L1_xattn_w_v', 'L1_xattn_w_o', 'L1_ffn_Win', 'L1_ffn_bin_', 'L1_ffn_W1', 'L1_ffn_b1', 'L1_ffn_W2',
        'L1_ffn_b2', 'L1_ffn_Wout', 'L1_ffn_bout']


def kernel(**inputs):
    import numpy as _np
    import concourse.bacc as _bacc
    from concourse import mybir as _mybir
    from concourse.bass_utils import run_bass_kernel_spmd as _run

    nc = _bacc.Bacc("TRN2", target_bir_lowering=False, num_devices=1, dynamic_dma_scratch_size=256)
    arrays, args = {}, []
    for name in _INS:
        a = _np.ascontiguousarray(inputs[name])
        arrays[f"in_{name}_dram"] = a
        args.append(nc.dram_tensor(f"in_{name}_dram", a.shape, _mybir.dt.from_np(a.dtype), kind="ExternalInput").ap())
    shape = arrays["in_x_dram"].shape
    args.append(nc.dram_tensor("out_0_dram", shape, _mybir.dt.float32, kind="ExternalOutput").ap())
    build(nc, *args)
    r = _run(nc, [arrays], core_ids=[0])
    return r.results[0]["out_0_dram"]
```

```python
from contextlib import ExitStack

import concourse.bass as bass
from concourse import mybir

F32 = mybir.dt.float32
F32R = mybir.dt.float32r
BF16 = mybir.dt.bfloat16
U32 = mybir.dt.uint32
ALU = mybir.AluOpType
ACT = mybir.ActivationFunctionType
AX = mybir.AxisListType.X

P = 128
G = 4
T = G * P
H0, D0 = 8, 16
E0, F0 = 8, 512
FC = F0 // P
NU = E0 * FC
H1, D1 = 16, 64
HQ = 4
NK = (H1 // HQ) * G
MI = 8
ROW2 = 32
BIG = 1e30
UNIT_AT = [17, 19, 21, 23, 25, 27]
LAG = 3
HS_AT = {22: 0, 26: 1, 31: 2}
MLP_AT = 9
EPS = 1e-5


class Group:

    def __init__(self, base, off=0):
        self.base, self.off = base, off

    def count(self, per, n):
        return self.base * per + (self.off * per + n)

    def known(self):
        return isinstance(self.base, int)

    def shift(self, d):
        return Group(self.base, self.off + d)


class Signal:

    def __init__(self, sem, per):
        self.sem, self.per = sem, per

    def at(self, g, n=None):
        v = g.count(self.per, self.per if n is None else n)
        return max(v, 0) if isinstance(v, int) else v


class Chain:

    def __init__(self, signal, eng):
        self.s, self.eng = signal, eng

    def begin(self, g):
        self.g, self.n = g, 0

    def link(self, ins):
        self.n += 1
        ins.then_inc(self.s.sem, 1)
        self.eng.wait_ge(self.s.sem, self.s.at(self.g, self.n))

    def end(self):
        assert self.n == self.s.per, (self.n, self.s.per)


def build(nc, x, ctx_in, Wi_w, Wi_b, Wf_w, Wf_b, gn_w, gn_b, gate_w, w1, w2, w_q, w_k, w_v, w_o,
          Win, bin_, W1, b1, W2, b2, Wout, bout, out):
    NG = x.shape[0] // G
    x_g = x.rearrange("(g b) s d -> g s b d", b=G)
    c_g = ctx_in.rearrange("(g b) s d -> g s b d", b=G)
    out_g = out.rearrange("(g b) s d -> g s b d", b=G)

    with ExitStack() as es:
        def sb(name, shape, dt=F32):
            return es.enter_context(nc.sbuf_tensor(name, shape, dt))

        def sig(name, per):
            return Signal(es.enter_context(nc.semaphore(name)), per)

        bank = [es.enter_context(nc.psum_tensor(f"bank{i}", [P, T], F32)) for i in range(8)]
        UP = bank[0:3]
        YB = bank[3:5]
        TB = bank[5]
        XB = bank[6]
        HB = bank[7]
        PTB = [XB, UP[2]]
        KB = [[UP[1], UP[0], UP[2], UP[0]]] + [[UP[1], UP[0], TB, UP[2]]] * 3

        ident = sb("ident", [P, P])
        ident_bf = sb("ident_bf", [P, P], BF16)
        causal = sb("causal", [P, P], BF16)
        sel = sb("sel", [ROW2 * 2, 8, P], F32R)
        headmask = sb("headmask", [P, H0])
        expert_no = sb("expert_no", [P, G, E0])
        neg_half, eps_col = sb("neg_half", [P, 32]), sb("eps_col", [P, 32])
        spare = sb("spare", [1, 1])
        keep = sb("keep", [H0, T])
        drop = sb("drop", [H0, T])
        wg = sb("wg", [ROW2 * 2, 3 * P])
        wgx = sb("wgx", [P, ROW2 * 2])
        wgc = sb("wgc", [P, ROW2 * 2])
        gbias = sb("gbias", [ROW2 * 2, 1])
        gnw = sb("gnw", [P, P])
        gnb = sb("gnb", [P, P])
        wgate = sb("wgate", [P, E0])
        w1h, w1l = sb("w1h", [P, E0, F0], F32R), sb("w1l", [P, E0, F0], F32R)
        w2h, w2l = sb("w2h", [P, NU, P], F32R), sb("w2l", [P, NU, P], F32R)
        wqk_h, wqk_l = sb("wqk_h", [P, H1, P], F32R), sb("wqk_l", [P, H1, P], F32R)
        wvo_h, wvo_l = sb("wvo_h", [P, H1, P], F32R), sb("wvo_l", [P, H1, P], F32R)
        f_inh, f_inl = sb("f_inh", [P, MI * P], F32R), sb("f_inl", [P, MI * P], F32R)
        f_bias = sb("f_bias", [P, MI])
        f_out = sb("f_out", [P, MI, P])
        f_last = sb("f_last", [P, P])
        x0, c0 = sb("x0", [P, G, P]), sb("c0", [P, G, P])
        xh = sb("xh", [P, G, P])
        xhT, cT = sb("xhT", [P, G, P]), sb("cT", [P, G, P])
        caug = sb("caug", [P, G, H0, D0 + 1])
        irow, frow = sb("irow", [H0, T]), sb("frow", [H0, T])
        trow = sb("trow", [H0, T])
        acat = sb("acat", [P, T])
        mhl = sb("mhl", [ROW2 * 2, G, P], F32R)
        acol, emd = sb("acol", [P, G, H0]), sb("emd", [P, G, H0])
        work = sb("work", [P, 5632])
        qm = work[:, 0:2048].rearrange("p (n h i) -> p n h i", n=2, h=H0)
        ex = work[:, 2048:3072].rearrange("p (n h i) -> p n h i", n=2, h=4)
        pr = work[:, 3072:4608].rearrange("p (n h i) -> p n h i", n=3, h=HQ)
        pts = work[:, 4608:5632].rearrange("p (n h i) -> p n h i", n=2, h=HQ)
        hs = sb("hs", [P, G * H0, D0 + 1])
        hn = work[:, 512:1024].rearrange("p (r d) -> p r d", d=D0)
        hq = work[:, 2048:2560].rearrange("p (r d) -> p r d", d=D0)
        sm = sb("sm", [P, 8, 32])
        stats = [sm[:, 6:8, :].rearrange("p a r -> p (a r)")[:, 6 * G * i:6 * G * i + 6 * G].rearrange("p (b s) -> p b s", s=6)
                 for i in range(2)]
        mv = [sb(f"mv{i}", [P, G, 2]) for i in range(4)]
        rstd = [sb(f"rstd{i}", [P, 32 if i == 4 else G]) for i in range(5)]
        x1, x2, x3 = sb("x1", [P, G, P]), sb("x2", [P, G, P]), sb("x3", [P, G, P])
        xh2T = work[:, 0:512].rearrange("p (b d) -> p b d", b=G)
        x2h, x2l = sb("x2h", [P, T], F32R), sb("x2l", [P, T], F32R)
        logit = sb("logit", [P, G, E0])
        top = sb("top", [P, G, 8])
        topi = sb("topi", [P, G, 8], U32)
        topf = sb("topf", [P, G, 2])
        pe12 = sb("pe12", [P, 4, G])
        comb = sb("comb", [P, 3, G, E0])
        chl = sb("chl", [ROW2 * 2, T], F32R)
        cb = sb("cb", [P, 2, T])
        yacc = sb("yacc", [P, G, P])
        ytmp = sb("ytmp", [P, 2, T])
        uh = sb("uh", [P, HQ, T], F32R)
        ul = sb("ul", [P, HQ, T], F32R)
        cA = sb("cA", [P, G, P])
        cTh, cTl = sb("cTh", [P, G, P], F32R), sb("cTl", [P, G, P], F32R)
        xg = sb("xg", [P, G, P])
        x3h, x3l = sb("x3h", [P, G, P], F32R), sb("x3l", [P, G, P], F32R)
        vv = [cb[:, 0, :], cb[:, 1, :], ytmp[:, 0, :], ytmp[:, 1, :]]
        pm = sb("pm", [P, 3, 3, HQ])
        xh4h, xh4l = (t[:, :, :].rearrange("p b d -> p (b d)") for t in (x3h, x3l))
        fh = work[:, 4608:5632].rearrange("p (n t) -> p n t", n=2)
        res = sb("res", [P, G, P])
        x3b = res

        gate_in = es.enter_context(nc.semaphore("gate_in"))
        affine_in = es.enter_context(nc.semaphore("affine_in"))
        set_pool = es.enter_context(nc.semaphore("set_pool"))
        blank = es.enter_context(nc.semaphore("blank"))
        stage_in = [es.enter_context(nc.semaphore(f"stage_in{i}")) for i in range(6)]
        stage_hi = es.enter_context(nc.semaphore("stage_hi"))
        stage_lo = es.enter_context(nc.semaphore("stage_lo"))
        qk_in = es.enter_context(nc.semaphore("qk_in"))
        vo_in = es.enter_context(nc.semaphore("vo_in"))
        dve_first = es.enter_context(nc.semaphore("dve_first"))
        gates_folded = es.enter_context(nc.semaphore("gates_folded"))
        fold_in = es.enter_context(nc.semaphore("fold_in"))
        set_pe = es.enter_context(nc.semaphore("set_pe"))
        set_act = es.enter_context(nc.semaphore("set_act"))
        set_dve = es.enter_context(nc.semaphore("set_dve"))
        ffn_in = es.enter_context(nc.semaphore("ffn_in"))
        ffn_fold = es.enter_context(nc.semaphore("ffn_fold"))
        ffn_pe = es.enter_context(nc.semaphore("ffn_pe"))
        zeroed = es.enter_context(nc.semaphore("zeroed"))

        x_in, c_in, ca_in = sig("x_in", 16), sig("c_in", 16), sig("ca_in", 16)
        stored = sig("stored", 16)
        ln_var = [sig(f"ln_var{i}", 1) for i in range(5)]
        ln_rstd = [sig(f"ln_rstd{i}", 4 if i == 4 else 1) for i in range(5)]
        dve_ln = [sig(f"dve_ln{i}", 1) for i in range(4)]
        pool_ln = [sig(f"pool_ln{i}", 1) for i in range(5)]
        xh1_ready, xh1_turned, xhT_ready = sig("xh1_ready", 1), sig("xh1_turned", 1), sig("xhT_ready", 1)
        c_turned, cT_ready, caug_ready = sig("c_turned", 1), sig("cT_ready", 1), sig("caug_ready", 1)
        gates_done, gates_read = sig("gates_done", 1), sig("gates_read", 1)
        act_gates, softplus_ready = sig("act_gates", 3), sig("softplus_ready", 1)
        dve_rows = sig("dve_rows", 6)
        acat_ready, acat_turned, acol_ready = sig("acat_ready", 1), sig("acat_turned", 1), sig("acol_ready", 1)
        qm_ready = sig("qm_ready", G)
        d_done, e_added, e_exp = sig("d_done", 2 * G), sig("e_added", 2 * G), sig("e_exp", 2 * G)
        s_done, c_done, h_done = sig("s_done", 2 * G), sig("c_done", 2 * G), sig("h_done", 2 * G)
        hs_ready, dve_gn = sig("hs_ready", G), sig("dve_gn", 9)
        hn_scaled, pool_gn = sig("hn_scaled", 1), sig("pool_gn", 2)
        x1_ready = sig("x1_ready", 1)
        xh2_ready, xh2_turned, xh2T_ready = sig("xh2_ready", 1), sig("xh2_turned", 1), sig("xh2T_ready", 1)
        x2hl_ready, dve_split = sig("x2hl_ready", 1), sig("dve_split", 1)
        logits_done, logits_read = sig("logits_done", 1), sig("logits_read", 1)
        dve_top, top_diff, top_exp = sig("dve_top", 9), sig("top_diff", 1), sig("top_exp", 1)
        comb_ready, comb_turned, chl_ready = sig("comb_ready", 1), sig("comb_turned", 1), sig("chl_ready", 1)
        dve_chl = sig("dve_chl", 1)
        cb_done, cb_ready = sig("cb_done", E0), sig("cb_ready", E0)
        up_done, hh_ready, hl_ready = sig("up_done", NU), sig("hh_ready", NU), sig("hl_ready", NU)
        down_done, ymul = sig("down_done", NU), sig("ymul", E0)
        yadd, y_turned, x2_ready = sig("yadd", E0 - 1), sig("y_turned", 1), sig("x2_ready", 1)
        ca_turned, cth_ready, ctl_ready = sig("ca_turned", 1), sig("cth_ready", 1), sig("ctl_ready", 1)
        xh3_ready, xh3_turned = sig("xh3_ready", 1), sig("xh3_turned", 1)
        x3h_ready, x3l_ready = sig("x3h_ready", 1), sig("x3l_ready", 1)
        u_done, uh_ready, ul_ready = sig("u_done", H1), sig("uh_ready", H1), sig("ul_ready", H1)
        v_done, v_ready = sig("v_done", NK), sig("v_ready", NK)
        a_done, a_max, p_exp = sig("a_done", NK), sig("a_max", NK), sig("p_exp", NK)
        r_ready, p_ready = sig("r_ready", NK), sig("p_ready", NK)
        pt_done, pts_ready, pv_done = sig("pt_done", NK), sig("pts_ready", NK), sig("pv_done", NK)
        x3_ready, x3b_ready = sig("x3_ready", 1), sig("x3b_ready", 1)
        xh4_ready, xh4_turned, xh4h_ready = sig("xh4_ready", 1), sig("xh4_turned", 1), sig("xh4h_ready", 1)
        xh4l_ready = sig("xh4l_ready", 1)
        fu_done, fh_ready, fd_done = sig("fu_done", MI), sig("fh_ready", MI), sig("fd_done", MI)
        res_ready = sig("res_ready", 1)

        selw = ytmp[0:ROW2 * 2, :, :].rearrange("p a (h i) -> p (a h) i", i=P)
        w1row = x1[:, :, :].rearrange("p b d -> p (b d)"), x2[:, :, :].rearrange("p b d -> p (b d)")
        yrow = yacc[:, :, :].rearrange("p b d -> p (b d)")
        win_s, wout_s, b2_rep = yrow[:, 0:64], yrow[0:64, 64:192], yrow[0:64, 192:320]
        bout_row, b2_col = yrow[:, 320:448], yrow[0:64, 448:449]
        bin_c, w1_c, b1_c, w2_c = (logit[:, i, :] for i in range(4))
        wT = work[:, 2048:4096]
        proj_s = [work[:, 0:1024], work[:, 1024:2048], cb[:, :, :].rearrange("p n t -> p (n t)")]
        wo_s = [x3, xg]
        stage = [work[:, 4096:4608], work[:, 4608:5120], work[:, 5120:5632], ytmp[:, 0, :], ytmp[:, 1, :],
                 res[:, :, :].rearrange("p b d -> p (b d)")]
        JB = [YB[0], YB[1], UP[2], HB]
        n_turned = lambda w, half: (2, 4, 10)[w] + half
        n_joined = lambda w, q: (0, 6, 12)[w] + q
        n_low = lambda w, q: 4 * (w - 1) + q + 1

        def joined(t, q):
            return t[:, :, :].rearrange("p (i two) d -> p two i d", two=2)[:, q % 2, 4 * (q // 2):4 * (q // 2) + 4]

        def expert_part(e, w1_, w2_):
            if e % 2 == 0:
                return w1_[:, e // 2, :]
            return w2_[:, FC * (e // 2):FC * (e // 2) + FC, :].rearrange("p c d -> p (c d)")


        block = es.enter_context(nc.Block())

        def pick(v, g):
            if g.known():
                return v[g.base + g.off]
            return v[bass.ds(g.base + g.off, 1)].rearrange("o s b d -> (o s) b d")

        def load(sp, signal, dst, src, g):
            sp.dma_start(dst[:, :, :], pick(src, g)).then_inc(signal.sem, 16)

        def store(sp, g):
            sp.dma_start(pick(out_g, g), res[:, :, :]).then_inc(stored.sem, 16)

        def run(body, prologue, epilogue, eng):
            prologue()
            body(Group(0), True, False)
            with eng.Fori(1, NG - 1) as g:
                body(Group(g), True, True)
            body(Group(NG - 1), False, True)
            epilogue(Group(NG - 1))

        @block.sync
        def _(sp):
            load(sp, x_in, x0, x_g, Group(0))
            sp.wait_ge(zeroed, 2)
            for dst, src in [
                (wg[0:H0, :], Wi_w), (wg[ROW2:ROW2 + H0, :], Wf_w),
                (gbias[0:H0, :], Wi_b.rearrange("(h o) -> h o", o=1)),
                (gbias[ROW2:ROW2 + H0, :], Wf_b.rearrange("(h o) -> h o", o=1)),
            ]:
                sp.dma_start(dst, src).then_inc(gate_in, 16)
            sp.dma_start(proj_s[0], w_q).then_inc(qk_in, 16)
            sp.dma_start(proj_s[1], w_k).then_inc(qk_in, 16)
            load(sp, c_in, c0, c_g, Group(0))
            sp.dma_start(proj_s[2], w_v).then_inc(vo_in, 16)
            for i in range(2):
                sp.dma_start(wo_s[i][:, :, :], w_o[512 * i:512 * i + 512].rearrange("(c p) d -> p c d", p=P)).then_inc(vo_in, 16)

            sp.wait_ge(fold_in, 1)
            for e in range(2 * E0):
                if e >= 6:
                    sp.wait_ge(stage_lo, e - 5)
                src = (w1[e // 2] if e % 2 == 0 else
                       w2[e // 2].rearrange("(c p) d -> p c d", p=P))
                dst = stage[e % 6]
                if e % 2:
                    dst = dst.rearrange("p (c d) -> p c d", c=FC)
                sp.dma_start(dst, src).then_inc(stage_in[e % 6], 16)
            for dst, src in [(gnw[:, :], gn_w.partition_broadcast(P)), (gnb[:, :], gn_b.partition_broadcast(P)),
                             (wgate[:, :], gate_w)]:
                sp.dma_start(dst, src).then_inc(affine_in, 16)
            units = lambda w: w.rearrange("(c m) i -> (m i) c", c=MI)
            for dst, src in [
                (w1row[0], W1[0:32].rearrange("m i -> (m i)").partition_broadcast(P)),
                (w1row[1], W1[32:64].rearrange("m i -> (m i)").partition_broadcast(P)), (win_s, Win), (wout_s, Wout),
                (bout_row, bout.partition_broadcast(P)), (b2_col, b2.rearrange("(m o) -> m o", o=1)),
                (w1_c, units(W1)), (b1_c, units(b1)), (w2_c, units(W2)),
            ]:
                sp.dma_start(dst, src, allow_slow_non_contiguous=True).then_inc(ffn_in, 16)
            for m in range(8):
                rows = slice(16 * m, 16 * m + 16)
                sp.dma_start(bin_c[rows, :], bin_.rearrange("(c m) -> m c", c=MI)[m].partition_broadcast(16),
                             allow_slow_non_contiguous=True).then_inc(ffn_in, 16)
                sp.dma_start(f_out[rows, :, :], Wout.rearrange("(c m) d -> m c d", c=MI)[m].partition_broadcast(16),
                             allow_slow_non_contiguous=True).then_inc(ffn_in, 16)

            def finish(g):
                sp.wait_ge(res_ready.sem, res_ready.at(g))
                store(sp, g)

            def body(g, more, prev):
                if more:
                    sp.wait_ge(x1_ready.sem, x1_ready.at(g))
                    load(sp, x_in, x0, x_g, g.shift(1))
                    sp.wait_ge(caug_ready.sem, caug_ready.at(g))
                    sp.wait_ge(c_turned.sem, c_turned.at(g))
                    load(sp, c_in, c0, c_g, g.shift(1))
                sp.wait_ge(ca_turned.sem, ca_turned.at(g.shift(-1)))
                load(sp, ca_in, cA, c_g, g)
                if prev:
                    finish(g.shift(-1))

            run(body, lambda: None, finish, sp)
            sp.wait_ge(stored.sem, stored.at(Group(NG - 1)))

        @block.gpsimd
        def _(pool):
            gp = nc.gpsimd
            gp.memset(ident[:], 0.0).then_inc(set_pool, 1)
            gp.memset(neg_half[:], -0.5)
            gp.memset(eps_col[:], EPS)
            pool.wait_ge(set_pool, 1)
            gp.affine_select(out=ident[:], in_=ident[:], compare_op=ALU.not_equal, fill=1.0, base=0,
                             pattern=[[-1, P]], channel_multiplier=1).then_inc(set_pool, 1)
            pool.wait_ge(blank, 1)
            gp.affine_select(out=selw, in_=selw, compare_op=ALU.not_equal, fill=1.0, base=0,
                             pattern=[[-1, 8], [0, P]], channel_multiplier=1)
            gp.affine_select(out=headmask[:], in_=headmask[:], compare_op=ALU.is_ge, fill=0.0, base=0,
                             pattern=[[-D0, H0]], channel_multiplier=1)
            gp.affine_select(out=causal[:], in_=causal[:], compare_op=ALU.is_ge, fill=-BIG, base=0,
                             pattern=[[1, P]], channel_multiplier=-1).then_inc(set_pool, 1)
            pool.wait_ge(set_pool, 3)
            gp.affine_select(out=selw, in_=selw, compare_op=ALU.not_equal, fill=1.0, base=-ROW2,
                             pattern=[[-1, 8], [0, P]], channel_multiplier=1)
            gp.affine_select(out=headmask[:], in_=headmask[:], compare_op=ALU.is_ge, fill=0.0,
                             base=D0 - 1, pattern=[[D0, H0]], channel_multiplier=-1)
            gp.affine_select(out=keep[:], in_=keep[:], compare_op=ALU.not_equal, fill=0.0, base=0,
                             pattern=[[0, G], [1, P]], channel_multiplier=0)
            gp.affine_select(out=drop[:], in_=drop[:], compare_op=ALU.not_equal, fill=-3e38, base=0,
                             pattern=[[0, G], [1, P]], channel_multiplier=0)
            gp.iota(expert_no[:], pattern=[[0, G], [1, E0]], base=0, channel_multiplier=0,
                    allow_small_or_imprecise_dtypes=True).then_inc(set_pool, 1)

            def rsqrt(i, g, var):
                n = var.shape[-1]
                r = rstd[i][:, 0:n]
                pool.wait_ge(ln_var[i].sem, ln_var[i].at(g))
                gp.tensor_tensor(r, var, eps_col[:, 0:n], ALU.add).then_inc(pool_ln[i].sem, 1)
                pool.wait_ge(pool_ln[i].sem, pool_ln[i].at(g))
                gp.tensor_tensor(r, r, neg_half[:, 0:n], ALU.pow).then_inc(ln_rstd[i].sem, 1)

            def masked_queries(g, b):
                if b == 0:
                    pool.wait_ge(xhT_ready.sem, xhT_ready.at(g))
                if b >= 2:
                    pool.wait_ge(s_done.sem, s_done.at(g, 2 * (b - 2) + 2))
                else:
                    pool.wait_ge(s_done.sem, s_done.at(g.shift(-1)))
                gp.tensor_tensor(qm[:, b % 2], xhT[:, b, :].unsqueeze(1).to_broadcast([P, H0, P]),
                                 headmask[:, :].unsqueeze(2).to_broadcast([P, H0, P]),
                                 ALU.mult).then_inc(qm_ready.sem, 1)

            def head_rstd(g, part):
                if part == 0:
                    pool.wait_ge(ln_var[4].sem, ln_var[4].at(g))
                    gp.tensor_tensor(rstd[4][:], sm[:, 5, :], eps_col[:], ALU.add).then_inc(pool_ln[4].sem, 1)
                    pool.wait_ge(pool_ln[4].sem, pool_ln[4].at(g))
                r = rstd[4][:, 8 * part:8 * part + 8]
                gp.tensor_tensor(r, r, neg_half[:, 0:8], ALU.pow).then_inc(ln_rstd[4].sem, 1)

            hb = hn[:].rearrange("p (b h) d -> p b (h d)", b=G)
            row = lambda t: t[:, :].unsqueeze(1).to_broadcast([P, G, P])

            def affine(g):
                pool.wait_ge(hn_scaled.sem, hn_scaled.at(g.shift(-1)))
                gp.tensor_tensor(hb, hb, row(gnw), ALU.mult).then_inc(pool_gn.sem, 1)
                pool.wait_ge(pool_gn.sem, pool_gn.at(g.shift(-1), 1))
                gp.tensor_tensor(hb, hb, row(gnb), ALU.add).then_inc(pool_gn.sem, 1)

            def residual0(g):
                pool.wait_ge(pool_gn.sem, pool_gn.at(g.shift(-1), 2))
                pool.wait_ge(x2_ready.sem, x2_ready.at(g.shift(-1)))
                gp.tensor_tensor(x1[:], hb, x0[:], ALU.add).then_inc(x1_ready.sem, 1)

            def expert_sum(g, e):
                pool.wait_ge(ymul.sem, ymul.at(g, e + 1))
                if e >= 2:
                    pool.wait_ge(yadd.sem, yadd.at(g, e - 1))
                gp.tensor_tensor(yacc[:, :, :].rearrange("p b d -> p (b d)"),
                                 yacc[:, :, :].rearrange("p b d -> p (b d)"), ytmp[:, e % 2, :],
                                 ALU.add).then_inc(yadd.sem, 1)

            def experts(g, more):
                n = g.shift(1)
                if more:
                    rsqrt(0, n, mv[0][:, :, 1])
                    masked_queries(n, 0)
                expert_sum(g, 1)
                if more:
                    masked_queries(n, 1)
                for e in range(2, E0 - 1):
                    expert_sum(g, e)
                    if more and e in (3, 4):
                        masked_queries(n, e - 1)

            def attention(g, more):
                n = g.shift(1)
                rsqrt(2, g, mv[2][:, :, 1])
                for k in range(NK):
                    pool.wait_ge(r_ready.sem, r_ready.at(g, k + 1))
                    gp.tensor_tensor(pr[:, k % 3], pr[:, k % 3],
                                     pm[:, k % 3, 2, :].unsqueeze(2).to_broadcast([P, HQ, P]),
                                     ALU.mult).then_inc(p_ready.sem, 1)
                    if more:
                        if k in (4, 5):
                            head_rstd(n, 2 * (k - 4))
                            head_rstd(n, 2 * (k - 4) + 1)
                        elif k == 6:
                            affine(n)
                        elif k == 7:
                            residual0(n)
                        elif k == 8:
                            rsqrt(1, n, mv[1][:, :, 1])
                rsqrt(3, g, mv[3][:, :, 1])
                pool.wait_ge(x3_ready.sem, x3_ready.at(g))
                pool.wait_ge(stored.sem, stored.at(g.shift(-1)))
                gp.tensor_tensor(x3b[:], x3[:], f_last[:, :].unsqueeze(1).to_broadcast([P, G, P]),
                                 ALU.add).then_inc(x3b_ready.sem, 1)

            def body(g, more, prev):
                experts(g, more)
                attention(g, more)

            def prologue():
                g = Group(0)
                rsqrt(0, g, mv[0][:, :, 1])
                pool.wait_ge(set_pe, n_joined(2, 3))
                for b in range(G):
                    masked_queries(g, b)
                for part in range(4):
                    head_rstd(g, part)
                rsqrt(1, g, mv[1][:, :, 1])

            run(body, prologue, lambda g: None, pool)

        @block.scalar
        def _(act):
            sc = nc.scalar
            act.preload_act_table_set("natural_log_exp_and_others")

            def turned_weights(w, half):
                act.wait_ge(set_pe, n_turned(w, half))
                dst = wT[:, 1024 * (w % 2) + 512 * half:1024 * (w % 2) + 512 * half + 512]
                sc.activation(dst, UP[half][:, :], ACT.Copy).then_inc(set_act, 1)

            def joined_high(w, q):
                act.wait_ge(set_pe, n_joined(w, q))
                sc.activation(joined(wqk_h if w == 1 else wvo_h, q), JB[q][:, :].rearrange("p (i d) -> p i d", i=4),
                              ACT.Copy, scale=D1 ** -0.5 if w == 1 else 1.0).then_inc(set_act, 1)

            def expert_high(e):
                act.wait_ge(stage_in[e % 6], 16 * (e // 6 + 1))
                sc.activation(expert_part(e, w1h, w2h), stage[e % 6], ACT.Copy).then_inc(stage_hi, 1)

            flat = lambda t: t[:].rearrange("p b d -> p (b d)")

            def queries(g):
                act.wait_ge(xh1_turned.sem, xh1_turned.at(g))
                act.wait_ge(s_done.sem, s_done.at(g.shift(-1)))
                sc.activation(flat(xhT), TB[:, :], ACT.Copy).then_inc(xhT_ready.sem, 1)

            def contexts(g):
                act.wait_ge(c_turned.sem, c_turned.at(g))
                act.wait_ge(h_done.sem, h_done.at(g.shift(-1)))
                sc.activation(flat(cT), TB[:, :], ACT.Copy).then_inc(cT_ready.sem, 1)
                sc.activation(caug[:, :, :, 0:D0], c0[:, :, :].rearrange("p b (h d) -> p b h d", h=H0),
                              ACT.Copy).then_inc(caug_ready.sem, 1)

            def gates(g):
                act.wait_ge(gates_done.sem, gates_done.at(g))
                act.wait_ge(dve_rows.sem, dve_rows.at(g.shift(-1)))
                sc.activation(frow[:], TB[ROW2:ROW2 + H0, :], ACT.Identity,
                              bias=gbias[ROW2:ROW2 + H0, :]).then_inc(act_gates.sem, 1)
                sc.activation(irow[:], TB[0:H0, :], ACT.Identity, bias=gbias[0:H0, :]).then_inc(gates_read.sem, 1)

            def softplus(g):
                act.wait_ge(act_gates.sem, act_gates.at(g, 1))
                sc.activation(trow[:], frow[:], ACT.Abs).then_inc(act_gates.sem, 1)
                act.wait_ge(act_gates.sem, act_gates.at(g, 2))
                sc.activation(trow[:], trow[:], ACT.Exp, scale=-1.0).then_inc(act_gates.sem, 1)
                act.wait_ge(act_gates.sem, act_gates.at(g, 3))
                sc.activation(trow[:], trow[:], ACT.Ln, bias=1.0).then_inc(softplus_ready.sem, 1)

            def columns(g):
                act.wait_ge(acat_turned.sem, acat_turned.at(g))
                act.wait_ge(x1_ready.sem, x1_ready.at(g.shift(-1)))
                tb = TB[:, :].rearrange("p (b r) -> p b r", b=G)
                sc.activation(acol[:], tb[:, :, 0:H0], ACT.Copy)
                sc.activation(emd[:], tb[:, :, ROW2:ROW2 + H0], ACT.Exp, scale=-1.0).then_inc(acol_ready.sem, 1)

            def decayed(g, k):
                act.wait_ge(e_added.sem, e_added.at(g, k + 1))
                sc.activation(ex[:, k % 2], ex[:, k % 2], ACT.Exp).then_inc(e_exp.sem, 1)

            def head_outputs(g, b):
                act.wait_ge(h_done.sem, h_done.at(g, 2 * b + 2))
                sc.activation(hs[:, H0 * b:H0 * b + H0, :].rearrange("p h d -> p (h d)"),
                              HB[:, 0:H0 * (D0 + 1)], ACT.Copy).then_inc(hs_ready.sem, 1)

            def tokens2(g):
                act.wait_ge(xh2_turned.sem, xh2_turned.at(g))
                sc.activation(flat(xh2T), TB[:, :], ACT.Copy).then_inc(xh2T_ready.sem, 1)

            def logits(g):
                act.wait_ge(logits_done.sem, logits_done.at(g))
                sc.activation(logit[:].rearrange("p b e -> p (b e)"), TB[:, 0:G * E0], ACT.Copy).then_inc(logits_read.sem, 1)

            def top_weight(g):
                act.wait_ge(top_diff.sem, top_diff.at(g))
                sc.activation(pe12[:, 1, :], pe12[:, 0, :], ACT.Exp).then_inc(top_exp.sem, 1)

            def tokens4(g):
                act.wait_ge(xh4_turned.sem, xh4_turned.at(g))
                sc.activation(xh4h, TB[:, :], ACT.Copy).then_inc(xh4h_ready.sem, 1)

            def mlp_inner(g, c, bank=XB):
                act.wait_ge(fu_done.sem, fu_done.at(g, c + 1))
                if c >= 2:
                    act.wait_ge(fd_done.sem, fd_done.at(g, c - 1))
                sc.activation(fh[:, c % 2, :], bank[:, :], ACT.Relu,
                              bias=f_bias[:, c:c + 1]).then_inc(fh_ready.sem, 1)

            def inner_high(g, u):
                act.wait_ge(up_done.sem, up_done.at(g, u + 1))
                if u >= 4:
                    act.wait_ge(down_done.sem, down_done.at(g, u - 3))
                sc.activation(uh[:, u % 4, :], UP[u % 3][:, :], ACT.Relu).then_inc(hh_ready.sem, 1)

            def experts(g, more, prev):
                n, p = g.shift(1), g.shift(-1)
                for u in range(NU):
                    e = u // FC
                    if u:
                        inner_high(g, u)
                    if u % FC == 1:
                        act.wait_ge(cb_done.sem, cb_done.at(g, e + 1))
                        if e >= 2:
                            act.wait_ge(ymul.sem, ymul.at(g, e - 1))
                        else:
                            act.wait_ge(ymul.sem, ymul.at(g.shift(-1)))
                        sc.activation(cb[:, e % 2, :], TB[:, :], ACT.Copy).then_inc(cb_ready.sem, 1)
                    if prev:
                        if u == 7:
                            tokens4(p)
                        if MLP_AT <= u < MLP_AT + MI:
                            mlp_inner(p, u - MLP_AT)
                    if more:
                        if u == 9:
                            queries(n)
                        elif u == 10:
                            contexts(n)
                        elif u == 11:
                            gates(n)
                        elif u == 12:
                            softplus(n)
                        elif u == 16:
                            columns(n)
                        if u - 1 in UNIT_AT:
                            decayed(n, UNIT_AT.index(u - 1))
                        if u == 31:
                            decayed(n, 6)
                        if u in HS_AT:
                            head_outputs(n, HS_AT[u])
                    if u == 30:
                        act.wait_ge(ca_turned.sem, ca_turned.at(g))
                        sc.activation(flat(cTh), TB[:, :], ACT.Copy).then_inc(cth_ready.sem, 1)

            def attention(g, more):
                n = g.shift(1)

                def key_side(h):
                    act.wait_ge(u_done.sem, u_done.at(g, h + 1))
                    sc.activation(uh[:, h % HQ, :], KB[h // HQ][h % HQ][:, :], ACT.Copy).then_inc(uh_ready.sem, 1)

                def exponentials(k):
                    act.wait_ge(a_max.sem, a_max.at(g, k + 1))
                    if k >= 3:
                        act.wait_ge(pt_done.sem, pt_done.at(g, k - 2))
                    for i in range(HQ):
                        last = sc.activation(pr[:, k % 3, i, :], YB[k % 2][:, P * i:P * i + P], ACT.Exp,
                                             bias=pm[:, k % 3, 0, i:i + 1], accum_out=pm[:, k % 3, 1, i:i + 1])
                    last.then_inc(p_exp.sem, 1)

                def turned(k):
                    act.wait_ge(pt_done.sem, pt_done.at(g, k + 1))
                    if k >= 2:
                        act.wait_ge(pv_done.sem, pv_done.at(g, k - 1))
                    sc.activation(pts[:, k % 2].rearrange("p h i -> p (h i)"), PTB[k % 2][:, :],
                                  ACT.Copy).then_inc(pts_ready.sem, 1)

                def values(k):
                    act.wait_ge(v_done.sem, v_done.at(g, k + 1))
                    sc.activation(vv[k % 4], UP[1][:, :],
                                  ACT.Copy).then_inc(v_ready.sem, 1)

                for h in range(HQ):
                    key_side(h)
                if more:
                    decayed(n, 7)
                values(0)
                values(1)
                act.wait_ge(xh3_turned.sem, xh3_turned.at(g))
                sc.activation(flat(x3h), TB[:, :], ACT.Copy).then_inc(x3h_ready.sem, 1)
                for k in range(NK + LAG):
                    next_q = k % HQ == HQ - 1 and k < NK - 1
                    if k >= LAG:
                        turned(k - LAG)
                    if next_q:
                        for h in range(k + 1, k + 1 + HQ):
                            key_side(h)
                    if k < NK:
                        exponentials(k)
                    if more:
                        if k == 0:
                            head_outputs(n, 3)
                        elif k == 11:
                            tokens2(n)
                        elif k == 12:
                            logits(n)
                        elif k == 13:
                            top_weight(n)
                        elif k == NK + 1:
                            inner_high(n, 0)

            def body(g, more, prev):
                experts(g, more, prev)
                attention(g, more)

            def prologue():
                g = Group(0)
                act.wait_ge(set_pe, 1)
                sc.activation(wgx[:], TB[:, 0:64], ACT.Copy)
                sc.activation(wgc[:], TB[:, 64:128], ACT.Copy).then_inc(set_act, 1)
                for w in range(2):
                    for half in range(2):
                        turned_weights(w, half)
                queries(g)
                contexts(g)
                joined_high(1, 0)
                joined_high(1, 1)
                gates(g)
                softplus(g)
                for q in range(4):
                    if q >= 2:
                        joined_high(1, q)
                    expert_high(q)
                for half in range(2):
                    turned_weights(2, half)
                for q in range(4):
                    joined_high(2, q)
                    expert_high(4 + q)
                columns(g)
                for k in range(2 * G + 1):
                    if k < 2 * G:
                        decayed(g, k)
                        expert_high(8 + k)
                    if k >= 2 and k % 2 == 0:
                        head_outputs(g, k // 2 - 1)
                tokens2(g)
                logits(g)
                top_weight(g)
                inner_high(g, 0)

            def epilogue(g):
                tokens4(g)
                for c in range(MI):
                    mlp_inner(g, c, (XB, UP[0])[c % 2])

            run(body, prologue, epilogue, act)

        @block.vector
        def _(dve):
            v = nc.vector
            ln_chain = [Chain(s, dve) for s in dve_ln]
            rows, gn, tp = Chain(dve_rows, dve), Chain(dve_gn, dve), Chain(dve_top, dve)

            def joined_low(w, q):
                dve.wait_ge(set_act, n_joined(w, q))
                hi, lo = (wqk_h, wqk_l) if w == 1 else (wvo_h, wvo_l)
                v.scalar_tensor_tensor(joined(lo, q), JB[q][:, :].rearrange("p (i d) -> p i d", i=4),
                                       D1 ** -0.5 if w == 1 else 1.0, joined(hi, q),
                                       ALU.mult, ALU.subtract).then_inc(set_dve, 1)

            def expert_low(e):
                dve.wait_ge(stage_hi, e + 1)
                v.tensor_tensor(expert_part(e, w1l, w2l), stage[e % 6], expert_part(e, w1h, w2h),
                                ALU.subtract).then_inc(stage_lo, 1)

            def fold_mlp():
                dve.wait_ge(ffn_in, 16 * 25)
                v.tensor_copy(b2_rep, b2_col.to_broadcast([64, P])).then_inc(ffn_fold, 1)
                v.tensor_tensor(bin_c, bin_c, w1_c, ALU.mult).then_inc(ffn_fold, 1)
                for n in range(2):
                    prod = w1row[n].rearrange("p (m i) -> p m i", i=16)
                    last = v.tensor_tensor(prod, win_s[:, 32 * n:32 * n + 32].unsqueeze(2).to_broadcast([P, 32, 16]),
                                           prod, ALU.mult)
                last.then_inc(ffn_fold, 1)
                v.tensor_tensor(f_out[:], f_out[:], w2_c.unsqueeze(2).to_broadcast([P, MI, P]), ALU.mult)
                dve.wait_ge(ffn_fold, 3)
                v.tensor_tensor(f_bias[:], bin_c, b1_c, ALU.add)
                for n in range(2):
                    last = v.tensor_copy(f_inh[:, 512 * n:512 * n + 512], w1row[n])
                last.then_inc(ffn_fold, 1)
                dve.wait_ge(ffn_fold, 4)
                for n in range(2):
                    cols = slice(512 * n, 512 * n + 512)
                    last = v.tensor_tensor(f_inl[:, cols], w1row[n], f_inh[:, cols], ALU.subtract)
                last.then_inc(ffn_fold, 1)
                dve.wait_ge(ffn_fold, 5)

            flat = lambda t: t[:].rearrange("p b d -> p (b d)")

            def moments(i, g, src):
                ch = ln_chain[i]
                ch.begin(g)
                for b in range(G):
                    last = v.bn_stats(stats[i % 2][:, b, :], src[:, b, :])
                ch.link(last)
                v.memset(spare[:, :], 0.0)
                for b in range(G):
                    last = v.bn_aggr(mv[i][:, b, :], stats[i % 2][:, b, :])
                last.then_inc(ln_var[i].sem, 1)

            def normalise(i, g, src, dst, ready):
                dve.wait_ge(ln_rstd[i].sem, ln_rstd[i].at(g))
                for b in range(G):
                    last = v.tensor_scalar(dst[:, b, :], src[:, b, :], mv[i][:, b, 0:1],
                                           rstd[i][:, b:b + 1], ALU.subtract, ALU.mult)
                last.then_inc(ready.sem, 1)

            def moments0(g):
                dve.wait_ge(x_in.sem, x_in.at(g))
                moments(0, g, x0)

            def normalise0(g):
                dve.wait_ge(xh2_turned.sem, xh2_turned.at(g.shift(-1)))
                normalise(0, g, x0, xh, xh1_ready)

            def gate_rows(g, part):
                if part == 0:
                    dve.wait_ge(softplus_ready.sem, softplus_ready.at(g))
                    dve.wait_ge(gates_read.sem, gates_read.at(g))
                    rows.begin(g)
                    rows.link(v.scalar_tensor_tensor(trow[:], frow[:], 0.0, trow[:], ALU.min, ALU.subtract))
                    rows.link(v.tensor_tensor_scan(frow[:], keep[:], trow[:], 0.0, ALU.mult, ALU.add))
                elif part == 1:
                    rows.link(v.tensor_tensor(acat[0:H0, :], irow[:], frow[:], ALU.subtract))
                    rows.link(v.tensor_tensor_scan(trow[:], drop[:], acat[0:H0, :], 0.0, ALU.add, ALU.max))
                    v.tensor_tensor(acat[ROW2:ROW2 + H0, :], frow[:], trow[:], ALU.add).then_inc(acat_ready.sem, 1)
                else:
                    dve.wait_ge(d_done.sem, d_done.at(g.shift(-1)))
                    mh = flat(mhl)
                    rows.link(v.tensor_scalar(mh[0:H0, :], trow[:], -1.0, None, ALU.mult))
                    rows.link(v.scalar_tensor_tensor(mh[ROW2:ROW2 + H0, :], trow[:], -1.0, mh[0:H0, :],
                                                     ALU.mult, ALU.subtract))
                    rows.end()

            def decay(g, k, bank=XB):
                b, hf = k // 2, k % 2
                if k == 0:
                    dve.wait_ge(acol_ready.sem, acol_ready.at(g))
                dve.wait_ge(d_done.sem, d_done.at(g, k + 1))
                dve.wait_ge(h_done.sem, h_done.at(g, k - 1))
                v.tensor_tensor(ex[:, k % 2], bank[:, :].rearrange("p (h i) -> p h i", h=4),
                                acol[:, b, 4 * hf:4 * hf + 4].unsqueeze(2).to_broadcast([P, 4, P]),
                                ALU.add).then_inc(e_added.sem, 1)

            def weigh(g, k, bank=XB):
                dve.wait_ge(s_done.sem, s_done.at(g, k + 1))
                dve.wait_ge(e_exp.sem, e_exp.at(g, k + 1))
                v.tensor_tensor(ex[:, k % 2], bank[:, :].rearrange("p (h i) -> p h i", h=4),
                                ex[:, k % 2], ALU.mult).then_inc(c_done.sem, 1)

            def head_norm(g, part):
                R = G * H0
                wide = lambda ap: ap.unsqueeze(2).to_broadcast([P, R, D0])
                if part == 0:
                    dve.wait_ge(hs_ready.sem, hs_ready.at(g))
                    gn.begin(g)
                    gn.link(v.scalar_tensor_tensor(sm[:, 0, :], hs[:, :, D0], -1.0, hs[:, :, D0], ALU.mult, ALU.max))
                    gn.link(v.tensor_tensor(sm[:, 0, :], sm[:, 0, :], emd[:].rearrange("p b h -> p (b h)"), ALU.max))
                    gn.link(v.tensor_scalar(sm[:, 1, :], sm[:, 0, :], 1e-6, None, ALU.add))
                    gn.link(v.reciprocal(sm[:, 2, :], sm[:, 1, :]))
                    gn.link(v.tensor_tensor(hn[:], hs[:, :, 0:D0], wide(sm[:, 2, :]), ALU.mult))
                elif part == 1:
                    gn.link(v.reduce_sum(sm[:, 3, :], hn[:], AX))
                    gn.link(v.scalar_tensor_tensor(hn[:], wide(sm[:, 3, :]), -1.0 / D0, hn[:], ALU.mult, ALU.add))
                elif part == 2:
                    gn.link(v.tensor_tensor(hq[:], hn[:], hn[:], ALU.mult))
                    gn.link(v.reduce_sum(sm[:, 4, :], hq[:], AX))
                    v.tensor_scalar(sm[:, 5, :], sm[:, 4, :], 1.0 / D0, None, ALU.mult).then_inc(ln_var[4].sem, 1)
                    gn.end()
                else:
                    dve.wait_ge(ln_rstd[4].sem, ln_rstd[4].at(g))
                    v.tensor_tensor(hn[:], hn[:], wide(rstd[4][:, :]), ALU.mult).then_inc(hn_scaled.sem, 1)

            def finish_heads(g, b):
                seq, rows8 = hn[:, H0 * b:H0 * b + H0, :], hn[:, H0 * b:H0 * b + H0, :].rearrange("p h d -> p (h d)")
                dve.wait_ge(ln_rstd[4].sem, ln_rstd[4].at(g, b + 1))
                v.tensor_tensor(seq, seq, rstd[4][:, H0 * b:H0 * b + H0].unsqueeze(2).to_broadcast([P, H0, D0]),
                                ALU.mult).then_inc(dve_first, 1)
                dve.wait_ge(dve_first, 3 * b + 1)
                v.tensor_tensor(rows8, rows8, gnw[:, :], ALU.mult).then_inc(dve_first, 1)
                dve.wait_ge(dve_first, 3 * b + 2)
                v.tensor_tensor(rows8, rows8, gnb[:, :], ALU.add).then_inc(dve_first, 1)
                dve.wait_ge(dve_first, 3 * b + 3)
                last = v.tensor_tensor(x1[:, b, :], rows8, x0[:, b, :], ALU.add)
                if b == G - 1:
                    last.then_inc(x1_ready.sem, 1)

            def moments1(g):
                dve.wait_ge(x1_ready.sem, x1_ready.at(g))
                moments(1, g, x1)

            def normalise1(g):
                dve.wait_ge(xh1_turned.sem, xh1_turned.at(g))
                normalise(1, g, x1, xh, xh2_ready)

            def split_tokens(g):
                dve.wait_ge(xh2T_ready.sem, xh2T_ready.at(g))
                dve.wait_ge(up_done.sem, up_done.at(g.shift(-1)))
                v.tensor_copy(x2h[:], flat(xh2T)).then_inc(dve_split.sem, 1)
                dve.wait_ge(dve_split.sem, dve_split.at(g))
                v.tensor_tensor(x2l[:], flat(xh2T), x2h[:], ALU.subtract).then_inc(x2hl_ready.sem, 1)

            def choose(g, part):
                wide2 = lambda ap: ap.unsqueeze(2).to_broadcast([P, G, E0])
                if part == 0:
                    dve.wait_ge(logits_read.sem, logits_read.at(g))
                    dve.memset(spare[:, :], 0.0)
                    tp.begin(g)
                    for b in range(G):
                        last = v.max(top[:, b, :], logit[:, b, :])
                    tp.link(last)
                    v.memset(spare[:, :], 0.0)
                    v.tensor_tensor(pe12[:, 0, :], top[:, :, 1], top[:, :, 0], ALU.subtract).then_inc(top_diff.sem, 1)
                    for b in range(G):
                        last = v.max_index(topi[:, b, :], top[:, b, :], logit[:, b, :])
                    tp.link(last)
                    tp.link(v.tensor_copy(topf[:], topi[:, :, 0:2]))
                    v.tensor_tensor(comb[:, 0], expert_no[:], wide2(topf[:, :, 0]), ALU.is_equal)
                    tp.link(v.tensor_tensor(comb[:, 1], expert_no[:], wide2(topf[:, :, 1]), ALU.is_equal))
                else:
                    dve.wait_ge(top_exp.sem, top_exp.at(g))
                    tp.link(v.tensor_scalar(pe12[:, 2, :], pe12[:, 1, :], 1.0, None, ALU.add))
                    tp.link(v.reciprocal(pe12[:, 3, :], pe12[:, 2, :]))
                    tp.link(v.tensor_tensor(pe12[:, 2, :], pe12[:, 1, :], pe12[:, 3, :], ALU.mult))
                    tp.link(v.tensor_tensor(comb[:, 0], comb[:, 0], wide2(pe12[:, 3, :]), ALU.mult))
                    tp.link(v.tensor_tensor(comb[:, 1], comb[:, 1], wide2(pe12[:, 2, :]), ALU.mult))
                    tp.end()
                    dve.wait_ge(comb_turned.sem, comb_turned.at(g.shift(-1)))
                    v.tensor_tensor(comb[:, 2], comb[:, 0], comb[:, 1], ALU.add).then_inc(comb_ready.sem, 1)

            def expert_rows(g):
                dve.wait_ge(comb_turned.sem, comb_turned.at(g))
                dve.wait_ge(cb_done.sem, cb_done.at(g.shift(-1)))
                v.tensor_copy(chl[0:E0, :], TB[0:E0, :]).then_inc(dve_chl.sem, 1)
                dve.wait_ge(dve_chl.sem, dve_chl.at(g))
                v.tensor_tensor(chl[ROW2:ROW2 + E0, :], TB[0:E0, :], chl[0:E0, :],
                                ALU.subtract).then_inc(chl_ready.sem, 1)

            def residual3(g):
                dve.wait_ge(pv_done.sem, pv_done.at(g))
                v.tensor_tensor(flat(x3), HB[:, :], flat(x2), ALU.add).then_inc(x3_ready.sem, 1)

            def moments3(g):
                dve.wait_ge(x3_ready.sem, x3_ready.at(g))
                moments(3, g, x3)

            def normalise3(g):
                dve.wait_ge(xh3_turned.sem, xh3_turned.at(g))
                normalise(3, g, x3, xg, xh4_ready)

            def tokens4(g):
                dve.wait_ge(xh4h_ready.sem, xh4h_ready.at(g))
                v.tensor_tensor(xh4l, TB[:, :], xh4h, ALU.subtract).then_inc(xh4l_ready.sem, 1)

            def result(g):
                dve.wait_ge(fd_done.sem, fd_done.at(g))
                dve.wait_ge(x3b_ready.sem, x3b_ready.at(g))
                v.tensor_tensor(flat(res), HB[:, :], flat(x3b), ALU.add).then_inc(res_ready.sem, 1)

            def experts(g, more, prev):
                n, p = g.shift(1), g.shift(-1)

                def scale_out(e):
                    dve.wait_ge(down_done.sem, down_done.at(g, FC * e + FC))
                    dve.wait_ge(cb_ready.sem, cb_ready.at(g, e + 1))
                    if e == 0:
                        dve.wait_ge(y_turned.sem, y_turned.at(g.shift(-1)))
                        dst = flat(yacc)
                    else:
                        if e >= 3:
                            dve.wait_ge(yadd.sem, yadd.at(g, e - 2))
                        else:
                            dve.wait_ge(yadd.sem, yadd.at(g.shift(-1)))
                        dst = ytmp[:, e % 2, :]
                    v.tensor_tensor(dst, YB[e % 2][:, :], cb[:, e % 2, :], ALU.mult).then_inc(ymul.sem, 1)

                for u in range(NU):
                    dve.wait_ge(hh_ready.sem, hh_ready.at(g, u + 1))
                    v.scalar_tensor_tensor(ul[:, u % 4, :], UP[u % 3][:, :], 0.0, uh[:, u % 4, :],
                                           ALU.max, ALU.subtract).then_inc(hl_ready.sem, 1)
                    if prev and u == 7:
                        tokens4(p)
                    if u % FC == FC - 1 and u > FC:
                        scale_out(u // FC - 1)
                    if prev:
                        if u == 1:
                            residual3(p)
                        elif u == 2:
                            moments3(p)
                        elif u == 4:
                            normalise3(p)
                        elif u == MLP_AT + MI + 1:
                            result(p)
                    if more:
                        if u == 5:
                            moments0(n)
                        elif u == 7:
                            normalise0(n)
                        elif 13 <= u <= 15:
                            gate_rows(n, u - 13)
                        if u - 1 in UNIT_AT:
                            weigh(n, UNIT_AT.index(u - 1))
                        if u in UNIT_AT:
                            decay(n, UNIT_AT.index(u))
                    if more and u == 30:
                        decay(n, 6)
                    if u == 30:
                        dve.wait_ge(cth_ready.sem, cth_ready.at(g))
                        v.tensor_tensor(flat(cTl), TB[:, :], flat(cTh), ALU.subtract).then_inc(ctl_ready.sem, 1)
                scale_out(E0 - 1)
                dve.wait_ge(ymul.sem, ymul.at(g))
                dve.wait_ge(yadd.sem, yadd.at(g, E0 - 2))
                v.tensor_tensor(flat(yacc), flat(yacc), ytmp[:, (E0 - 1) % 2, :], ALU.add).then_inc(yadd.sem, 1)

            def attention(g, more):
                n = g.shift(1)

                def key_side(h):
                    dve.wait_ge(uh_ready.sem, uh_ready.at(g, h + 1))
                    v.tensor_tensor(ul[:, h % HQ, :], KB[h // HQ][h % HQ][:, :], uh[:, h % HQ, :],
                                    ALU.subtract).then_inc(ul_ready.sem, 1)

                def row_max(k):
                    s = YB[k % 2][:, :].rearrange("p (h j) -> p h j", h=HQ)
                    dve.wait_ge(a_done.sem, a_done.at(g, k + 1))
                    if k >= 3:
                        dve.wait_ge(p_exp.sem, p_exp.at(g, k - 2))
                    v.reduce_max(pm[:, k % 3, 0, :], s, AX, negate=True).then_inc(a_max.sem, 1)

                def values(k):
                    dve.wait_ge(v_done.sem, v_done.at(g, k + 1))
                    if k >= 4:
                        dve.wait_ge(pv_done.sem, pv_done.at(g, k - 3))
                    v.tensor_copy(vv[k % 4], UP[1][:, :]).then_inc(v_ready.sem, 1)

                def row_scale(k):
                    dve.wait_ge(p_exp.sem, p_exp.at(g, k + 1))
                    v.reciprocal(pm[:, k % 3, 2, :], pm[:, k % 3, 1, :]).then_inc(r_ready.sem, 1)

                key_side(0)
                key_side(1)
                if more:
                    weigh(n, 6)
                dve.wait_ge(y_turned.sem, y_turned.at(g))
                v.tensor_tensor(flat(x2), TB[:, :], flat(x1), ALU.add).then_inc(x2_ready.sem, 1)
                dve.wait_ge(x2_ready.sem, x2_ready.at(g))
                moments(2, g, x2)
                if more:
                    decay(n, 7)
                key_side(2)
                key_side(3)
                dve.wait_ge(xh4_turned.sem, xh4_turned.at(g.shift(-1)))
                normalise(2, g, x2, xg, xh3_ready)
                if more:
                    weigh(n, 7)
                dve.wait_ge(x3h_ready.sem, x3h_ready.at(g))
                v.tensor_tensor(flat(x3l), TB[:, :], flat(x3h), ALU.subtract).then_inc(x3l_ready.sem, 1)
                for k in range(NK + 1):
                    next_q = k % HQ == HQ - 1 and k < NK - 1
                    if k < NK:
                        row_max(k)
                    if k >= 1:
                        row_scale(k - 1)
                    if next_q:
                        for h in range(k + 1, k + 1 + HQ):
                            key_side(h)
                    if 2 <= k + 1 < NK:
                        values(k + 1)
                    if more:
                        if 2 <= k <= 4:
                            head_norm(n, k - 2)
                        elif k == 7:
                            head_norm(n, 3)
                        elif k == 9:
                            moments1(n)
                        elif k == 10:
                            normalise1(n)
                        elif k == 12:
                            split_tokens(n)
                        elif k == 13:
                            choose(n, 0)
                        elif k == 14:
                            choose(n, 1)
                        elif k == 16:
                            expert_rows(n)

            def body(g, more, prev):
                experts(g, more, prev)
                attention(g, more)

            def prologue():
                g = Group(0)
                v.memset(gbias[:], 0.0).then_inc(zeroed, 1)
                v.memset(wg[:], 0.0).then_inc(zeroed, 1)
                v.memset(selw, 0.0)
                v.memset(headmask[:], D0 ** -0.5)
                v.memset(causal[:], 0.0)
                v.memset(keep[:], 1.0)
                v.memset(drop[:], 0.0).then_inc(blank, 1)
                v.memset(acat[:], 0.0)
                v.memset(mhl[:].bitcast(F32), 0.0)
                v.memset(chl[:].bitcast(F32), 0.0)
                v.memset(caug[:], 1.0)
                moments0(g)
                dve.wait_ge(gate_in, 16 * 4)
                v.tensor_tensor(wg[:, P:2 * P], wg[:, P:2 * P], wg[:, 2 * P:3 * P], ALU.add).then_inc(gates_folded, 1)
                dve.wait_ge(set_pool, 4)
                v.tensor_copy(ident_bf[:], ident[:])
                v.tensor_copy(sel[:], selw).then_inc(fold_in, 1)
                normalise0(g)
                joined_low(1, 0)
                joined_low(1, 1)
                for part in range(3):
                    gate_rows(g, part)
                for q in range(4):
                    if q >= 2:
                        joined_low(1, q)
                    expert_low(q)
                for q in range(4):
                    joined_low(2, q)
                    expert_low(4 + q)
                for k in range(2 * G):
                    decay(g, k, (XB, YB[0])[k % 2])
                    if k:
                        expert_low(7 + k)
                    weigh(g, k, (UP[0], UP[1])[k % 2])
                expert_low(15)
                for part in range(3):
                    head_norm(g, part)
                fold_mlp()
                dve.wait_ge(ffn_pe, 1)
                v.tensor_tensor(f_last[:], UP[2][:, 0:P], bout_row, ALU.add).then_inc(ffn_fold, 1)
                dve.wait_ge(affine_in, 16 * 3)
                for b in range(G):
                    finish_heads(g, b)
                moments1(g)
                normalise1(g)
                split_tokens(g)
                choose(g, 0)
                choose(g, 1)
                expert_rows(g)

            def epilogue(g):
                residual3(g)
                moments3(g)
                normalise3(g)
                tokens4(g)
                result(g)

            run(body, prologue, epilogue, dve)

        @block.tensor
        def _(pe):
            def split(o, lh, ll, rh, rl, start, stop):
                pe.matmul(o, lh, rh, start=start, stop=False)
                pe.matmul(o, lh, rl, start=False, stop=False)
                return pe.matmul(o, ll, rh, start=False, stop=stop)

            def turn(src, signal):
                for b in range(G):
                    last = pe.transpose(TB[:, P * b:P * b + P], src[:, b, :], ident[:])
                last.then_inc(signal.sem, 1)

            def turn_gates():
                pe.wait_ge(gates_folded, 1)
                pe.wait_ge(set_pool, 2)
                pe.transpose(TB[:, 0:64], wg[:, 0:P], ident[0:64, 0:64])
                pe.transpose(TB[:, 64:128], wg[:, P:2 * P], ident[0:64, 0:64]).then_inc(set_pe, 1)

            def turn_weights(w, half):
                if w < 2:
                    pe.wait_ge(qk_in, 16 * 2)
                else:
                    pe.wait_ge(vo_in, 16 * 3)
                if w:
                    pe.wait_ge(set_act, n_turned(w - 1, half))
                for i in range(4):
                    col = 512 * half + P * i
                    last = pe.transpose(UP[half][:, P * i:P * i + P], proj_s[w][:, col:col + P], ident[:])
                last.then_inc(set_pe, 1)

            def join(w, q):
                pe.wait_ge(set_act, n_turned(w, 1))
                if w == 2:
                    pe.wait_ge(set_dve, n_low(1, q))
                par, lo = q % 2, 4 * (q // 2)
                rows = slice(64 * par, 64 * par + 64)
                for i in range(4):
                    c = lo + i
                    if w == 1:
                        lhs = wT[rows, 1024 + P * c:1024 + P * c + P]
                        rhs = wT[rows, P * c:P * c + P]
                    else:
                        lhs = wT[rows, P * c:P * c + P]
                        rhs = wo_s[c // 4][rows, c % 4, :]
                    last = pe.matmul(JB[q][:, P * i:P * i + P], lhs, rhs, start=True, stop=True)
                last.then_inc(set_pe, 1)

            flat = lambda t: t[:].rearrange("p b d -> p (b d)")

            def gates(g):
                pe.wait_ge(cT_ready.sem, cT_ready.at(g))
                pe.matmul(TB[0:64, :], wgx[:], flat(xhT), start=True, stop=False)
                pe.matmul(TB[0:64, :], wgc[:], flat(cT), start=False, stop=True).then_inc(gates_done.sem, 1)

            def turn_rows(g):
                pe.wait_ge(acat_ready.sem, acat_ready.at(g))
                for b in range(G):
                    last = pe.transpose(TB[:, P * b:P * b + P], acat[:, P * b:P * b + P], ident[:])
                last.then_inc(acat_turned.sem, 1)

            def decay(g, k, bank=XB):
                b, hf = k // 2, k % 2
                if k == 0:
                    pe.wait_ge(dve_rows.sem, dve_rows.at(g))
                pe.matmul(bank[:, :], ident_bf[:], causal[:, :].unsqueeze(1).to_broadcast([P, 4, P]),
                          start=True, stop=True)
                for i in range(4):
                    last = pe.matmul(bank[:, P * i:P * i + P], sel[:, 4 * hf + i, :], mhl[:, b, :],
                                     start=False, stop=True, skip_group_check=True)
                last.then_inc(d_done.sem, 1)

            def scores0(g, k, bank=XB):
                b, hf = k // 2, k % 2
                pe.wait_ge(qm_ready.sem, qm_ready.at(g, b + 1))
                pe.matmul(bank[:, :], cT[:, b, :], qm[:, b % 2, 4 * hf:4 * hf + 4, :].rearrange("p h i -> p (h i)"),
                          start=True, stop=True).then_inc(s_done.sem, 1)

            def decay_after(g, k):
                pe.wait_ge(c_done.sem, c_done.at(g, k))
                decay(g, k)

            def scores_after(g, k):
                pe.wait_ge(e_added.sem, e_added.at(g, k + 1))
                scores0(g, k)

            def outputs(g, k):
                b, hf = k // 2, k % 2
                pe.wait_ge(c_done.sem, c_done.at(g, k + 1))
                pe.wait_ge(caug_ready.sem, caug_ready.at(g))
                if hf == 0:
                    pe.wait_ge(hs_ready.sem, hs_ready.at(g, b))
                for i in range(4):
                    h = 4 * hf + i
                    last = pe.matmul(HB[:, h * (D0 + 1):(h + 1) * (D0 + 1)], ex[:, k % 2, i, :],
                                     caug[:, b, h, :], start=True, stop=True)
                last.then_inc(h_done.sem, 1)

            def logits(g):
                pe.wait_ge(xh2T_ready.sem, xh2T_ready.at(g))
                for b in range(G):
                    last = pe.matmul(TB[:, E0 * b:E0 * b + E0], xh2T[:, b, :], wgate[:], start=True, stop=True)
                last.then_inc(logits_done.sem, 1)

            def turn_choice(g):
                pe.wait_ge(logits_read.sem, logits_read.at(g))
                pe.wait_ge(comb_ready.sem, comb_ready.at(g))
                for b in range(G):
                    last = pe.transpose(TB[0:E0, P * b:P * b + P], comb[:, 2, b, :], ident[:])
                last.then_inc(comb_turned.sem, 1)

            def inner(g, c, bank=XB, alone=True):
                if c == 0:
                    pe.wait_ge(xh4l_ready.sem, xh4l_ready.at(g))
                elif alone:
                    pe.wait_ge(fh_ready.sem, fh_ready.at(g, c))
                cols = slice(P * c, P * c + P)
                split(bank[:, :], f_inh[:, cols], f_inl[:, cols], xh4h, xh4l, True, True).then_inc(fu_done.sem, 1)

            def outer(g, c):
                pe.wait_ge(fh_ready.sem, fh_ready.at(g, c + 1))
                for b in range(G):
                    last = pe.matmul(HB[:, P * b:P * b + P], fh[:, c % 2, P * b:P * b + P], f_out[:, c, :],
                                     start=(c == 0 and b == 0), stop=(c == MI - 1), skip_group_check=True)
                last.then_inc(fd_done.sem, 1)

            def up(g, u):
                e, c = u // FC, u % FC
                if u >= 3:
                    pe.wait_ge(hl_ready.sem, hl_ready.at(g, u - 2))
                cols = slice(P * c, P * c + P)
                split(UP[u % 3][:, :], w1h[:, e, cols], w1l[:, e, cols], x2h[:], x2l[:],
                      True, True).then_inc(up_done.sem, 1)

            def experts(g, more, prev):
                n, p = g.shift(1), g.shift(-1)

                def spread(e):
                    if e == 0:
                        pe.wait_ge(chl_ready.sem, chl_ready.at(g))
                    else:
                        pe.wait_ge(cb_ready.sem, cb_ready.at(g, e))
                    if prev and e == 2:
                        pe.wait_ge(xh4l_ready.sem, xh4l_ready.at(p))
                    if more and e == 3:
                        pe.wait_ge(gates_read.sem, gates_read.at(n))
                        pe.wait_ge(act_gates.sem, act_gates.at(n, 1))
                    elif more and e == 4:
                        pe.wait_ge(acol_ready.sem, acol_ready.at(n))
                    pe.matmul(TB[:, :], sel[:, e, :], chl[:, :], start=True, stop=True).then_inc(cb_done.sem, 1)

                def down(u):
                    e, c = u // FC, u % FC
                    pe.wait_ge(hl_ready.sem, hl_ready.at(g, u + 1))
                    if c == 0 and e >= 2:
                        pe.wait_ge(ymul.sem, ymul.at(g, e - 1))
                    split(YB[e % 2][:, :], w2h[:, u, :], w2l[:, u, :], uh[:, u % 4, :], ul[:, u % 4, :],
                          c == 0, c == FC - 1).then_inc(down_done.sem, 1)

                for u in range(NU + 3):
                    if 3 <= u < NU:
                        up(g, u)
                    if prev and u == 7:
                        pe.wait_ge(xh4_ready.sem, xh4_ready.at(p))
                        pe.wait_ge(cb_ready.sem, cb_ready.at(g, 2))
                        turn(xg, xh4_turned)
                    if u >= 3:
                        down(u - 3)
                    if u < NU and u % FC == 1:
                        spread(u // FC)
                    if prev:
                        if MLP_AT <= u < MLP_AT + MI:
                            inner(p, u - MLP_AT)
                        if MLP_AT < u <= MLP_AT + MI:
                            outer(p, u - MLP_AT - 1)
                    if more:
                        if u == 9:
                            pe.wait_ge(xh1_ready.sem, xh1_ready.at(n))
                            pe.wait_ge(cb_ready.sem, cb_ready.at(g, 3))
                            turn(xh, xh1_turned)
                        elif u == 10:
                            pe.wait_ge(c_in.sem, c_in.at(n))
                            pe.wait_ge(xhT_ready.sem, xhT_ready.at(n))
                            turn(c0, c_turned)
                        elif u == 11:
                            gates(n)
                        elif u == 16:
                            pe.wait_ge(cb_ready.sem, cb_ready.at(g, 4))
                            turn_rows(n)
                        if u in UNIT_AT:
                            k = UNIT_AT.index(u)
                            if k == 0 and prev:
                                pe.wait_ge(fh_ready.sem, fh_ready.at(p))
                            decay_after(n, k)
                            if k == 1 and prev:
                                pe.wait_ge(res_ready.sem, res_ready.at(p))
                            if k:
                                outputs(n, k - 1)
                        if u - 1 in UNIT_AT:
                            scores_after(n, UNIT_AT.index(u - 1))
                    if more and u == 30:
                        decay_after(n, 6)
                        outputs(n, 5)
                    if u == 30:
                        pe.wait_ge(ca_in.sem, ca_in.at(g))
                        pe.wait_ge(cb_ready.sem, cb_ready.at(g, E0))
                        turn(cA, ca_turned)

            def attention(g, more, prev):
                n = g.shift(1)

                def key_side(h):
                    if h == 0:
                        pe.wait_ge(ctl_ready.sem, ctl_ready.at(g))
                        pe.wait_ge(hl_ready.sem, hl_ready.at(g))
                    elif h == HQ - 1:
                        pe.wait_ge(ul_ready.sem, ul_ready.at(g, 2))
                    elif h >= HQ and h % HQ == 0:
                        pe.wait_ge(v_ready.sem, v_ready.at(g, h))
                    elif h >= HQ and h % HQ == HQ - 1:
                        pe.wait_ge(pts_ready.sem, pts_ready.at(g, h - 2 * HQ + 1))
                    split(KB[h // HQ][h % HQ][:, :], wqk_h[:, h, :], wqk_l[:, h, :], flat(cTh), flat(cTl),
                          True, True).then_inc(u_done.sem, 1)

                def scores(k):
                    q, b = k // G, k % G
                    if k == 0:
                        pe.wait_ge(x3l_ready.sem, x3l_ready.at(g))
                    if b == 0:
                        pe.wait_ge(ul_ready.sem, ul_ready.at(g, HQ * (q + 1)))
                    if k == 1:
                        pe.wait_ge(ymul.sem, ymul.at(g))
                    if k >= 2:
                        pe.wait_ge(p_exp.sem, p_exp.at(g, k - 1))
                    cols = slice(P * b, P * b + P)
                    split(YB[k % 2][:, :].rearrange("p (h j) -> p h j", h=HQ), x3h[:, b, :], x3l[:, b, :],
                          uh[:, :, cols], ul[:, :, cols], True, True).then_inc(a_done.sem, 1)

                def values(k):
                    q, b = k // G, k % G
                    if k:
                        pe.wait_ge(v_ready.sem, v_ready.at(g, k))
                    if k == 0:
                        pe.wait_ge(ul_ready.sem, ul_ready.at(g, 1))
                    elif k % HQ == 0:
                        pe.wait_ge(ul_ready.sem, ul_ready.at(g, k + 1))
                    cols = slice(HQ * q, HQ * q + HQ)
                    split(UP[1][:, :].rearrange("p (h j) -> p h j", h=HQ), cTh[:, b, :], cTl[:, b, :],
                          wvo_h[:, cols, :], wvo_l[:, cols, :], True, True).then_inc(v_done.sem, 1)

                def turn_probs(k):
                    pe.wait_ge(p_ready.sem, p_ready.at(g, k + 1))
                    if k >= 2:
                        pe.wait_ge(pts_ready.sem, pts_ready.at(g, k - 1))
                    if k % HQ == 1:
                        pe.wait_ge(ul_ready.sem, ul_ready.at(g, min(HQ * (k // HQ + 2), H1)))
                    for i in range(HQ):
                        last = pe.transpose(PTB[k % 2][:, P * i:P * i + P], pr[:, k % 3, i, :], ident[:])
                    last.then_inc(pt_done.sem, 1)

                def weighted(k):
                    q, b = k // G, k % G
                    if k == 0 and more:
                        pe.wait_ge(hs_ready.sem, hs_ready.at(n))
                    elif k == 0 and prev:
                        pe.wait_ge(res_ready.sem, res_ready.at(g.shift(-1)))
                    pe.wait_ge(pts_ready.sem, pts_ready.at(g, k + 1))
                    pe.wait_ge(v_ready.sem, v_ready.at(g, k + 1))
                    for i in range(HQ):
                        last = pe.matmul(HB[:, P * b:P * b + P], pts[:, k % 2, i, :], vv[k % 4][:, P * i:P * i + P],
                                         start=(k == 0 and i == 0), stop=(q == 3 and i == HQ - 1),
                                         skip_group_check=True)
                    last.then_inc(pv_done.sem, 1)

                key_side(0)
                key_side(1)
                if more:
                    scores_after(n, 6)
                pe.wait_ge(yadd.sem, yadd.at(g))
                turn(yacc, y_turned)
                key_side(2)
                if more:
                    decay_after(n, 7)
                key_side(3)
                values(0)
                if more:
                    outputs(n, 6)
                    scores_after(n, 7)
                values(1)
                pe.wait_ge(x2_ready.sem, x2_ready.at(g))
                pe.wait_ge(xh3_ready.sem, xh3_ready.at(g))
                turn(xg, xh3_turned)
                if more:
                    outputs(n, 7)
                for k in range(NK + LAG):
                    next_q = k % HQ == HQ - 1 and k < NK - 1
                    if LAG <= k < NK + LAG - 1:
                        turn_probs(k - LAG)
                    if k < NK:
                        scores(k)
                    if next_q:
                        for h in range(k + 1, k + 1 + HQ):
                            key_side(h)
                    if 2 <= k + 1 < NK:
                        values(k + 1)
                    if more:
                        if k == NK:
                            pe.wait_ge(x2hl_ready.sem, x2hl_ready.at(n))
                            up(n, 0)
                        elif k == NK + 1:
                            pe.wait_ge(v_ready.sem, v_ready.at(g))
                            up(n, 1)
                        elif k == 15:
                            turn_choice(n)
                    if k == NK + LAG - 2:
                        turn_probs(NK - 1)
                    if k >= LAG:
                        weighted(k - LAG)
                    if more:
                        if k == 11:
                            pe.wait_ge(ul_ready.sem, ul_ready.at(g))
                            pe.wait_ge(xh2_ready.sem, xh2_ready.at(n))
                            turn(xh, xh2_turned)
                        elif k == 12:
                            logits(n)
                        elif k == NK + 2:
                            up(n, 2)

            def body(g, more, prev):
                experts(g, more, prev)
                attention(g, more, prev)

            def prologue():
                g = Group(0)
                turn_gates()
                for w in range(2):
                    for half in range(2):
                        turn_weights(w, half)
                pe.wait_ge(set_act, 1)
                pe.wait_ge(xh1_ready.sem, xh1_ready.at(g))
                turn(xh, xh1_turned)
                join(1, 0)
                join(1, 1)
                pe.wait_ge(c_in.sem, c_in.at(g))
                pe.wait_ge(xhT_ready.sem, xhT_ready.at(g))
                turn(c0, c_turned)
                join(1, 2)
                gates(g)
                join(1, 3)
                for half in range(2):
                    turn_weights(2, half)
                for q in range(4):
                    join(2, q)
                pe.wait_ge(gates_read.sem, gates_read.at(g))
                pe.wait_ge(act_gates.sem, act_gates.at(g, 1))
                turn_rows(g)
                pe.wait_ge(set_dve, n_low(2, 3))
                for k in range(2 * G + 1):
                    if k < 2 * G:
                        if k >= 2:
                            pe.wait_ge(e_added.sem, e_added.at(g, k - 1))
                        decay(g, k, (XB, YB[0])[k % 2])
                        if k >= 2:
                            pe.wait_ge(c_done.sem, c_done.at(g, k - 1))
                        scores0(g, k, (UP[0], UP[1])[k % 2])
                    if k >= 1:
                        outputs(g, k - 1)
                pe.wait_ge(ffn_fold, 1)
                pe.matmul(UP[2][:, 0:P], b2_rep, wout_s, start=True, stop=True).then_inc(ffn_pe, 1)
                pe.wait_ge(xh2_ready.sem, xh2_ready.at(g))
                turn(xh, xh2_turned)
                logits(g)
                pe.wait_ge(x2hl_ready.sem, x2hl_ready.at(g))
                turn_choice(g)
                for u in range(3):
                    up(g, u)

            def epilogue(g):
                pe.wait_ge(xh4_ready.sem, xh4_ready.at(g))
                turn(xg, xh4_turned)
                for c in range(MI + 1):
                    if c < MI:
                        if c >= 2:
                            pe.wait_ge(fh_ready.sem, fh_ready.at(g, c - 1))
                        inner(g, c, (XB, UP[0])[c % 2], alone=False)
                    if c >= 1:
                        outer(g, c - 1)

            run(body, prologue, epilogue, pe)


_INS = ['x', 'ctx_1024', 'L0_xattn_Wi_w', 'L0_xattn_Wi_b', 'L0_xattn_Wf_w', 'L0_xattn_Wf_b', 'L0_xattn_gn_w',
        'L0_xattn_gn_b', 'L0_ffn_gate_w', 'L0_ffn_w1', 'L0_ffn_w2', 'L1_xattn_w_q', 'L1_xattn_w_k',
        'L1_xattn_w_v', 'L1_xattn_w_o', 'L1_ffn_Win', 'L1_ffn_bin_', 'L1_ffn_W1', 'L1_ffn_b1', 'L1_ffn_W2',
        'L1_ffn_b2', 'L1_ffn_Wout', 'L1_ffn_bout']


def kernel(**inputs):
    import numpy as _np
    import concourse.bacc as _bacc
    from concourse import mybir as _mybir
    from concourse.bass_utils import run_bass_kernel_spmd as _run

    nc = _bacc.Bacc("TRN2", target_bir_lowering=False, num_devices=1, dynamic_dma_scratch_size=256)
    arrays, args = {}, []
    for name in _INS:
        a = _np.ascontiguousarray(inputs[name])
        arrays[f"in_{name}_dram"] = a
        args.append(nc.dram_tensor(f"in_{name}_dram", a.shape, _mybir.dt.from_np(a.dtype), kind="ExternalInput").ap())
    shape = arrays["in_x_dram"].shape
    args.append(nc.dram_tensor("out_0_dram", shape, _mybir.dt.float32, kind="ExternalOutput").ap())
    build(nc, *args)
    r = _run(nc, [arrays], core_ids=[0])
    return r.results[0]["out_0_dram"]
```
